# Optimizing a Trainium2 kernel written in Bass

```python
import numpy as np
import jax
import jax.numpy as jnp

def _softmax(x, axis=-1):
    return jax.nn.softmax(x, axis=axis)

def _gelu(x):
    return jax.nn.gelu(x, approximate=True)

def _silu(x):
    return jax.nn.silu(x)

def _sigmoid(x):
    return jax.nn.sigmoid(x)

def _layernorm(x, axis=-1, eps=1e-05):
    m = jnp.mean(x, axis=axis, keepdims=True)
    v = jnp.var(x, axis=axis, keepdims=True)
    return (x - m) / jnp.sqrt(v + eps)

def _scatter_add(tgt, idx, src, axis=0):
    return tgt.at[idx].add(src)

def _segment_sum(src, seg, n):
    return jax.ops.segment_sum(src, seg, n)
kernel_name = 'mk_gps_d2_gnn_r32_20de54'

def setup_inputs(seed: int=0):
    np.random.seed(seed)
    _w = jnp.asarray

    def _rec_inputs():
        import jax
        import jax.numpy as jnp
        _gk = jax.random.key(seed)
        x = -0.0002117 + 1 * jax.random.normal(jax.random.fold_in(_gk, 1), (3125, 256), jnp.float32)
        src = jax.random.randint(jax.random.fold_in(_gk, 2), (50000,), 0, 3125, jnp.int32)
        dst = jnp.minimum((3125 * jax.random.uniform(jax.random.fold_in(_gk, 3), (50000,)) ** 2.0).astype(jnp.int32), 99999)
        _o = jnp.argsort(dst, stable=True)
        src = src[_o]
        dst = dst[_o]
        edge_weight = jax.random.uniform(jax.random.fold_in(_gk, 13), (50000,), jnp.float32, 0.0, 1)
        return (x, src, dst, edge_weight)
    x, src, dst, edge_weight = _rec_inputs()

    def _L0_gnn_setup():
        import jax, jax.numpy as jnp
        import numpy as np
        N = 3125
        E = 100000
        IN_F = 256
        OUT_F = 256
        BN_EPS = 1e-05

        def make_quaternion_mul(kernel):
            dim = kernel.shape[1] // 4
            r, i, j, k = jnp.split(kernel, 4, axis=1)
            r2 = jnp.concatenate([r, -i, -j, -k], axis=0)
            i2 = jnp.concatenate([i, r, -k, j], axis=0)
            j2 = jnp.concatenate([j, k, r, -i], axis=0)
            k2 = jnp.concatenate([k, -j, i, r], axis=0)
            return jnp.concatenate([r2, i2, j2, k2], axis=1)
        key = jax.random.key(seed)
        k1, k2, k3, k4, k5, k6 = jax.random.split(key, 6)
        stdv = float(np.sqrt(6.0 / (IN_F // 8 + OUT_F // 2)))
        return {'input': jax.random.normal(k1, (N, IN_F), dtype=jnp.float32), 'A': jax.random.uniform(k2, (IN_F // 8, OUT_F // 2), jnp.float32, -stdv, stdv), 'B': jax.random.uniform(k3, (IN_F // 8, OUT_F // 2), jnp.float32, -stdv, stdv), 'edge_row': jax.random.randint(k4, (E,), 0, N, dtype=jnp.int32), 'edge_col': jax.random.randint(k5, (E,), 0, N, dtype=jnp.int32), 'edge_w': jax.random.uniform(k6, (E,), dtype=jnp.float32), 'bn_weight': jnp.ones((OUT_F,), jnp.float32), 'bn_bias': jnp.zeros((OUT_F,), jnp.float32)}
    _L0_gnn_all = _L0_gnn_setup()
    _L0_gnn_in = {k: v for k, v in _L0_gnn_all.items() if k in ('A', 'B', 'bn_weight', 'bn_bias')}
    del _L0_gnn_all

    def _L0_mix_setup():
        import jax, jax.numpy as jnp
        import numpy as np
        N, F, C, H = (32, 128, 256, 8)
        D = C // H
        EPS_ATTN = 1e-06
        EPS_LN = 1e-05

        def layer_norm(x, g, b):
            mu = jnp.mean(x, axis=-1, keepdims=True)
            var = jnp.var(x, axis=-1, keepdims=True)
            return (x - mu) * jax.lax.rsqrt(var + EPS_LN) * g + b
        key = jax.random.key(seed)
        ks = jax.random.split(key, 8)
        s = 1.0 / np.sqrt(C)
        return {'x': jax.random.normal(ks[0], (N, F, C), jnp.float32), 'Wqkv': jax.random.uniform(ks[1], (3 * C, C), jnp.float32, -s, s), 'ln1_g': jnp.ones((C,), jnp.float32), 'ln1_b': jnp.zeros((C,), jnp.float32), 'W1': jax.random.uniform(ks[2], (C, C), jnp.float32, -s, s), 'b1': jax.random.uniform(ks[3], (C,), jnp.float32, -s, s), 'W2': jax.random.uniform(ks[4], (C, C), jnp.float32, -s, s), 'b2': jax.random.uniform(ks[5], (C,), jnp.float32, -s, s), 'ln2_g': jnp.ones((C,), jnp.float32), 'ln2_b': jnp.zeros((C,), jnp.float32)}
    _L0_mix_all = _L0_mix_setup()
    _L0_mix_in = {k: v for k, v in _L0_mix_all.items() if k in ('Wqkv', 'ln1_g', 'ln1_b', 'W1', 'b1', 'W2', 'b2', 'ln2_g', 'ln2_b')}
    del _L0_mix_all

    def _L0_ffn_setup():
        import jax, jax.numpy as jnp
        import numpy as np
        B, S, D, H, E, K = (8, 256, 256, 1024, 8, 2)
        key = jax.random.key(seed)
        ks = jax.random.split(key, 7)
        s_in = 1.0 / np.sqrt(D)
        s_hid = 1.0 / np.sqrt(H)
        return {'x': jax.random.normal(ks[0], (B, S, D), dtype=jnp.float32), 'Wg': jax.random.uniform(ks[1], (E, D), jnp.float32, -s_in, s_in), 'bg': jax.random.uniform(ks[2], (E,), jnp.float32, -s_in, s_in), 'W1': jax.random.uniform(ks[3], (E, H, D), jnp.float32, -s_in, s_in), 'b1': jax.random.uniform(ks[4], (E, H), jnp.float32, -s_in, s_in), 'W2': jax.random.uniform(ks[5], (E, D, H), jnp.float32, -s_hid, s_hid), 'b2': jax.random.uniform(ks[6], (E, D), jnp.float32, -s_hid, s_hid)}
    _L0_ffn_all = _L0_ffn_setup()
    _L0_ffn_in = {k: v for k, v in _L0_ffn_all.items() if k in ('Wg', 'bg', 'W1', 'b1', 'W2', 'b2')}
    del _L0_ffn_all

    def _L1_gnn_setup():
        import jax, jax.numpy as jnp
        import numpy as np
        N, IN_CH, HEADS, OUT_CH, E = (50000, 256, 4, 64, 25000)
        key = jax.random.key(seed)
        k1, k2, k3, k4, k5 = jax.random.split(key, 5)
        x = jax.random.normal(k1, (N, IN_CH), dtype=jnp.float32)
        edge_index = jax.random.randint(k2, (2, E), 0, N, dtype=jnp.int64)
        bw = float(np.sqrt(6.0 / (IN_CH + HEADS * OUT_CH)))
        ba = float(np.sqrt(6.0 / (HEADS + OUT_CH)))
        weight = jax.random.uniform(k3, (IN_CH, HEADS * OUT_CH), jnp.float32, -bw, bw)
        attn_l = jax.random.uniform(k4, (HEADS, OUT_CH), jnp.float32, -ba, ba)
        attn_r = jax.random.uniform(k5, (HEADS, OUT_CH), jnp.float32, -ba, ba)
        return {'x': x, 'edge_index': edge_index, 'weight': weight, 'attn_l': attn_l, 'attn_r': attn_r}
    _L1_gnn_all = _L1_gnn_setup()
    _L1_gnn_in = {k: v for k, v in _L1_gnn_all.items() if k in ('weight', 'attn_l', 'attn_r')}
    del _L1_gnn_all

    def _L1_mix_setup():
        import jax, jax.numpy as jnp
        import numpy as np
        import math
        EMBED = 256
        HEADS = 4
        HEAD_DIM = EMBED // HEADS
        OUT_DIM = 256
        LN_EPS = 1e-05

        def _qkv_init(key):
            spread = math.sqrt(3.0 / EMBED)
            gain, delta = (0.01, 0.01)
            w = jax.random.uniform(key, (EMBED, EMBED), minval=-spread, maxval=spread) * gain
            return w + delta * jnp.eye(EMBED, dtype=w.dtype)

        def _layer_norm(x, g, b):
            mu = jnp.mean(x, axis=-1, keepdims=True)
            var = jnp.mean(jnp.square(x - mu), axis=-1, keepdims=True)
            return (x - mu) * jax.lax.rsqrt(var + LN_EPS) * g + b

        def _split_heads(x, B, S):
            return x.reshape(B, S, HEADS, HEAD_DIM).transpose(0, 2, 1, 3)
        key = jax.random.key(seed)
        ks = jax.random.split(key, 6)
        seq = jax.random.normal(ks[0], (4, 256, EMBED), dtype=jnp.float32)
        wq = _qkv_init(ks[1])
        wk = _qkv_init(ks[2])
        wv = _qkv_init(ks[3])
        bound = 1.0 / math.sqrt(EMBED)
        wo = jax.random.uniform(ks[4], (OUT_DIM, EMBED), minval=-bound, maxval=bound)
        bo = jax.random.uniform(ks[5], (OUT_DIM,), minval=-bound, maxval=bound)
        ln_k_g = jnp.ones((HEAD_DIM,), jnp.float32)
        ln_k_b = jnp.zeros((HEAD_DIM,), jnp.float32)
        ln_v_g = jnp.ones((HEAD_DIM,), jnp.float32)
        ln_v_b = jnp.zeros((HEAD_DIM,), jnp.float32)
        return {'seq': seq, 'wq': wq, 'wk': wk, 'wv': wv, 'wo': wo, 'bo': bo, 'ln_k_g': ln_k_g, 'ln_k_b': ln_k_b, 'ln_v_g': ln_v_g, 'ln_v_b': ln_v_b}
    _L1_mix_all = _L1_mix_setup()
    _L1_mix_in = {k: v for k, v in _L1_mix_all.items() if k in ('wq', 'wk', 'wv', 'wo', 'bo', 'ln_k_g', 'ln_k_b', 'ln_v_g', 'ln_v_b')}
    del _L1_mix_all

    def _L1_ffn_setup():
        import jax, jax.numpy as jnp
        import numpy as np
        C = 256
        HID = 1024
        E = 8
        TEMP = 1.0
        key = jax.random.key(seed)
        ks = jax.random.split(key, 7)
        x = jax.random.normal(ks[0], (8, 512, C), dtype=jnp.float32)
        W1 = jax.random.normal(ks[1], (C, HID), dtype=jnp.float32) * 0.02
        b1 = jnp.zeros((HID,), dtype=jnp.float32)
        Wg = jax.random.normal(ks[2], (HID, E), dtype=jnp.float32) * 0.02
        bg = jnp.zeros((E,), dtype=jnp.float32)
        Wd = jax.random.normal(ks[3], (E, HID, C), dtype=jnp.float32) * 0.02
        bd = jnp.zeros((E, C), dtype=jnp.float32)
        return {'x': x, 'W1': W1, 'b1': b1, 'Wg': Wg, 'bg': bg, 'Wd': Wd, 'bd': bd}
    _L1_ffn_all = _L1_ffn_setup()
    _L1_ffn_in = {k: v for k, v in _L1_ffn_all.items() if k in ('W1', 'b1', 'Wg', 'bg', 'Wd', 'bd')}
    del _L1_ffn_all
    return {'x': x, 'src': src, 'dst': dst, 'edge_weight': edge_weight, 'L0_gnn_A': _L0_gnn_in['A'], 'L0_gnn_B': _L0_gnn_in['B'], 'L0_gnn_bn_weight': _L0_gnn_in['bn_weight'], 'L0_gnn_bn_bias': _L0_gnn_in['bn_bias'], 'L0_mix_Wqkv': _L0_mix_in['Wqkv'], 'L0_mix_ln1_g': _L0_mix_in['ln1_g'], 'L0_mix_ln1_b': _L0_mix_in['ln1_b'], 'L0_mix_W1': _L0_mix_in['W1'], 'L0_mix_b1': _L0_mix_in['b1'], 'L0_mix_W2': _L0_mix_in['W2'], 'L0_mix_b2': _L0_mix_in['b2'], 'L0_mix_ln2_g': _L0_mix_in['ln2_g'], 'L0_mix_ln2_b': _L0_mix_in['ln2_b'], 'L0_ffn_Wg': _L0_ffn_in['Wg'], 'L0_ffn_bg': _L0_ffn_in['bg'], 'L0_ffn_W1': _L0_ffn_in['W1'], 'L0_ffn_b1': _L0_ffn_in['b1'], 'L0_ffn_W2': _L0_ffn_in['W2'], 'L0_ffn_b2': _L0_ffn_in['b2'], 'L1_gnn_weight': _L1_gnn_in['weight'], 'L1_gnn_attn_l': _L1_gnn_in['attn_l'], 'L1_gnn_attn_r': _L1_gnn_in['attn_r'], 'L1_mix_wq': _L1_mix_in['wq'], 'L1_mix_wk': _L1_mix_in['wk'], 'L1_mix_wv': _L1_mix_in['wv'], 'L1_mix_wo': _L1_mix_in['wo'], 'L1_mix_bo': _L1_mix_in['bo'], 'L1_mix_ln_k_g': _L1_mix_in['ln_k_g'], 'L1_mix_ln_k_b': _L1_mix_in['ln_k_b'], 'L1_mix_ln_v_g': _L1_mix_in['ln_v_g'], 'L1_mix_ln_v_b': _L1_mix_in['ln_v_b'], 'L1_ffn_W1': _L1_ffn_in['W1'], 'L1_ffn_b1': _L1_ffn_in['b1'], 'L1_ffn_Wg': _L1_ffn_in['Wg'], 'L1_ffn_bg': _L1_ffn_in['bg'], 'L1_ffn_Wd': _L1_ffn_in['Wd'], 'L1_ffn_bd': _L1_ffn_in['bd']}

def reference(x, src, dst, edge_weight, L0_gnn_A, L0_gnn_B, L0_gnn_bn_weight, L0_gnn_bn_bias, L0_mix_Wqkv, L0_mix_ln1_g, L0_mix_ln1_b, L0_mix_W1, L0_mix_b1, L0_mix_W2, L0_mix_b2, L0_mix_ln2_g, L0_mix_ln2_b, L0_ffn_Wg, L0_ffn_bg, L0_ffn_W1, L0_ffn_b1, L0_ffn_W2, L0_ffn_b2, L1_gnn_weight, L1_gnn_attn_l, L1_gnn_attn_r, L1_mix_wq, L1_mix_wk, L1_mix_wv, L1_mix_wo, L1_mix_bo, L1_mix_ln_k_g, L1_mix_ln_k_b, L1_mix_ln_v_g, L1_mix_ln_v_b, L1_ffn_W1, L1_ffn_b1, L1_ffn_Wg, L1_ffn_bg, L1_ffn_Wd, L1_ffn_bd):
    import jax
    import jax.numpy as jnp

    def _L0_gnn_ref(input, A, B, edge_row, edge_col, edge_w, bn_weight, bn_bias):
        import jax, jax.numpy as jnp
        import numpy as np
        N = 3125
        E = 100000
        IN_F = 256
        OUT_F = 256
        BN_EPS = 1e-05

        def make_quaternion_mul(kernel):
            dim = kernel.shape[1] // 4
            r, i, j, k = jnp.split(kernel, 4, axis=1)
            r2 = jnp.concatenate([r, -i, -j, -k], axis=0)
            i2 = jnp.concatenate([i, r, -k, j], axis=0)
            j2 = jnp.concatenate([j, k, r, -i], axis=0)
            k2 = jnp.concatenate([k, -j, i, r], axis=0)
            return jnp.concatenate([r2, i2, j2, k2], axis=1)
        half = input.shape[1] // 2
        C, D = (input[:, :half], input[:, half:])
        A_h = make_quaternion_mul(A)
        B_h = make_quaternion_mul(B)
        AC = C @ A_h
        AD_plus_BC = D @ A_h + C @ B_h
        support = jnp.concatenate([AC, AD_plus_BC], axis=1)
        vals = support[edge_col] * edge_w[:, None]
        output = jax.ops.segment_sum(vals, edge_row, num_segments=N)
        mean = jnp.mean(output, axis=0)
        var = jnp.mean(jnp.square(output - mean), axis=0)
        normed = (output - mean) * jax.lax.rsqrt(var + BN_EPS) * bn_weight + bn_bias
        return jnp.tanh(normed)

    def _L0_mix_ref(x, Wqkv, ln1_g, ln1_b, W1, b1, W2, b2, ln2_g, ln2_b):
        import jax, jax.numpy as jnp
        import numpy as np
        N, F, C, H = (32, 128, 256, 8)
        D = C // H
        EPS_ATTN = 1e-06
        EPS_LN = 1e-05

        def layer_norm(x, g, b):
            mu = jnp.mean(x, axis=-1, keepdims=True)
            var = jnp.var(x, axis=-1, keepdims=True)
            return (x - mu) * jax.lax.rsqrt(var + EPS_LN) * g + b
        n, f, c = x.shape
        qkv = jnp.einsum('nfc,oc->nfo', x, Wqkv)
        q, k, v = jnp.split(qkv, 3, axis=-1)
        q = q.reshape(n, f, H, D)
        k = k.reshape(n, f, H, D)
        v = v.reshape(n, f, H, D)
        q = jax.nn.elu(q) + 1.0
        k = jax.nn.elu(k) + 1.0
        kv = jnp.einsum('nshd,nshm->nhmd', k, v)
        ksum = jnp.sum(k, axis=1)
        z = 1.0 / (jnp.einsum('nlhd,nhd->nlh', q, ksum) + EPS_ATTN)
        t = jnp.einsum('nlhd,nhmd,nlh->nlhm', q, kv, z)
        t = t.reshape(n, f, c)
        x1 = layer_norm(t + x, ln1_g, ln1_b)
        h = jax.nn.gelu(jnp.einsum('nfc,oc->nfo', x1, W1) + b1, approximate=False)
        y = jnp.einsum('nfc,oc->nfo', h, W2) + b2
        return layer_norm(y + x1, ln2_g, ln2_b)

    def _L0_ffn_ref(x, Wg, bg, W1, b1, W2, b2):
        import jax, jax.numpy as jnp
        import numpy as np
        B, S, D, H, E, K = (8, 256, 256, 1024, 8, 2)
        gate_scores = jnp.einsum('bsd,ed->bse', x, Wg) + bg
        topk_scores, topk_idx = jax.lax.top_k(gate_scores, K)
        topk_probs = jax.nn.softmax(topk_scores, axis=-1)
        combine = jnp.sum(topk_probs[..., None] * jax.nn.one_hot(topk_idx, E, dtype=x.dtype), axis=-2)
        out = jnp.zeros_like(x)
        for e in range(E):
            h = jax.nn.relu(jnp.einsum('bsd,hd->bsh', x, W1[e]) + b1[e])
            y = jnp.einsum('bsh,dh->bsd', h, W2[e]) + b2[e]
            out = out + combine[..., e:e + 1] * y
        return out

    def _L1_gnn_ref(x, edge_index, weight, attn_l, attn_r):
        import jax, jax.numpy as jnp
        import numpy as np
        N, IN_CH, HEADS, OUT_CH, E = (50000, 256, 4, 64, 25000)
        heads, out_ch = attn_l.shape
        n = x.shape[0]
        xt = jnp.matmul(x, weight).reshape(-1, heads, out_ch)
        row, col = (edge_index[0], edge_index[1])
        alpha_l = jnp.einsum('ehd,hd->eh', xt[row], attn_l)
        alpha_r = jnp.einsum('ehd,hd->eh', xt[col], attn_r)
        alpha = jax.nn.softmax(jax.nn.leaky_relu(alpha_l + alpha_r, 0.01), axis=1)
        tmp = jnp.einsum('nh,nhd->nd', alpha[:n], xt[col[:n]])
        out = jnp.broadcast_to(tmp[:, None, :], (n, heads, out_ch))
        return out.reshape(n, heads * out_ch)

    def _L1_mix_ref(seq, wq, wk, wv, wo, bo, ln_k_g, ln_k_b, ln_v_g, ln_v_b):
        import jax, jax.numpy as jnp
        import numpy as np
        import math
        EMBED = 256
        HEADS = 4
        HEAD_DIM = EMBED // HEADS
        OUT_DIM = 256
        LN_EPS = 1e-05

        def _qkv_init(key):
            spread = math.sqrt(3.0 / EMBED)
            gain, delta = (0.01, 0.01)
            w = jax.random.uniform(key, (EMBED, EMBED), minval=-spread, maxval=spread) * gain
            return w + delta * jnp.eye(EMBED, dtype=w.dtype)

        def _layer_norm(x, g, b):
            mu = jnp.mean(x, axis=-1, keepdims=True)
            var = jnp.mean(jnp.square(x - mu), axis=-1, keepdims=True)
            return (x - mu) * jax.lax.rsqrt(var + LN_EPS) * g + b

        def _split_heads(x, B, S):
            return x.reshape(B, S, HEADS, HEAD_DIM).transpose(0, 2, 1, 3)
        B, S, _ = seq.shape
        q = _split_heads(seq @ wq.T, B, S)
        k = _split_heads(seq @ wk.T, B, S)
        v = _split_heads(seq @ wv.T, B, S)
        k = _layer_norm(k, ln_k_g, ln_k_b)
        v = _layer_norm(v, ln_v_g, ln_v_b)
        kv = jnp.einsum('bhsd,bhse->bhde', k, v) / S
        ga = jnp.einsum('bhsd,bhde->bhse', q, kv)
        ga = ga.transpose(0, 2, 1, 3).reshape(B, S, EMBED)
        return ga @ wo.T + bo

    def _L1_ffn_ref(x, W1, b1, Wg, bg, Wd, bd):
        import jax, jax.numpy as jnp
        import numpy as np
        C = 256
        HID = 1024
        E = 8
        TEMP = 1.0
        orig_shape = x.shape
        xf = x.reshape(-1, orig_shape[-1])
        H = jax.nn.gelu(xf @ W1 + b1, approximate=False)
        probs = jax.nn.softmax((H @ Wg + bg) / TEMP, axis=-1)
        assign = jnp.argmax(probs, axis=-1)
        out = jnp.zeros_like(xf)
        for e in range(Wd.shape[0]):
            y = H @ Wd[e] + bd[e]
            sel = (assign == e)[:, None]
            out = out + jnp.where(sel, probs[:, e:e + 1] * y, 0.0)
        return out.reshape(orig_shape)
    edge_index = jnp.stack([src, dst])
    xn = _layernorm(x, axis=-1)
    x = x + _L0_gnn_ref(xn, L0_gnn_A, L0_gnn_B, src, dst, edge_weight, L0_gnn_bn_weight, L0_gnn_bn_bias) + _L0_mix_ref(xn[None], L0_mix_Wqkv, L0_mix_ln1_g, L0_mix_ln1_b, L0_mix_W1, L0_mix_b1, L0_mix_W2, L0_mix_b2, L0_mix_ln2_g, L0_mix_ln2_b)[0]
    x = x + _L0_ffn_ref(_layernorm(x, axis=-1)[None], L0_ffn_Wg, L0_ffn_bg, L0_ffn_W1, L0_ffn_b1, L0_ffn_W2, L0_ffn_b2)[0]
    xn = _layernorm(x, axis=-1)
    x = x + _L1_gnn_ref(xn, edge_index, L1_gnn_weight, L1_gnn_attn_l, L1_gnn_attn_r) + _L1_mix_ref(xn[None], L1_mix_wq, L1_mix_wk, L1_mix_wv, L1_mix_wo, L1_mix_bo, L1_mix_ln_k_g, L1_mix_ln_k_b, L1_mix_ln_v_g, L1_mix_ln_v_b)[0]
    x = x + _L1_ffn_ref(_layernorm(x, axis=-1)[None], L1_ffn_W1, L1_ffn_b1, L1_ffn_Wg, L1_ffn_bg, L1_ffn_Wd, L1_ffn_bd)[0]
    return x

_drawn_inputs = setup_inputs


def setup_inputs(seed=0):
    import zlib

    import numpy as np

    out = dict(_drawn_inputs(seed))
    spreads = {'L0_gnn_bn_weight': (1.0, 0.2),
     'L0_gnn_bn_bias': (0.0, 0.1),
     'L0_mix_ln1_g': (1.0, 0.2),
     'L0_mix_ln1_b': (0.0, 0.1),
     'L0_mix_ln2_g': (1.0, 0.2),
     'L0_mix_ln2_b': (0.0, 0.1),
     'L1_mix_ln_k_g': (1.0, 0.6),
     'L1_mix_ln_k_b': (0.0, 0.8),
     'L1_mix_ln_v_g': (1.0, 0.6),
     'L1_mix_ln_v_b': (0.0, 0.8),
     'L1_ffn_b1': (0.0, 0.8),
     'L1_ffn_bg': (0.0, 0.756),
     'L1_ffn_bd': (0.0, 0.8)}
    factors = {'L0_mix_Wqkv': 8.0,
     'L0_mix_b1': 8.0,
     'L0_mix_b2': 2.996,
     'L0_ffn_bg': 3.609,
     'L0_ffn_b1': 8.0,
     'L0_ffn_b2': 8.0,
     'L1_mix_wq': 8.0,
     'L1_mix_wk': 8.0,
     'L1_mix_wv': 8.0,
     'L1_mix_wo': 8.0,
     'L1_mix_bo': 3.37,
     'L1_ffn_W1': 5.784,
     'L1_ffn_Wg': 5.954,
     'L1_ffn_Wd': 7.107}
    for name, (base, spread) in spreads.items():
        noise = np.random.default_rng([zlib.crc32(name.encode()), seed]).standard_normal(out[name].shape)
        drawn = base * np.exp(spread * noise) if base else spread * noise
        out[name] = jnp.asarray(drawn.astype(out[name].dtype))
    for name, factor in factors.items():
        out[name] = (out[name] * factor).astype(out[name].dtype)
    return out
```

```python
import concourse.bass as bass
from concourse import mybir
from contextlib import ExitStack, contextmanager

F32 = mybir.dt.float32
I32 = mybir.dt.int32
U32 = mybir.dt.uint32
ALU = mybir.AluOpType
ACT = mybir.ActivationFunctionType
AX = mybir.AxisListType

P = 128
N = 3125
C = 256
CH = C // P
T = -(-N // P)
LAST = N - (T - 1) * P
E = 50000
EROWS = 125
ECOLS = E // EROWS
EBUF = 8
GB = 16
X = 8
HID = 1024
HC = HID // P
H0, D0 = 8, 32
H1, D1 = 4, 64
KVW = P + 4
SLOTS = 2


def blocks_for(rows, buckets):
    return (rows + buckets * (P - 1)) // P


EBLK = -(-blocks_for(P * ECOLS, T) // GB) * GB
FBLK0 = blocks_for(2 * T * P, X)
FBLK1 = blocks_for(T * P, X)


def done(t):
    return t + 1 + SLOTS


def freed(t):
    return t + 1


def opened(eng, *sems):
    for s in sems:
        eng.sem_inc(s, SLOTS)


def tiles(eng, step, n=T, peel=False):
    if peel:
        step(0, 0, 0, False)
        step(1, 1, 0, False)
    with eng.Fori(int(peel), (n - 1) // 2) as k:
        step(k * 2, 0, k, False)
        step(k * 2 + 1, 1, k, False)
    for t in range((n - 1) // 2 * 2, n):
        step(t, t % 2, t // 2, t == n - 1)


class Chain:

    def __init__(self, eng, sem, start=0):
        self.eng, self.sem, self.value = eng, sem, start

    def __call__(self, ins):
        self.value = self.value + 1
        ins.then_inc(self.sem, 1)
        self.eng.wait_ge(self.sem, self.value)


def landed(eng, sem, k, dmas=1):
    if not isinstance(k, int) or k > 0:
        eng.wait_ge(sem, k * (16 * dmas))


def row(ap, t):
    return ap[:, bass.ds(t, 1)] if not isinstance(t, int) else ap[:, t:t + 1]


class Machine:

    def __init__(self, nc, ctx):
        self.nc, self.ctx, self.used = nc, ctx, []
        self.psum = [ctx.enter_context(nc.psum_tensor(f"bank{i}", [P, 512], F32)) for i in range(8)]

    def sb(self, name, shape, dt=F32):
        return self.ctx.enter_context(self.nc.sbuf_tensor(name, shape, dt))

    def sem(self, name):
        self.used.append(self.nc.alloc_semaphore(name))
        return self.used[-1]

    @contextmanager
    def scope(self):
        outer = self.ctx
        with ExitStack() as self.ctx:
            yield
        self.ctx = outer

    def recycle(self):
        self.nc.clear_and_free_semaphores(self.used)
        self.nc.all_engine_barrier()
        self.used = []

    def sems(self, phase, names):
        return [self.sem(f"{phase}_{n}") for n in names.split()]



def norm_vector(dve, src, dst, tmp, small, s_chain, s_centred, s_square, s_var, s_std, groups=T, width=C):
    link = Chain(dve, s_chain)
    mean, var, std, rstd = (small[:, i, 0:groups] for i in range(4))
    wide = lambda a: a.unsqueeze(2).to_broadcast([P, groups, width])
    link(dve.tensor_reduce(mean, src, AX.X, ALU.add))
    link(dve.tensor_scalar(mean, mean, 1.0 / width, None, ALU.mult))
    dve.tensor_tensor(dst, src, wide(mean), ALU.subtract).then_inc(s_centred, 1)
    dve.wait_ge(s_square, 1)
    link(dve.tensor_reduce(var, tmp, AX.X, ALU.add))
    dve.tensor_scalar(var, var, 1.0 / width, 1e-5, ALU.mult, ALU.add).then_inc(s_var, 1)
    dve.wait_ge(s_std, 1)
    link(dve.reciprocal(rstd, std))
    link(dve.tensor_tensor(dst, dst, wide(rstd), ALU.mult))
    return link


def norm_scalar(act, dst, tmp, small, s_centred, s_square, s_var, s_std, groups=T):
    act.wait_ge(s_centred, 1)
    act.activation(tmp, dst, ACT.Square).then_inc(s_square, 1)
    act.wait_ge(s_var, 1)
    act.activation(small[:, 2, 0:groups], small[:, 1, 0:groups], ACT.Sqrt).then_inc(s_std, 1)


NORM = "centred square var std"



def sort_vector(dve, m, link, key, onehot, count, small, psum, pos, owner, s_counts, s_totals, buckets, cols, nblk):
    oh = onehot[:, 0:buckets * cols].rearrange("p (b c) -> p b c", b=buckets)
    cn = count[:, 0:buckets * cols].rearrange("p (b c) -> p b c", b=buckets)
    link(dve.tensor_tensor(oh, key.unsqueeze(1).to_broadcast([P, buckets, cols]),
                           m.iota[:, 0:buckets].unsqueeze(2).to_broadcast([P, buckets, cols]), ALU.is_equal))
    link(dve.tensor_tensor_scan(count[:, 0:buckets * cols], onehot[:, 0:buckets * cols],
                                onehot[:, 0:buckets * cols], 0.0, ALU.add, ALU.max))
    own, before, base, full, blk, end = (small[:, i, 0:buckets] for i in range(6))
    link(dve.memset(before, 0.0))
    link(dve.tensor_copy(small[:, 1, 1:buckets], cn[:, 0:buckets - 1, cols - 1]))
    dve.tensor_tensor(own, cn[:, :, cols - 1], before, ALU.subtract).then_inc(s_counts, 1)
    dve.wait_ge(s_totals, 1)
    link(dve.tensor_scalar(full, psum[:, 64:64 + buckets], float(P - 1), None, ALU.add))
    whole = m.small_int[:, 0:buckets]
    link(dve.tensor_copy(whole, full))
    link(dve.tensor_scalar(whole, whole, 7, None, ALU.arith_shift_right))
    link(dve.tensor_copy(blk, whole))
    link(dve.tensor_tensor_scan(end, blk, blk, 0.0, ALU.add, ALU.max))
    link(dve.tensor_tensor(base, end, blk, ALU.subtract))
    link(dve.tensor_scalar(base, base, float(P), -1.0, ALU.mult, ALU.add))
    link(dve.tensor_tensor(base, base, before, ALU.subtract))
    link(dve.tensor_tensor(base, base, psum[:, 0:buckets], ALU.add))
    for b in range(buckets):
        ins = dve.scalar_tensor_tensor(out=cn[:, b, :], in0=cn[:, b, :], scalar=base[:, b:b + 1],
                                       in1=oh[:, b, :], op0=ALU.add, op1=ALU.mult)
    link(ins)
    link(dve.tensor_reduce(pos, count[:, 0:buckets * cols].rearrange("p (b c) -> p c b", b=buckets),
                           AX.X, ALU.add))
    past = onehot[:, 0:buckets * nblk].rearrange("p (j b) -> p j b", b=buckets)
    link(dve.tensor_tensor(past, m.iota[:, 0:nblk].unsqueeze(2).to_broadcast([P, nblk, buckets]),
                           end.unsqueeze(1).to_broadcast([P, nblk, buckets]), ALU.is_ge))
    link(dve.tensor_reduce(count[:, 0:nblk], past, AX.X, ALU.add))
    link(dve.tensor_scalar(owner, count[:, 0:nblk], float(buckets - 1), None, ALU.min))


def sort_tensor(pe, m, small, psum, s_counts, s_totals, buckets):
    pe.wait_ge(s_counts, 1)
    pe.matmul(psum[:, 0:buckets], m.earlier[:, :], small[:, 0, 0:buckets], start=True, stop=True)
    pe.matmul(psum[:, 64:64 + buckets], m.ones[:, :], small[:, 0, 0:buckets], start=True, stop=True)\
      .then_inc(s_totals, 1)



def phase_start(nc, m, d):
    sc_chain, s_load, s_const, s_pad = m.sems("start", "chain load const pad")
    norm = m.sems("start", NORM)
    s_edge, s_eload, s_edges, s_counts, s_totals, s_rec, s_wchain = m.sems("start", "edge eload edges counts totals rec wchain")
    with ExitStack() as mem, nc.Block() as block:
        sb = lambda name, shape, dt=F32: mem.enter_context(nc.sbuf_tensor(name, shape, dt))
        tmp = m.mix
        onehot = sb("st_onehot", [P, max(ECOLS, EBLK) * T])
        count = sb("st_count", [P, max(ECOLS, EBLK) * T])
        small = sb("st_small", [P, 6, 32])
        src_i = sb("st_src", [P, ECOLS], I32)
        dst_i = sb("st_dst", [P, ECOLS], I32)
        w = sb("st_w", [P, ECOLS])
        key = sb("st_key", [P, ECOLS])
        pos = sb("st_pos", [P, ECOLS])
        pos_i = sb("st_pos_i", [P, ECOLS], I32)
        lo_i = sb("st_lo_i", [P, ECOLS], I32)
        small2 = sb("st_small2", [P, 4, T])
        zrec = sb("st_zrec", [P, EBLK * 4])

        @block.gpsimd
        def _(pool):
            c = Chain(pool, s_const)
            c(pool.memset(m.ones[:, :], 1.0))
            c(pool.memset(m.zeros[:, :], 0.0))
            c(pool.iota(m.iota[:, :], [[1, EBLK]], base=0, channel_multiplier=0, allow_small_or_imprecise_dtypes=True))
            c(pool.affine_select(out=m.ident[:, :], in_=m.zeros[:, 0:P], compare_op=ALU.not_equal, fill=1.0,
                                 base=0, pattern=[[-1, P]], channel_multiplier=1))
            c(pool.affine_select(out=m.earlier[:, :], in_=m.zeros[:, 0:P], compare_op=ALU.is_ge, fill=1.0,
                                 base=0, pattern=[[-1, P]], channel_multiplier=1))
            c(pool.affine_select(out=m.lastmask[:, :], in_=m.ones[:, 0:1], compare_op=ALU.is_ge, fill=0.0,
                                 base=LAST - 1, pattern=[[0, 1]], channel_multiplier=-1))
            pool.memset(zrec[:, :], 0.0).then_inc(s_rec, 1)

        @block.sync
        def _(sp):
            sp.wait_ge(s_edge, 4)
            sp.dma_start(src_i[0:EROWS, :], d.src.rearrange("(p c) -> p c", p=EROWS)).then_inc(s_edges, 16)
            sp.dma_start(dst_i[0:EROWS, :], d.dst.rearrange("(p c) -> p c", p=EROWS)).then_inc(s_edges, 16)
            sp.dma_start(w[0:EROWS, :], d.edge_weight.rearrange("(p c) -> p c", p=EROWS)).then_inc(s_edges, 16)
            sp.wait_ge(s_rec, 1)
            sp.dma_start(d.rec.rearrange("(p j) r -> p (j r)", p=P), zrec[:, :]).then_inc(s_eload, 16)
            for rows, nblk in ((d.xs0, FBLK0), (d.xs1, FBLK1)):
                sp.dma_start(rows.rearrange("(j p) c -> p j c", p=P), m.zeros[:, :].unsqueeze(1).to_broadcast([P, nblk, C])).then_inc(s_eload, 16)
            sp.wait_ge(s_eload, 48)
            sp.wait_ge(s_load, 32)

        @block.scalar
        def _(act):
            act.wait_ge(s_pad, 1)
            full = (T - 1) * P
            act.dma_start(m.x[:, 0:T - 1, :], d.x[0:full, :].rearrange("(t p) c -> p t c", p=P)).then_inc(s_load, 16)
            act.dma_start(m.x[0:LAST, T - 1, :], d.x[full:N, :]).then_inc(s_load, 16)
            norm_scalar(act, m.xn[:, :, :], tmp[:, :, :], small2[:, :, :], *norm)

        @block.vector
        def _(dve):
            dve.memset(src_i[:, :], 0).then_inc(s_edge, 1)
            dve.memset(dst_i[:, :], 0).then_inc(s_edge, 1)
            dve.memset(w[:, :], 0.0).then_inc(s_edge, 1)
            dve.memset(m.rec[:, :, :], 0.0).then_inc(s_edge, 1)
            dve.memset(m.x[:, T - 1, :], 0.0).then_inc(s_pad, 1)
            dve.wait_ge(s_const, 6)
            dve.wait_ge(s_edges, 48)
            link = Chain(dve, s_wchain)
            link(dve.tensor_scalar(lo_i[:, :], src_i[:, :], 7, None, ALU.arith_shift_right))
            link(dve.tensor_copy(key[:, :], lo_i[:, :]))
            link(dve.tensor_scalar(lo_i[:, :], src_i[:, :], P - 1, None, ALU.bitwise_and))
            dve.tensor_copy(m.rec[:, :, 0], lo_i[:, :])
            dve.tensor_copy(m.rec[:, :, 1], w[:, :])
            link(dve.tensor_copy(m.rec.bitcast(I32)[:, :, 2], dst_i[:, :]))
            sort_vector(dve, m, link, key[:, :], onehot, count, small, m.psum[0], pos[:, :], m.eowner[:, :],
                        s_counts, s_totals, T, ECOLS, EBLK)
            link(dve.tensor_copy(pos_i[:, :], pos[:, :]))
            link(dve.tensor_scalar(lo_i[:, :], pos_i[:, :], P - 1, None, ALU.bitwise_and))
            link(dve.tensor_scalar(pos_i[:, :], pos_i[:, :], 7, None, ALU.arith_shift_right))
            link(dve.tensor_scalar(pos[:, :], lo_i[:, :], float(EBLK), None, ALU.mult))
            link(dve.tensor_tensor(m.epos[:, :], pos[:, :], pos_i[:, :], ALU.add))
            dve.wait_ge(s_load, 32)
            norm_vector(dve, m.x[:, :, :], m.xn[:, :, :], tmp[:, :, :], small2[:, :, :], sc_chain, *norm)

        @block.tensor
        def _(pe):
            pe.wait_ge(s_const, 6)
            sort_tensor(pe, m, small, m.psum[0], s_counts, s_totals, T)


def scatter_edges(pool, m, d, first, last):
    s_copied, s_sent, s_issue = m.s_copied, m.s_sent, m.s_issue
    step = 2 * EBUF

    def both(k):
        for h in range(2):
            col = k * step + h * EBUF
            landed(pool, s_sent[h], k, EBUF)
            pool.tensor_copy(m.buf_rec[h][:, :], m.rec[:, bass.ds(col, EBUF), :].rearrange("p c r -> p (c r)"))
            pool.tensor_copy(m.buf_pos[h][:, :], m.epos[:, bass.ds(col, EBUF)]).then_inc(s_copied, 1)
            pool.wait_ge(s_copied, k * 2 + h + 1)
            pool.sem_inc(s_issue, 1)
            for u in range(EBUF):
                pool.indirect_dma_start(out=d.rec, out_offset=bass.IndirectOffsetOnAxis(ap=m.buf_pos[h][:, u:u + 1], axis=0),
                                        in_=m.buf_rec[h][:, 4 * u:4 * u + 4], in_offset=None).then_inc(s_sent[h], 16)

    if first == 0:
        both(0)
    with pool.Fori(max(first // step, 1), last // step) as k:
        both(k)
    for h in range(2):
        pool.wait_ge(s_sent[h], last // step * 16 * EBUF)



QUATERNION = [[(0, 1), (1, 1), (2, 1), (3, 1)],
              [(1, -1), (0, 1), (3, 1), (2, -1)],
              [(2, -1), (3, -1), (0, 1), (1, 1)],
              [(3, -1), (2, 1), (1, -1), (0, 1)]]


def phase_support_kv(nc, m, d, share):
    (s_w, s_built, s_chain, s_copied, s_flipped, s_row, s_rowall, s_proj, s_kmin, s_kexp, s_k, s_v, s_kv, s_sup,
     s_bd) = m.sems("skv", "w built chain copied flipped row rowall proj kmin kexp k v kv sup bd")
    s_store = m.sems("skv", "store0 store1")
    with ExitStack() as mem, nc.Block() as block:
        sb = lambda name, shape, dt=F32: mem.enter_context(nc.sbuf_tensor("skv_" + name, shape, dt))
        w = sb("w", [P, CH, 3 * C])
        ab = sb("ab", [P, 2, P])
        g = w[:, :, 2 * C:3 * C]
        xs = [sb(f"xs{s}", [P, C]) for s in range(SLOTS)]
        xt = [sb(f"xt{s}", [P, CH, P]) for s in range(SLOTS)]
        sup = [sb(f"sup{s}", [P, C]) for s in range(SLOTS)]
        kmin = [sb(f"kmin{s}", [P, C]) for s in range(SLOTS)]
        kexp = [sb(f"kexp{s}", [P, C]) for s in range(SLOTS)]
        ks = [sb(f"ks{s}", [P, C]) for s in range(SLOTS)]
        vs = [sb(f"vs{s}", [P, CH, KVW]) for s in range(SLOTS)]
        flip, kp, vsp, kv = m.psum[0:2], m.psum[2:4], m.psum[4:6], m.psum[6:8]

        @block.sync
        def _(sp):
            sp.dma_start(w[:, :, 0:2 * C], d.wqkv[:, C:3 * C].rearrange("(h p) o -> p h o", p=P)).then_inc(s_w, 16)
            for b in range(4):
                sp.dma_start(ab[32 * b:32 * b + 32, 0, :], d.A).then_inc(s_w, 16)
                sp.dma_start(ab[32 * b:32 * b + 32, 1, :], d.B).then_inc(s_w, 16)

            def step(t, s, k, last):
                sp.wait_ge(s_sup, done(t))
                sp.dma_start(d.support[bass.ds(t * P, P), :], sup[s][:, :]).then_inc(s_store[s], 16)
            tiles(sp, step)
            for s in range(SLOTS):
                sp.wait_ge(s_store[s], 16 * ((T - s + 1) // 2))

        @block.gpsimd
        def _(pool):
            scatter_edges(pool, m, d, *share)

        @block.scalar
        def _(act):
            opened(act, s_copied, s_rowall, s_v, s_kexp, s_sup)

            def copy_rows(t, s):
                act.wait_ge(s_flipped, freed(t))
                act.activation(xs[s][:, :].unsqueeze(1), row(m.xn, t), ACT.Copy).then_inc(s_copied, 1)

            def step(t, s, k, last):
                if not last:
                    copy_rows(t + 1, 1 - s)
                act.wait_ge(s_row, done(t))
                act.activation(m.xnT[:, :, bass.ds(t * P, P)], xt[s][:, :, :], ACT.Copy).then_inc(s_rowall, 1)
                act.wait_ge(s_kmin, done(t))
                act.activation(kexp[s][:, :], kmin[s][:, :], ACT.Exp).then_inc(s_kexp, 1)
                act.wait_ge(s_kv, freed(t))
                act.activation(vs[s][:, :, 0:P], vsp[s][:, 0:C].rearrange("p (h c) -> p h c", h=CH),
                               ACT.Copy).then_inc(s_v, 1)
                landed(act, s_store[s], k)
                act.activation(sup[s][:, :], vsp[s][:, C:2 * C], ACT.Copy).then_inc(s_sup, 1)

            copy_rows(0, 0)
            tiles(act, step, peel=True)

        @block.vector
        def _(dve):
            link = Chain(dve, s_chain)
            opened(dve, s_row, s_kmin, s_k)
            for s in range(SLOTS):
                link(dve.memset(vs[s][:, :, P:KVW], 1.0))
            link(dve.memset(g, 0.0))
            link(dve.memset(m.bd[:, :, :], 0.0))
            dve.wait_ge(s_w, 16 * 9)
            for b in range(4):
                for c, (part, sign) in enumerate(QUATERNION[b]):
                    q = slice(32 * b, 32 * b + 32)
                    out = slice(32 * c, 32 * c + 32)
                    src = slice(32 * part, 32 * part + 32)
                    dve.tensor_scalar(g[q, 0, out], ab[q, 0, src], float(sign), None, ALU.mult)
                    dve.tensor_scalar(g[q, 1, P + 32 * c:P + 32 * c + 32], ab[q, 0, src], float(sign), None, ALU.mult)
                    ins = dve.tensor_scalar(g[q, 0, P + 32 * c:P + 32 * c + 32], ab[q, 1, src], float(sign), None, ALU.mult)
            ins.then_inc(s_built, 1)

            def turn(t, s):
                dve.wait_ge(s_flipped, done(t))
                dve.wait_ge(s_proj, freed(t))
                dve.wait_ge(s_rowall, freed(t))
                dve.tensor_copy(xt[s][:, :, :], flip[s][:, 0:C].rearrange("p (h c) -> p h c", h=CH)).then_inc(s_row, 1)

            def step(t, s, k, last):
                dve.wait_ge(s_proj, done(t))
                dve.wait_ge(s_kexp, freed(t))
                dve.tensor_scalar(kmin[s][:, :], kp[s][:, 0:C], 0.0, None, ALU.min).then_inc(s_kmin, 1)
                if not last:
                    turn(t + 1, 1 - s)
                dve.wait_ge(s_kexp, done(t))
                dve.wait_ge(s_kv, freed(t))
                if last:
                    link(dve.tensor_copy(vs[s][:, :, P:KVW], m.lastmask[:, 0:1].unsqueeze(1).to_broadcast([P, CH, 4])))
                dve.scalar_tensor_tensor(out=ks[s][:, :], in0=kp[s][:, 0:C], scalar=0.0, in1=kexp[s][:, :],
                                         op0=ALU.max, op1=ALU.add).then_inc(s_k, 1)

            turn(0, 0)
            tiles(dve, step)
            dve.wait_ge(s_kv, done(T - 1))
            for h in range(CH):
                for i in range(4):
                    q = slice(D0 * i, D0 * i + D0)
                    dve.tensor_copy(m.bd[q, h, q], kv[h][q, q])
                    ins = dve.tensor_copy(m.bd[q, h, P + i:P + i + 1], kv[h][q, P:P + 1])
            link(ins)

        @block.tensor
        def _(pe):
            opened(pe, s_flipped, s_proj, s_kv)
            for h in range(CH):
                pe.matmul(kv[h][:, 0:KVW], m.zeros[:, 0:P], m.zeros[:, 0:KVW], start=True, stop=False)

            def flips(t, s):
                pe.wait_ge(s_copied, done(t))
                pe.wait_ge(s_row, freed(t))
                for h in range(CH):
                    ins = pe.transpose(flip[s][:, h * P:h * P + P], xs[s][:, h * P:h * P + P], m.ident[:, :])
                ins.then_inc(s_flipped, 1)

            def step(t, s, k, last):
                pe.wait_ge(s_row, done(t))
                pe.wait_ge(s_k, freed(t))
                pe.wait_ge(s_v, freed(t))
                pe.wait_ge(s_sup, freed(t))
                for h in range(CH):
                    pe.matmul(kp[s][:, 0:C], xt[s][:, h, :], w[:, h, 0:C], start=h == 0, stop=h == CH - 1)
                for h in range(CH):
                    ins = pe.matmul(vsp[s][:, :], xt[s][:, h, :], w[:, h, C:3 * C], start=h == 0, stop=h == CH - 1)
                ins.then_inc(s_proj, 1)
                if not last:
                    flips(t + 1, 1 - s)
                pe.wait_ge(s_k, done(t))
                pe.wait_ge(s_v, done(t))
                for h in range(CH):
                    ins = pe.matmul(kv[h][:, 0:KVW], ks[s][:, h * P:h * P + P], vs[s][:, h, :],
                                    start=False, stop=last)
                ins.then_inc(s_kv, 1)

            flips(0, 0)
            pe.wait_ge(s_w, 16 * 9)
            pe.wait_ge(s_built, 1)
            tiles(pe, step)



def phase_attend(nc, m, d, share):
    s_w, s_q, s_qmin, s_qexp, s_qs, s_att, s_out, s_chain = m.sems("att", "w q qmin qexp qs att out chain")
    with ExitStack() as mem, nc.Block() as block:
        sb = lambda name, shape, dt=F32: mem.enter_context(nc.sbuf_tensor("att_" + name, shape, dt))
        wq = sb("wq", [P, CH, C])
        qmin = [sb(f"qmin{s}", [P, C]) for s in range(SLOTS)]
        qexp = [sb(f"qexp{s}", [P, C]) for s in range(SLOTS)]
        qs = [sb(f"qs{s}", [P, CH, P]) for s in range(SLOTS)]
        z = [sb(f"z{s}", [P, CH, 4]) for s in range(SLOTS)]
        part = [sb(f"part{s}", [P, C]) for s in range(SLOTS)]
        qp, ap = m.psum[0:2], m.psum[2:4]

        @block.sync
        def _(sp):
            sp.dma_start(wq[:, :, :], d.wqkv[:, 0:C].rearrange("(h p) o -> p h o", p=P)).then_inc(s_w, 16)

        @block.gpsimd
        def _(pool):
            scatter_edges(pool, m, d, *share)

        @block.scalar
        def _(act):
            opened(act, s_qexp)

            def step(t, s, k, last):
                act.wait_ge(s_qmin, done(t))
                act.wait_ge(s_qs, freed(t))
                act.activation(qexp[s][:, :], qmin[s][:, :], ACT.Exp).then_inc(s_qexp, 1)
            tiles(act, step)

        @block.vector
        def _(dve):
            opened(dve, s_qmin, s_qs, s_out)

            def low(t, s):
                dve.wait_ge(s_q, done(t))
                dve.wait_ge(s_qexp, freed(t))
                dve.tensor_scalar(qmin[s][:, :], qp[s][:, 0:C], 0.0, None, ALU.min).then_inc(s_qmin, 1)

            def step(t, s, k, last):
                dve.wait_ge(s_qexp, done(t))
                dve.wait_ge(s_att, freed(t))
                dve.scalar_tensor_tensor(out=qs[s][:, :, :].rearrange("p h c -> p (h c)"), in0=qp[s][:, 0:C],
                                         scalar=0.0, in1=qexp[s][:, :], op0=ALU.max, op1=ALU.add).then_inc(s_qs, 1)
                if not last:
                    low(t + 1, 1 - s)
                dve.wait_ge(s_att, done(t))
                link = Chain(dve, s_chain, t * 3)
                a = ap[s][:, 0:CH * KVW].rearrange("p (h c) -> p h c", h=CH)
                link(dve.tensor_scalar(z[s][:, :, :], a[:, :, P:KVW], 1e-6, None, ALU.add))
                link(dve.reciprocal(z[s][:, :, :], z[s][:, :, :]))
                for h in range(CH):
                    ins = dve.tensor_tensor(part[s][:, h * P:h * P + P].rearrange("p (i c) -> p i c", c=D0),
                                            a[:, h, 0:P].rearrange("p (i c) -> p i c", c=D0),
                                            z[s][:, h, :].unsqueeze(2).to_broadcast([P, 4, D0]), ALU.mult)
                link(ins)
                dve.tensor_tensor(row(m.mix, t), part[s][:, :].unsqueeze(1), row(m.xn, t), ALU.add).then_inc(s_out, 1)

            low(0, 0)
            tiles(dve, step)

        @block.tensor
        def _(pe):
            opened(pe, s_q, s_att)

            def queries(t, s):
                pe.wait_ge(s_qs, freed(t))
                for o in range(CH):
                    for h in range(CH):
                        ins = pe.matmul(qp[s][:, o * P:o * P + P], wq[:, h, o * P:o * P + P],
                                        m.xnT[:, h, bass.ds(t * P, P)], start=h == 0, stop=h == CH - 1)
                ins.then_inc(s_q, 1)

            def step(t, s, k, last):
                if not last:
                    queries(t + 1, 1 - s)
                pe.wait_ge(s_qs, done(t))
                pe.wait_ge(s_out, freed(t))
                for h in range(CH):
                    ins = pe.matmul(ap[s][:, h * KVW:h * KVW + KVW], qs[s][:, h, :], m.bd[:, h, :],
                                    start=True, stop=True)
                ins.then_inc(s_att, 1)

            pe.wait_ge(s_w, 16)
            queries(0, 0)
            tiles(pe, step)



def affine(dve, link, a, gb, i):
    link(dve.tensor_tensor(a, a, gb[:, i:i + 1, :].to_broadcast([P, T, C]), ALU.mult))
    link(dve.tensor_tensor(a, a, gb[:, i + 1:i + 2, :].to_broadcast([P, T, C]), ALU.add))


def phase_mlp(nc, m, d, share):
    s_w, s_copied, s_flipped, s_row, s_hid, s_gelu, s_y, s_out, s_ready, s_wchain, s_wchain2 = m.sems(
        "mlp", "w copied flipped row hid gelu y out ready wchain wchain2")
    norm1, norm2 = m.sems("mlp_n1", NORM), m.sems("mlp_n2", NORM)
    with ExitStack() as mem, nc.Block() as block:
        sb = lambda name, shape, dt=F32: mem.enter_context(nc.sbuf_tensor("mlp_" + name, shape, dt))
        w1 = sb("w1", [P, CH, C])
        w2 = sb("w2", [P, CH, C])
        b1 = sb("b1", [P, CH])
        gb = sb("gb", [P, 5, C])
        small = sb("small", [P, 4, T])
        x1 = sb("x1", [P, T, C])
        tmp = sb("tmp", [P, T, C])
        xs = [sb(f"xs{s}", [P, C]) for s in range(SLOTS)]
        xt = [sb(f"xt{s}", [P, CH, P]) for s in range(SLOTS)]
        hs = [sb(f"hs{s}", [P, CH, P]) for s in range(SLOTS)]
        flip, hp, yp = m.psum[0:2], m.psum[2:4], m.psum[4:6]
        NW = 3 + 5

        @block.sync
        def _(sp):
            sp.dma_start(w1[:, :, :], d.mw1.rearrange("(h p) o -> p h o", p=P)).then_inc(s_w, 16)
            sp.dma_start(w2[:, :, :], d.mw2.rearrange("(h p) o -> p h o", p=P)).then_inc(s_w, 16)
            sp.dma_start(b1[:, :], d.mb1).then_inc(s_w, 16)
            for i, v in enumerate((d.ln1_g, d.ln1_b, d.ln2_g, d.ln2_b, d.mb2)):
                sp.dma_start(gb[:, i, :], v.rearrange("(a c) -> a c", a=1).to_broadcast([P, C])).then_inc(s_w, 16)

        @block.gpsimd
        def _(pool):
            scatter_edges(pool, m, d, *share)

        @block.scalar
        def _(act):
            opened(act, s_copied, s_gelu)
            norm_scalar(act, x1[:, :, :], tmp[:, :, :], small[:, :, :], *norm1)
            act.wait_ge(s_ready, 1)

            def copy_rows(t, s):
                act.wait_ge(s_flipped, freed(t))
                act.activation(xs[s][:, :].unsqueeze(1), row(x1, t), ACT.Copy).then_inc(s_copied, 1)

            def step(t, s, k, last):
                if not last:
                    copy_rows(t + 1, 1 - s)
                act.wait_ge(s_hid, done(t))
                act.wait_ge(s_y, freed(t))
                for h in range(CH):
                    ins = act.activation(hs[s][:, h, :], hp[s][:, h * P:h * P + P], ACT.Gelu, bias=b1[:, h:h + 1])
                ins.then_inc(s_gelu, 1)

            act.wait_ge(s_w, 16 * NW)
            copy_rows(0, 0)
            tiles(act, step)
            norm_scalar(act, x1[:, :, :], tmp[:, :, :], small[:, :, :], *norm2)

        @block.vector
        def _(dve):
            link = norm_vector(dve, m.mix[:, :, :], x1[:, :, :], tmp[:, :, :], small[:, :, :], s_wchain, *norm1)
            dve.wait_ge(s_w, 16 * NW)
            affine(dve, link, x1[:, :, :], gb, 0)
            dve.sem_inc(s_ready, 1)
            opened(dve, s_row, s_out)

            def turn(t, s):
                dve.wait_ge(s_flipped, done(t))
                dve.wait_ge(s_hid, freed(t))
                dve.tensor_copy(xt[s][:, :, :], flip[s][:, 0:C].rearrange("p (h c) -> p h c", h=CH)).then_inc(s_row, 1)

            def step(t, s, k, last):
                if not last:
                    turn(t + 1, 1 - s)
                dve.wait_ge(s_y, done(t))
                dve.tensor_tensor(row(m.mix, t), yp[s][:, 0:C].unsqueeze(1), row(x1, t), ALU.add).then_inc(s_out, 1)

            turn(0, 0)
            tiles(dve, step)
            dve.wait_ge(s_out, done(T - 1))
            link(dve.tensor_tensor(m.mix[:, :, :], m.mix[:, :, :], gb[:, 4:5, :].to_broadcast([P, T, C]), ALU.add))
            link2 = norm_vector(dve, m.mix[:, :, :], x1[:, :, :], tmp[:, :, :], small[:, :, :], s_wchain2, *norm2)
            affine(dve, link2, x1[:, :, :], gb, 2)
            link2(dve.tensor_tensor(m.x[:, :, :], m.x[:, :, :], x1[:, :, :], ALU.add))

        @block.tensor
        def _(pe):
            opened(pe, s_flipped, s_hid, s_y)

            def flips(t, s):
                pe.wait_ge(s_copied, done(t))
                pe.wait_ge(s_row, freed(t))
                for h in range(CH):
                    ins = pe.transpose(flip[s][:, h * P:h * P + P], xs[s][:, h * P:h * P + P], m.ident[:, :])
                ins.then_inc(s_flipped, 1)

            def step(t, s, k, last):
                pe.wait_ge(s_row, done(t))
                pe.wait_ge(s_gelu, freed(t))
                for o in range(CH):
                    for h in range(CH):
                        ins = pe.matmul(hp[s][:, o * P:o * P + P], w1[:, h, o * P:o * P + P], xt[s][:, h, :],
                                        start=h == 0, stop=h == CH - 1)
                ins.then_inc(s_hid, 1)
                if not last:
                    flips(t + 1, 1 - s)
                pe.wait_ge(s_gelu, done(t))
                pe.wait_ge(s_out, freed(t))
                for h in range(CH):
                    ins = pe.matmul(yp[s][:, 0:C], hs[s][:, h, :], w2[:, h, :], start=h == 0, stop=h == CH - 1)
                ins.then_inc(s_y, 1)

            pe.wait_ge(s_w, 16 * NW)
            flips(0, 0)
            tiles(pe, step)



def phase_aggregate(nc, m, d):
    s_rec, s_idx, s_issue, s_hot, s_sum, s_add, s_zero, s_wchain = m.sems("agg", "rec idx issue hot sum add zero wchain")
    s_mean, s_dev, s_sq, s_var, s_vare, s_sd, s_aff, s_tanh = m.sems("agg", "mean dev sq var vare sd aff tanh")
    s_row = m.sems("agg", " ".join(f"row{u}" for u in range(GB)))
    HALF = GB // 2
    OH = 4
    with ExitStack() as mem, nc.Block() as block:
        sb = lambda name, shape, dt=F32: mem.enter_context(nc.sbuf_tensor("agg_" + name, shape, dt))
        acc = sb("acc", [P, T, C])
        tmp = sb("tmp", [P, T, C])
        recs = sb("recs", [P, EBLK, 4])
        bn = sb("bn", [P, 2, C])
        stat = sb("stat", [P, 4, C])
        rows = [sb(f"rows{u}", [P, C]) for u in range(GB)]
        idx = [sb(f"idx{h}", [P, HALF], I32) for h in range(2)]
        hot = [sb(f"hot{u}", [P, P]) for u in range(OH)]
        bank = m.psum[0:OH]

        @block.sync
        def _(sp):
            sp.dma_start(recs[:, :, :].rearrange("p j r -> p (j r)"), d.rec.rearrange("(p j) r -> p (j r)", p=P)).then_inc(s_rec, 16)
            sp.dma_start(bn[:, 0, :], d.bn_w.rearrange("(a c) -> a c", a=1).to_broadcast([P, C])).then_inc(s_rec, 16)
            sp.dma_start(bn[:, 1, :], d.bn_b.rearrange("(a c) -> a c", a=1).to_broadcast([P, C])).then_inc(s_rec, 16)

        @block.gpsimd
        def _(pool):
            pool.wait_ge(s_rec, 48)
            with pool.Fori(0, EBLK // GB) as k:
                for h in range(2):
                    col = k * GB + h * HALF
                    pool.wait_ge(s_sum, col + HALF)
                    pool.tensor_copy(idx[h][:, :], recs.bitcast(I32)[:, bass.ds(col, HALF), 2]).then_inc(s_idx, 1)
                    pool.wait_ge(s_idx, k * 2 + h + 1)
                    pool.sem_inc(s_issue, 1)
                    for u in range(HALF):
                        v = h * HALF + u
                        pool.indirect_dma_start(out=rows[v][:, :], out_offset=None, in_=d.support,
                                                in_offset=bass.IndirectOffsetOnAxis(ap=idx[h][:, u:u + 1], axis=0))\
                            .then_inc(s_row[v], 16)

        @block.vector
        def _(dve):
            dve.memset(acc[:, :, :], 0.0).then_inc(s_zero, 1)
            dve.sem_inc(s_add, OH)
            dve.wait_ge(s_zero, 1)
            dve.wait_ge(s_rec, 48)

            def weigh(j, u):
                dve.wait_ge(s_sum, j + 1 + GB - OH)
                dve.tensor_scalar(hot[u % OH][:, :], m.iota[:, 0:P], recs[:, bass.ds(j, 1), 0], recs[:, bass.ds(j, 1), 1],
                                  ALU.is_equal, ALU.mult).then_inc(s_hot, 1)

            def add(j, u):
                owner = dve.value_load(m.eowner[0:1, bass.ds(j, 1)], min_val=0, max_val=T - 1)
                dve.wait_ge(s_sum, j + GB + 1)
                dve.wait_ge(s_add, j + OH)
                a = acc[:, bass.ds(owner, 1), :]
                dve.tensor_tensor(a, a, bank[u % OH][:, 0:C].unsqueeze(1), ALU.add).then_inc(s_add, 1)

            weigh(0, 0)
            with dve.Fori(0, EBLK // OH - 1) as k:
                for u in range(OH):
                    weigh(k * OH + u + 1, u + 1)
                    add(k * OH + u, u)
            for u in range(OH):
                if u < OH - 1:
                    weigh(EBLK - OH + u + 1, u + 1)
                add(EBLK - OH + u, u)
            link = Chain(dve, s_wchain)
            dve.wait_ge(s_add, EBLK + OH)
            dve.sem_inc(s_mean, 1)
            dve.wait_ge(s_mean, 2)
            mean, var, gain, shift = (stat[:, i, :] for i in range(4))
            link(dve.tensor_scalar(mean, m.psum[4][:, 0:C], 1.0 / N, None, ALU.mult))
            link(dve.tensor_tensor(acc[:, :, :], acc[:, :, :], stat[:, 0:1, :].to_broadcast([P, T, C]), ALU.subtract))
            link(dve.tensor_tensor(tmp[:, :, :], acc[:, :, :], acc[:, :, :], ALU.mult))
            dve.tensor_scalar(tmp[:, T - 1, :], tmp[:, T - 1, :], m.lastmask[:, 0:1], None, ALU.mult).then_inc(s_sq, 1)
            dve.wait_ge(s_var, 1)
            dve.tensor_scalar(var, m.psum[5][:, 0:C], 1.0 / N, 1e-5, ALU.mult, ALU.add).then_inc(s_vare, 1)
            dve.wait_ge(s_sd, 1)
            link(dve.reciprocal(gain, shift))
            link(dve.tensor_tensor(gain, gain, bn[:, 0, :], ALU.mult))
            link(dve.tensor_tensor(acc[:, :, :], acc[:, :, :], stat[:, 2:3, :].to_broadcast([P, T, C]), ALU.mult))
            dve.tensor_tensor(acc[:, :, :], acc[:, :, :], bn[:, 1:2, :].to_broadcast([P, T, C]), ALU.add).then_inc(s_aff, 1)
            dve.wait_ge(s_tanh, 1)
            link(dve.tensor_tensor(m.x[:, :, :], m.x[:, :, :], tmp[:, :, :], ALU.add))

        @block.scalar
        def _(act):
            act.wait_ge(s_vare, 1)
            act.activation(stat[:, 3, :], stat[:, 1, :], ACT.Sqrt).then_inc(s_sd, 1)
            act.wait_ge(s_aff, 1)
            act.activation(tmp[:, :, :], acc[:, :, :], ACT.Tanh).then_inc(s_tanh, 1)

        @block.tensor
        def _(pe):
            pe.sem_inc(s_sum, GB)
            with pe.Fori(0, EBLK // GB) as k:
                for u in range(GB):
                    j = k * GB + u
                    pe.wait_ge(s_hot, j + 1)
                    pe.wait_ge(s_row[u], k * 16 + 16)
                    pe.wait_ge(s_add, j + 1)
                    pe.matmul(bank[u % OH][:, 0:C], hot[u % OH][:, :], rows[u][:, :], start=True, stop=True)\
                      .then_inc(s_sum, 1)

            def over_nodes(out, a):
                pe.matmul(out, m.zeros[:, 0:P], m.zeros[:, 0:C], start=True, stop=False)
                with pe.Fori(0, T - 1) as t:
                    pe.matmul(out, m.ones[:, :], a[:, bass.ds(t, 1), :], start=False, stop=False)
                return pe.matmul(out, m.ones[:, :], a[:, T - 1, :], start=False, stop=True)

            pe.wait_ge(s_mean, 1)
            over_nodes(m.psum[4][:, 0:C], acc).then_inc(s_mean, 1)
            pe.wait_ge(s_sq, 1)
            over_nodes(m.psum[5][:, 0:C], tmp).then_inc(s_var, 1)


def first_best(dve, m, link, score, best, place, tmp):
    wide = lambda a: a.unsqueeze(2).to_broadcast([P, T, X])
    link(dve.tensor_reduce(best, score[:, :, :], AX.X, ALU.max))
    link(dve.tensor_tensor(tmp[:, :, :], score[:, :, :], wide(best), ALU.is_lt))
    link(dve.scalar_tensor_tensor(out=tmp[:, :, :], in0=tmp[:, :, :], scalar=float(X),
                                  in1=m.iota[:, 0:X].unsqueeze(1).to_broadcast([P, T, X]), op0=ALU.mult, op1=ALU.add))
    link(dve.tensor_reduce(place, tmp[:, :, :], AX.X, ALU.min))



def phase_route0(nc, m, d, w1):
    s_w, s_ready, s_copied, s_flipped, s_row, s_gate, s_gated, s_wchain, s_diff, s_exp, s_counts, s_totals, \
        s_pos, s_staged, s_pcopy, s_issue, s_lchain = m.sems(
            "rt0", "w ready copied flipped row gate gated wchain diff exp counts totals pos staged pcopy issue lchain")
    norm = m.sems("rt0_n", NORM)
    s_sent = m.sems("rt0", "sent0 sent1")
    K = 2
    with ExitStack() as mem, nc.Block() as block:
        sb = lambda name, shape, dt=F32: mem.enter_context(nc.sbuf_tensor("rt0_" + name, shape, dt))
        xn = sb("xn", [P, T, C])
        tmp = sb("tmp", [P, T, C])
        small = sb("small", [P, 4, T])
        small6 = sb("small6", [P, 6, 32])
        wg = sb("wg", [P, CH, X])
        bg = sb("bg", [P, X])
        xs = [sb(f"xs{s}", [P, C]) for s in range(SLOTS)]
        xt = [sb(f"xt{s}", [P, CH, P]) for s in range(SLOTS)]
        score = sb("score", [P, T, X])
        equal = sb("equal", [P, T, X])
        top = sb("top", [P, T, K])
        key = sb("key", [P, T, K])
        onehot = sb("onehot", [P, max(K * T, FBLK0) * X])
        count = sb("count", [P, max(K * T, FBLK0) * X])
        pos = sb("pos", [P, T * K])
        ps = [sb(f"ps{s}", [P, K], I32) for s in range(SLOTS)]
        flip, gp = m.psum[0:2], m.psum[2:4]

        @block.sync
        def _(sp):
            sp.dma_start(wg[:, :, :], d.f0_wg.rearrange("(h p) e -> p h e", p=P)).then_inc(s_w, 16)
            sp.dma_start(bg[:, :], d.f0_bg.rearrange("(a c) -> a c", a=1).to_broadcast([P, X])).then_inc(s_w, 16)
            for e in range(X):
                sp.dma_start(w1[:, e, :, :], d.f0_w1[e, :, :].rearrange("(h p) o -> p h o", p=P)).then_inc(m.s_w1, 16)
            sp.wait_ge(m.s_w1, 16 * X)

        @block.scalar
        def _(act):
            opened(act, s_copied, s_staged)
            norm_scalar(act, xn[:, :, :], tmp[:, :, :], small[:, :, :], *norm)
            act.wait_ge(s_ready, 1)

            def step(t, s, k, last):
                act.wait_ge(s_flipped, freed(t))
                act.activation(xs[s][:, :].unsqueeze(1), row(xn, t), ACT.Copy).then_inc(s_copied, 1)
            tiles(act, step)
            act.wait_ge(s_diff, 1)
            act.activation(m.prob[:, :, 1], top[:, :, 1], ACT.Exp).then_inc(s_exp, 1)
            act.wait_ge(s_flipped, done(T - 1))

            def stage(t, s, k, last):
                landed(act, s_sent[s], k, K)
                act.activation(xs[s][:, :].unsqueeze(1), row(xn, t), ACT.Copy).then_inc(s_staged, 1)
            tiles(act, stage, peel=True)

        @block.vector
        def _(dve):
            norm_vector(dve, m.x[:, :, :], xn[:, :, :], tmp[:, :, :], small[:, :, :], s_wchain, *norm)
            dve.sem_inc(s_ready, 1)
            dve.wait_ge(s_w, 32)
            opened(dve, s_row, s_gated)

            def turn(t, s):
                dve.wait_ge(s_flipped, done(t))
                dve.wait_ge(s_gate, freed(t))
                dve.tensor_copy(xt[s][:, :, :], flip[s][:, 0:C].rearrange("p (h c) -> p h c", h=CH)).then_inc(s_row, 1)

            def step(t, s, k, last):
                if not last:
                    turn(t + 1, 1 - s)
                dve.wait_ge(s_gate, done(t))
                dve.tensor_tensor(row(score, t), gp[s][:, 0:X].unsqueeze(1), bg[:, :].unsqueeze(1), ALU.add).then_inc(s_gated, 1)

            turn(0, 0)
            tiles(dve, step)
            dve.wait_ge(s_gated, done(T - 1))
            link = Chain(dve, s_lchain)
            first_best(dve, m, link, score, top[:, :, 0], key[:, :, 0], equal)
            link(dve.tensor_tensor(equal[:, :, :], m.iota[:, 0:X].unsqueeze(1).to_broadcast([P, T, X]),
                                   key[:, :, 0].unsqueeze(2).to_broadcast([P, T, X]), ALU.is_equal))
            link(dve.scalar_tensor_tensor(out=score[:, :, :], in0=equal[:, :, :], scalar=-3e38, in1=score[:, :, :],
                                          op0=ALU.mult, op1=ALU.add))
            first_best(dve, m, link, score, top[:, :, 1], key[:, :, 1], equal)
            dve.tensor_tensor(top[:, :, 1], top[:, :, 1], top[:, :, 0], ALU.subtract).then_inc(s_diff, 1)
            dve.wait_ge(s_exp, 1)
            link(dve.tensor_scalar(m.prob[:, :, 0], m.prob[:, :, 1], 1.0, None, ALU.add))
            link(dve.reciprocal(m.prob[:, :, 0], m.prob[:, :, 0]))
            link(dve.tensor_tensor(m.prob[:, :, 1], m.prob[:, :, 1], m.prob[:, :, 0], ALU.mult))
            sort_vector(dve, m, link, key[:, :, :].rearrange("p t k -> p (t k)"), onehot, count, small6, m.psum[4],
                        pos[:, :], m.fown[:, 0:FBLK0], s_counts, s_totals, X, K * T, FBLK0)
            dve.tensor_copy(m.fpos[:, 0:K * T], pos[:, :]).then_inc(s_pos, 1)

        @block.tensor
        def _(pe):
            opened(pe, s_flipped, s_gate)
            pe.wait_ge(s_w, 32)

            def flips(t, s):
                pe.wait_ge(s_copied, done(t))
                pe.wait_ge(s_row, freed(t))
                for h in range(CH):
                    ins = pe.transpose(flip[s][:, h * P:h * P + P], xs[s][:, h * P:h * P + P], m.ident[:, :])
                ins.then_inc(s_flipped, 1)

            def step(t, s, k, last):
                pe.wait_ge(s_row, done(t))
                pe.wait_ge(s_gated, freed(t))
                for h in range(CH):
                    ins = pe.matmul(gp[s][:, 0:X], xt[s][:, h, :], wg[:, h, :], start=h == 0, stop=h == CH - 1)
                ins.then_inc(s_gate, 1)
                if not last:
                    flips(t + 1, 1 - s)

            flips(0, 0)
            tiles(pe, step)
            sort_tensor(pe, m, small6, m.psum[4], s_counts, s_totals, X)

        @block.gpsimd
        def _(pool):
            pool.wait_ge(s_pos, 1)

            def step(t, s, k, last):
                pool.wait_ge(s_staged, done(t))
                landed(pool, s_sent[s], k, K)
                pool.tensor_copy(ps[s][:, :], m.fpos[:, bass.ds(t * K, K)]).then_inc(s_pcopy, 1)
                pool.wait_ge(s_pcopy, t + 1)
                pool.sem_inc(s_issue, 1)
                for u in range(K):
                    pool.indirect_dma_start(out=d.xs0, out_offset=bass.IndirectOffsetOnAxis(ap=ps[s][:, u:u + 1], axis=0),
                                            in_=xs[s][:, :], in_offset=None).then_inc(s_sent[s], 16)
            tiles(pool, step, peel=True)
            for s in range(SLOTS):
                pool.wait_ge(s_sent[s], 16 * K * ((T - s + 1) // 2))



def phase_experts0(nc, m, d, w1):
    s_w, s_flipped, s_row, s_hid, s_held, s_turned, s_bias, s_relu, s_y, s_out = m.sems(
        "ex0", "w flipped row hid held turned bias relu y out")
    s_load, s_store = m.sems("ex0", "load0 load1"), m.sems("ex0", "store0 store1")
    s_w2 = m.sem("ex0_w2")
    NF = HID // 512
    with ExitStack() as mem, nc.Block() as block:
        sb = lambda name, shape, dt=F32: mem.enter_context(nc.sbuf_tensor("ex0_" + name, shape, dt))
        w2 = sb("w2", [P, X, HC, C])
        b1 = sb("b1", [P, X, HC])
        b2 = sb("b2", [P, X, C])
        xin = [sb(f"xin{s}", [P, C]) for s in range(SLOTS)]
        xt = [sb(f"xt{s}", [P, CH, P]) for s in range(SLOTS)]
        h = sb("h", [P, HID])
        hb = sb("hb", [P, HC, P])
        hs = [sb(f"hs{s}", [P, HC, P]) for s in range(SLOTS)]
        ys = [sb(f"ys{s}", [P, C]) for s in range(SLOTS)]
        hp = [m.psum[0:2], m.psum[2:4]]
        tp, flip, yp = m.psum[4:6], m.psum[6], m.psum[7]
        loop = lambda eng, step: tiles(eng, step, FBLK0)

        @block.sync
        def _(sp):
            sp.dma_start(b1[:, :, :], d.f0_b1).then_inc(s_w, 16)
            sp.dma_start(b2[:, :, :].rearrange("p e c -> p (e c)"),
                         d.f0_b2.rearrange("e c -> (e c)").rearrange("(a c) -> a c", a=1).to_broadcast([P, X * C])).then_inc(s_w, 16)

            def step(j, s, k, last):
                sp.wait_ge(s_flipped, freed(j))
                sp.dma_start(xin[s][:, :], d.xs0[bass.ds(j * P, P), :]).then_inc(s_load[s], 16)
            loop(sp, step)

        @block.gpsimd
        def _(pool):
            for e in range(X):
                pool.dma_start(w2[:, e, :, :], d.f0_w2[e, :, :].rearrange("(h p) o -> p h o", p=P)).then_inc(s_w2, 16)
            def step(j, s, k, last):
                pool.wait_ge(s_out, done(j))
                pool.dma_start(d.ys0[bass.ds(j * P, P), :], ys[s][:, :]).then_inc(s_store[s], 16)
            loop(pool, step)
            for s in range(SLOTS):
                pool.wait_ge(s_store[s], 16 * ((FBLK0 - s + 1) // 2))

        @block.scalar
        def _(act):
            opened(act, s_held, s_relu)

            def step(j, s, k, last):
                act.wait_ge(s_hid, done(j))
                act.wait_ge(s_turned, done(j) - 1)
                for n in range(NF):
                    ins = act.activation(h[:, n * 512:n * 512 + 512], hp[s][n][:, :], ACT.Copy)
                ins.then_inc(s_held, 1)
                act.wait_ge(s_bias, done(j))
                act.wait_ge(s_y, freed(j))
                act.activation(hs[s][:, :, :], hb[:, :, :], ACT.Relu).then_inc(s_relu, 1)
            loop(act, step)

        @block.vector
        def _(dve):
            opened(dve, s_row, s_bias, s_out)
            dve.wait_ge(s_w, 32)

            def turn(j, s):
                dve.wait_ge(s_flipped, done(j))
                dve.wait_ge(s_hid, freed(j))
                dve.tensor_copy(xt[s][:, :, :], flip[:, 0:C].rearrange("p (h c) -> p h c", h=CH)).then_inc(s_row, 1)

            def result(j, s, k):
                e = dve.value_load(m.fown[0:1, bass.ds(j, 1)], min_val=0, max_val=X - 1)
                dve.wait_ge(s_y, done(j))
                landed(dve, s_store[s], k)
                dve.tensor_tensor(ys[s][:, :].unsqueeze(1), yp[:, 0:C].unsqueeze(1), b2[:, bass.ds(e, 1), :], ALU.add).then_inc(s_out, 1)

            def biases(j, s):
                e = dve.value_load(m.fown[0:1, bass.ds(j, 1)], min_val=0, max_val=X - 1)
                dve.wait_ge(s_turned, done(j))
                dve.wait_ge(s_relu, done(j) - 1)
                for n in range(NF):
                    half = HC // NF
                    ins = dve.tensor_tensor(hb[:, n * half:n * half + half, :].unsqueeze(1),
                                            tp[n][:, :].rearrange("p (m c) -> p m c", c=P).unsqueeze(1),
                                            b1[:, bass.ds(e, 1), n * half:n * half + half].unsqueeze(3).to_broadcast([P, 1, half, P]),
                                            ALU.add)
                ins.then_inc(s_bias, 1)

            turn(0, 0)
            turn(1, 1)
            biases(0, 0)

            def step(i, s, k, last):
                if not last:
                    turn(i + 2, s)
                result(i, s, k)
                biases(i + 1, 1 - s)
            tiles(dve, step, FBLK0 - 1, peel=True)
            result(FBLK0 - 1, (FBLK0 - 1) % 2, (FBLK0 - 1) // 2)

        @block.tensor
        def _(pe):
            opened(pe, s_flipped, s_hid, s_turned, s_y)

            def flips(j, s, k):
                pe.wait_ge(s_load[s], 16 * k + 16)
                pe.wait_ge(s_row, done(j) - 1)
                for c in range(CH):
                    ins = pe.transpose(flip[:, c * P:c * P + P], xin[s][:, c * P:c * P + P], m.ident[:, :])
                ins.then_inc(s_flipped, 1)

            def hidden(j, s):
                e = pe.value_load(m.fown[0:1, bass.ds(j, 1)], min_val=0, max_val=X - 1)
                pe.wait_ge(s_row, done(j))
                pe.wait_ge(s_held, freed(j))
                for n in range(NF):
                    for c in range(CH):
                        ins = pe.matmul(hp[s][n][:, :], xt[s][:, c, :],
                                        w1[:, bass.ds(e, 1), c, n * 512:n * 512 + 512], start=c == 0, stop=c == CH - 1)
                ins.then_inc(s_hid, 1)

            def turns(j):
                pe.wait_ge(s_held, done(j))
                pe.wait_ge(s_bias, done(j) - 1)
                for q in range(HC):
                    ins = pe.transpose(tp[q // 4][:, q % 4 * P:q % 4 * P + P], h[:, q * P:q * P + P], m.ident[:, :])
                ins.then_inc(s_turned, 1)

            def result(j, s):
                e = pe.value_load(m.fown[0:1, bass.ds(j, 1)], min_val=0, max_val=X - 1)
                pe.wait_ge(s_relu, done(j))
                pe.wait_ge(s_out, done(j) - 1)
                for q in range(HC):
                    ins = pe.matmul(yp[:, 0:C], hs[s][:, q, :], w2[:, bass.ds(e, 1), q, :], start=q == 0, stop=q == HC - 1)
                ins.then_inc(s_y, 1)

            pe.wait_ge(m.s_w1, 16 * X)
            flips(0, 0, 0)
            hidden(0, 0)
            flips(1, 1, 0)
            turns(0)
            pe.wait_ge(s_w2, 16 * X)

            def step(i, s, k, last):
                hidden(i + 1, 1 - s)
                if not last:
                    flips(i + 2, s, k + 1)
                result(i, s)
                turns(i + 1)
            tiles(pe, step, FBLK0 - 1)
            result(FBLK0 - 1, (FBLK0 - 1) % 2)



def phase_combine(nc, m, name, d_ys, K):
    s_pcopy, s_issue, s_added, s_chain = m.sems(name, "pcopy issue added chain")
    s_got = m.sems(name, "got0 got1")
    with ExitStack() as mem, nc.Block() as block:
        sb = lambda n, shape, dt=F32: mem.enter_context(nc.sbuf_tensor(name + n, shape, dt))
        rows = [[sb(f"rows{s}{u}", [P, C]) for u in range(K)] for s in range(SLOTS)]
        ps = [sb(f"ps{s}", [P, K], I32) for s in range(SLOTS)]

        @block.gpsimd
        def _(pool):
            def step(t, s, k, last):
                pool.wait_ge(s_added, freed(t))
                pool.tensor_copy(ps[s][:, :], m.fpos[:, bass.ds(t * K, K)]).then_inc(s_pcopy, 1)
                pool.wait_ge(s_pcopy, t + 1)
                pool.sem_inc(s_issue, 1)
                for u in range(K):
                    pool.indirect_dma_start(out=rows[s][u][:, :], out_offset=None, in_=d_ys,
                                            in_offset=bass.IndirectOffsetOnAxis(ap=ps[s][:, u:u + 1], axis=0)).then_inc(s_got[s], 16)
            tiles(pool, step)

        @block.vector
        def _(dve):
            opened(dve, s_added)

            def step(t, s, k, last):
                dve.wait_ge(s_got[s], 16 * K * (k + 1))
                for u in range(K):
                    ins = dve.scalar_tensor_tensor(out=row(m.x, t), in0=rows[s][u][:, :].unsqueeze(1),
                                                   scalar=m.prob[:, bass.ds(t, 1), u], in1=row(m.x, t), op0=ALU.mult, op1=ALU.add)
                    if u < K - 1:
                        Chain(dve, s_chain, t * (K - 1) + u)(ins)
                ins.then_inc(s_added, 1)
            tiles(dve, step)



def phase_project1(nc, m, d):
    s_w, s_ready, s_copied, s_flipped, s_row, s_rowall, s_proj, s_held, s_xt, s_wchain, s_kchain, s_kv, s_vcopy, \
        s_block, s_r, s_rheld, s_m, s_kready = m.sems(
            "pr1", "w ready copied flipped row rowall proj held xt wchain kchain kv vcopy block r rheld m kready")
    norm, knorm = m.sems("pr1_n", NORM), m.sems("pr1_k", NORM)
    s_store = m.sems("pr1", "store0 store1")
    G = 2 * H1
    with ExitStack() as mem, nc.Block() as block:
        sb = lambda name, shape, dt=F32: mem.enter_context(nc.sbuf_tensor("pr1_" + name, shape, dt))
        w = sb("w", [P, CH, 3 * C])
        wo = sb("wo", [P, CH, C])
        wq = sb("wq", [P, CH, C])
        gb = sb("gb", [P, 2, G * D1])
        xn = sb("xn", [P, T, C])
        big = sb("big", [P, T * G, D1])
        kv = sb("kv", [P, T * G, D1])
        small = sb("small", [P, 4, T * G])
        xs = [sb(f"xs{s}", [P, C]) for s in range(SLOTS)]
        xt = [sb(f"xt{s}", [P, CH, P]) for s in range(SLOTS)]
        gr = [sb(f"gr{s}", [P, C]) for s in range(SLOTS)]
        bd = sb("bd", [P, CH, P])
        r_ = xn[:, 0:CH, :]
        flip, kvp, grp, acc = m.psum[0:2], m.psum[2:4], m.psum[4:6], m.psum[6:8]
        tmp = big[:, 0:T * C // D1, :].rearrange("p (t g) c -> p t (g c)", t=T)
        kvt = kv[:, :, :].rearrange("p (t g) c -> p t (g c)", t=T)
        NW = 5 + 4 * H1

        @block.sync
        def _(sp):
            for i, a in enumerate((d.wk, d.wv, d.g_w)):
                sp.dma_start(w[:, :, i * C:i * C + C], a.rearrange("(h p) o -> p h o", p=P)).then_inc(s_w, 16)
            sp.dma_start(wo[:, :, :], d.wo.rearrange("(h p) o -> p h o", p=P)).then_inc(s_w, 16)
            sp.dma_start(wq[:, :, :], d.wq.rearrange("(h p) o -> p h o", p=P)).then_inc(s_w, 16)
            for i, pair in enumerate(((d.k_g, d.v_g), (d.k_b, d.v_b))):
                for g in range(G):
                    v = pair[g // H1]
                    sp.dma_start(gb[:, i, g * D1:g * D1 + D1], v.rearrange("(a c) -> a c", a=1).to_broadcast([P, D1])).then_inc(s_w, 16)

            def step(t, s, k, last):
                sp.wait_ge(s_xt, done(t))
                sp.dma_start(d.graph[bass.ds(t * P, P), :], gr[s][:, :]).then_inc(s_store[s], 16)
            tiles(sp, step)
            for s in range(SLOTS):
                sp.wait_ge(s_store[s], 16 * ((T - s + 1) // 2))

        @block.scalar
        def _(act):
            opened(act, s_copied, s_rowall, s_xt, s_vcopy)
            norm_scalar(act, xn[:, :, :], tmp, small, *norm)
            act.wait_ge(s_ready, 1)

            def copy_rows(t, s):
                act.wait_ge(s_flipped, freed(t))
                act.activation(xs[s][:, :].unsqueeze(1), row(xn, t), ACT.Copy).then_inc(s_copied, 1)

            def step(t, s, k, last):
                if not last:
                    copy_rows(t + 1, 1 - s)
                act.wait_ge(s_row, done(t))
                act.activation(m.xnT[:, :, bass.ds(t * P, P)], xt[s][:, :, :], ACT.Copy).then_inc(s_rowall, 1)
                act.wait_ge(s_proj, done(t))
                landed(act, s_store[s], k)
                act.activation(gr[s][:, :], grp[s][:, 0:C], ACT.Copy).then_inc(s_xt, 1)
            copy_rows(0, 0)
            tiles(act, step, peel=True)
            norm_scalar(act, kv[:, :, :], big[:, :, :], small, *knorm, groups=T * G)
            act.wait_ge(s_kready, 1)

            def vstep(t, s, k, last):
                act.wait_ge(s_kv, freed(t))
                act.activation(xs[s][:, :].unsqueeze(1), row(kvt, t)[:, :, C:2 * C], ACT.Copy).then_inc(s_vcopy, 1)
            tiles(act, vstep)

        @block.vector
        def _(dve):
            norm_vector(dve, m.x[:, :, :], xn[:, :, :], tmp, small, s_wchain, *norm)
            dve.sem_inc(s_ready, 1)
            opened(dve, s_row, s_held)

            def turn(t, s):
                dve.wait_ge(s_flipped, done(t))
                dve.wait_ge(s_proj, freed(t))
                dve.wait_ge(s_rowall, freed(t))
                dve.tensor_copy(xt[s][:, :, :], flip[s][:, 0:C].rearrange("p (h c) -> p h c", h=CH)).then_inc(s_row, 1)

            def step(t, s, k, last):
                if not last:
                    turn(t + 1, 1 - s)
                dve.wait_ge(s_proj, done(t))
                dve.tensor_copy(row(kvt, t), kvp[s][:, :].unsqueeze(1)).then_inc(s_held, 1)
            turn(0, 0)
            tiles(dve, step)
            dve.wait_ge(s_held, done(T - 1))
            link = norm_vector(dve, kv[:, :, :], kv[:, :, :], big[:, :, :], small, s_kchain, *knorm,
                               groups=T * G, width=D1)
            dve.wait_ge(s_w, 16 * NW)
            link(dve.tensor_tensor(kvt, kvt, gb[:, 0:1, :].to_broadcast([P, T, G * D1]), ALU.mult))
            link(dve.tensor_tensor(kvt, kvt, gb[:, 1:2, :].to_broadcast([P, T, G * D1]), ALU.add))
            link(dve.tensor_scalar(kvt[:, T - 1, 0:C], kvt[:, T - 1, 0:C], m.lastmask[:, 0:1], None, ALU.mult))
            link(dve.memset(bd[:, :, :], 0.0))
            dve.sem_inc(s_kready, 1)
            dve.wait_ge(s_kv, done(T - 1))
            for h in range(CH):
                for i in range(P // D1):
                    q = slice(D1 * i, D1 * i + D1)
                    ins = dve.tensor_scalar(bd[q, h, q], acc[h][q, q], 1.0 / N, None, ALU.mult)
            ins.then_inc(s_block, 1)
            dve.wait_ge(s_r, 1)
            for h in range(CH):
                ins = dve.tensor_copy(r_[:, h, :], m.psum[h][:, 0:C])
            ins.then_inc(s_rheld, 1)
            dve.wait_ge(s_m, 1)
            for h in range(CH):
                ins = dve.tensor_copy(m.mixer[:, h, :], m.psum[2 + h][:, 0:C])
            link(ins)

        @block.tensor
        def _(pe):
            opened(pe, s_flipped, s_proj, s_kv)
            for h in range(CH):
                pe.matmul(acc[h][:, 0:P], m.zeros[:, 0:P], m.zeros[:, 0:P], start=True, stop=False)

            def flips(t, s):
                pe.wait_ge(s_copied, done(t))
                pe.wait_ge(s_row, freed(t))
                for h in range(CH):
                    ins = pe.transpose(flip[s][:, h * P:h * P + P], xs[s][:, h * P:h * P + P], m.ident[:, :])
                ins.then_inc(s_flipped, 1)

            def step(t, s, k, last):
                pe.wait_ge(s_row, done(t))
                pe.wait_ge(s_held, freed(t))
                pe.wait_ge(s_xt, freed(t))
                for h in range(CH):
                    pe.matmul(kvp[s][:, :], xt[s][:, h, :], w[:, h, 0:2 * C], start=h == 0, stop=h == CH - 1)
                for h in range(CH):
                    ins = pe.matmul(grp[s][:, 0:C], xt[s][:, h, :], w[:, h, 2 * C:3 * C], start=h == 0, stop=h == CH - 1)
                ins.then_inc(s_proj, 1)
                if not last:
                    flips(t + 1, 1 - s)
            flips(0, 0)
            pe.wait_ge(s_w, 16 * NW)
            tiles(pe, step)

            def kstep(t, s, k, last):
                pe.wait_ge(s_vcopy, done(t))
                for h in range(CH):
                    ins = pe.matmul(acc[h][:, 0:P], xs[s][:, h * P:h * P + P], row(kvt, t)[:, :, h * P:h * P + P],
                                    start=False, stop=last)
                ins.then_inc(s_kv, 1)
            tiles(pe, kstep)
            pe.wait_ge(s_block, 1)
            for h in range(CH):
                ins = pe.matmul(m.psum[h][:, 0:C], bd[:, h, :], wo[:, h, :], start=True, stop=True)
            ins.then_inc(s_r, 1)
            pe.wait_ge(s_rheld, 1)
            for c in range(CH):
                for h in range(CH):
                    ins = pe.matmul(m.psum[2 + c][:, 0:C], wq[:, h, c * P:c * P + P], r_[:, h, :], start=h == 0, stop=h == CH - 1)
            ins.then_inc(s_m, 1)



def phase_graph1(nc, m, d):
    s_w, s_copied, s_y, s_out, s_idx, s_pcopy, s_issue, s_moved, s_chain, s_exp, s_exped = m.sems(
        "gr1", "w copied y out idx pcopy issue moved chain exp exped")
    s_got = m.sems("gr1", "got0 got1")
    with ExitStack() as mem, nc.Block() as block:
        sb = lambda name, shape, dt=F32: mem.enter_context(nc.sbuf_tensor("gr1_" + name, shape, dt))
        bo = sb("bo", [P, C])
        attn = sb("attn", [P, 2, C])
        idx = sb("idx", [P, T, 2], I32)
        ps = [sb(f"ps{s}", [P, 2], I32) for s in range(SLOTS)]
        got = [sb(f"got{s}", [P, 2, C]) for s in range(SLOTS)]
        ends = sb("ends", [P, 2, T, C])
        prod = sb("prod", [P, 2, T, C])
        logit = sb("logit", [P, T, H1])
        tmp = sb("tmp", [P, T, H1])
        one = sb("one", [P, T])
        mean = sb("mean", [P, T, D1])
        xt = [sb(f"xt{s}", [P, CH, P]) for s in range(SLOTS)]
        yp = m.psum[0:2]

        @block.sync
        def _(sp):
            sp.dma_start(bo[:, :], d.bo.rearrange("(a c) -> a c", a=1).to_broadcast([P, C])).then_inc(s_w, 16)
            sp.dma_start(attn[:, 0, :], d.g_al.rearrange("h c -> (h c)").rearrange("(a c) -> a c", a=1).to_broadcast([P, C])).then_inc(s_w, 16)
            sp.dma_start(attn[:, 1, :], d.g_ar.rearrange("h c -> (h c)").rearrange("(a c) -> a c", a=1).to_broadcast([P, C])).then_inc(s_w, 16)
            sp.wait_ge(s_idx, 1)
            sp.dma_start(idx[:, 0:T - 1, :], d.ends).then_inc(s_w, 16)
            sp.dma_start(idx[0:LAST, T - 1, :], d.ends_last).then_inc(s_w, 16)

        @block.gpsimd
        def _(pool):
            pool.memset(idx[:, :, :], 0).then_inc(s_idx, 1)
            pool.wait_ge(s_w, 80)

            def step(t, s, k, last):
                pool.wait_ge(s_moved, freed(t))
                pool.tensor_copy(ps[s][:, :].unsqueeze(1), row(idx, t)).then_inc(s_pcopy, 1)
                pool.wait_ge(s_pcopy, t + 1)
                pool.sem_inc(s_issue, 1)
                for u in range(2):
                    pool.indirect_dma_start(out=got[s][:, u, :], out_offset=None, in_=d.graph,
                                            in_offset=bass.IndirectOffsetOnAxis(ap=ps[s][:, u:u + 1], axis=0)).then_inc(s_got[s], 16)
            tiles(pool, step)

        @block.scalar
        def _(act):
            opened(act, s_copied, s_moved)

            def step(t, s, k, last):
                act.wait_ge(s_y, freed(t))
                act.activation(xt[s][:, :, :], m.xnT[:, :, bass.ds(t * P, P)], ACT.Copy).then_inc(s_copied, 1)
                act.wait_ge(s_got[s], 32 * (k + 1))
                act.activation(ends[:, :, bass.ds(t, 1), :], got[s][:, :, :].unsqueeze(2), ACT.Copy).then_inc(s_moved, 1)
            tiles(act, step)
            act.wait_ge(s_exp, 1)
            act.activation(tmp[:, :, :], logit[:, :, :], ACT.Exp).then_inc(s_exped, 1)

        @block.tensor
        def _(pe):
            opened(pe, s_y)

            def step(t, s, k, last):
                pe.wait_ge(s_copied, done(t))
                pe.wait_ge(s_out, freed(t))
                for h in range(CH):
                    ins = pe.matmul(yp[s][:, 0:C], xt[s][:, h, :], m.mixer[:, h, :], start=h == 0, stop=h == CH - 1)
                ins.then_inc(s_y, 1)
            tiles(pe, step)

        @block.vector
        def _(dve):
            opened(dve, s_out)

            def step(t, s, k, last):
                dve.wait_ge(s_y, done(t))
                dve.tensor_tensor(row(m.x, t), yp[s][:, 0:C].unsqueeze(1), row(m.x, t), ALU.add).then_inc(s_out, 1)
            tiles(dve, step)
            dve.wait_ge(s_out, done(T - 1))
            link = Chain(dve, s_chain)
            dve.wait_ge(s_w, 80)
            link(dve.tensor_tensor(m.x[:, :, :], m.x[:, :, :], bo[:, :].unsqueeze(1).to_broadcast([P, T, C]), ALU.add))
            dve.wait_ge(s_moved, done(T - 1))
            for u in range(2):
                ins = dve.tensor_tensor(prod[:, u, :, :], ends[:, u, :, :], attn[:, u:u + 1, :].to_broadcast([P, T, C]), ALU.mult)
            link(ins)
            link(dve.tensor_tensor(prod[:, 0, :, :], prod[:, 0, :, :], prod[:, 1, :, :], ALU.add))
            link(dve.tensor_reduce(logit[:, :, :], prod[:, 0, :, :].rearrange("p t (h c) -> p t h c", h=H1), AX.X, ALU.add))
            link(dve.scalar_tensor_tensor(out=logit[:, :, :], in0=logit[:, :, :], scalar=0.01, in1=logit[:, :, :], op0=ALU.mult, op1=ALU.max))
            link(dve.tensor_reduce(one[:, :], logit[:, :, :], AX.X, ALU.max))
            dve.tensor_tensor(logit[:, :, :], logit[:, :, :], one[:, :].unsqueeze(2).to_broadcast([P, T, H1]), ALU.subtract).then_inc(s_exp, 1)
            dve.wait_ge(s_exped, 1)
            link(dve.tensor_reduce(one[:, :], tmp[:, :, :], AX.X, ALU.add))
            link(dve.reciprocal(one[:, :], one[:, :]))
            link(dve.tensor_tensor(logit[:, :, :], tmp[:, :, :], one[:, :].unsqueeze(2).to_broadcast([P, T, H1]), ALU.mult))
            link(dve.tensor_tensor(prod[:, 0, :, :].rearrange("p t (h c) -> p t h c", h=H1),
                                   ends[:, 1, :, :].rearrange("p t (h c) -> p t h c", h=H1),
                                   logit[:, :, :].unsqueeze(3).to_broadcast([P, T, H1, D1]), ALU.mult))
            link(dve.tensor_reduce(mean[:, :, :], prod[:, 0, :, :].rearrange("p t (h c) -> p t c h", h=H1), AX.X, ALU.add))
            x4 = m.x[:, :, :].rearrange("p t (h c) -> p t h c", h=H1)
            link(dve.tensor_tensor(x4, x4, mean[:, :, :].unsqueeze(2).to_broadcast([P, T, H1, D1]), ALU.add))



def hidden_turned(pe, hp, w1, xt):
    for q in range(HC):
        for h in range(CH):
            ins = pe.matmul(hp[q // 4][:, q % 4 * P:q % 4 * P + P], w1[:, h, q * P:q * P + P], xt[:, h, :],
                            start=h == 0, stop=h == CH - 1)
    return ins


def phase_route1(nc, m, d):
    s_ready, s_copied, s_flipped, s_row, s_hid, s_gelu, s_gate, s_gated, s_wchain, s_diff, s_exp, s_counts, s_totals, \
        s_pos, s_staged, s_pcopy, s_issue, s_lchain, s_w = m.sems(
            "rt1", "ready copied flipped row hid gelu gate gated wchain diff exp counts totals pos staged pcopy issue lchain w")
    norm = m.sems("rt1_n", NORM)
    s_sent = m.sems("rt1", "sent0 sent1")
    with ExitStack() as mem, nc.Block() as block:
        sb = lambda name, shape, dt=F32: mem.enter_context(nc.sbuf_tensor("rt1_" + name, shape, dt))
        xn = sb("xn", [P, T, C])
        tmp = sb("tmp", [P, T, C])
        small = sb("small", [P, 4, T])
        small6 = sb("small6", [P, 6, 32])
        wg = sb("wg", [P, HC, X])
        bg = sb("bg", [P, X])
        xs = [sb(f"xs{s}", [P, C]) for s in range(SLOTS)]
        xt = [sb(f"xt{s}", [P, CH, P]) for s in range(SLOTS)]
        hs = [sb(f"hs{s}", [P, HC, P]) for s in range(SLOTS)]
        score = sb("score", [P, T, X])
        equal = sb("equal", [P, T, X])
        best = sb("best", [P, T])
        key = sb("key", [P, T])
        onehot = sb("onehot", [P, max(T, FBLK1) * X])
        count = sb("count", [P, max(T, FBLK1) * X])
        pos = sb("pos", [P, T])
        ps = [sb(f"ps{s}", [P, 1], I32) for s in range(SLOTS)]
        flip, gp, hp = m.psum[0:2], m.psum[2:4], [m.psum[4:6], m.psum[6:8]]

        @block.sync
        def _(sp):
            sp.dma_start(m.f1_w1[:, :, :], d.f1_w1.rearrange("(h p) o -> p h o", p=P)).then_inc(s_w, 16)
            sp.dma_start(m.f1_b1[:, :], d.f1_b1).then_inc(s_w, 16)
            sp.dma_start(wg[:, :, :], d.f1_wg.rearrange("(q p) e -> p q e", p=P)).then_inc(s_w, 16)
            sp.dma_start(bg[:, :], d.f1_bg.rearrange("(a c) -> a c", a=1).to_broadcast([P, X])).then_inc(s_w, 16)
            sp.wait_ge(s_w, 64)

        @block.scalar
        def _(act):
            opened(act, s_copied, s_gelu, s_staged)
            norm_scalar(act, xn[:, :, :], tmp[:, :, :], small[:, :, :], *norm)
            act.wait_ge(s_ready, 1)
            act.wait_ge(s_w, 64)

            def copy_rows(t, s):
                act.wait_ge(s_flipped, freed(t))
                act.activation(xs[s][:, :].unsqueeze(1), row(xn, t), ACT.Copy).then_inc(s_copied, 1)

            def step(t, s, k, last):
                if not last:
                    copy_rows(t + 1, 1 - s)
                act.wait_ge(s_hid, done(t))
                act.wait_ge(s_gate, freed(t))
                for q in range(HC):
                    ins = act.activation(hs[s][:, q, :], hp[s][q // 4][:, q % 4 * P:q % 4 * P + P], ACT.Gelu, bias=m.f1_b1[:, q:q + 1])
                ins.then_inc(s_gelu, 1)
            copy_rows(0, 0)
            tiles(act, step)
            act.wait_ge(s_diff, 1)
            act.activation(score[:, :, :], equal[:, :, :], ACT.Exp).then_inc(s_exp, 1)

            def stage(t, s, k, last):
                landed(act, s_sent[s], k)
                act.activation(xs[s][:, :].unsqueeze(1), row(xn, t), ACT.Copy).then_inc(s_staged, 1)
            act.wait_ge(s_flipped, done(T - 1))
            tiles(act, stage, peel=True)

        @block.vector
        def _(dve):
            norm_vector(dve, m.x[:, :, :], xn[:, :, :], tmp[:, :, :], small[:, :, :], s_wchain, *norm)
            dve.sem_inc(s_ready, 1)
            dve.wait_ge(s_w, 64)
            opened(dve, s_row, s_gated)

            def turn(t, s):
                dve.wait_ge(s_flipped, done(t))
                dve.wait_ge(s_hid, freed(t))
                dve.tensor_copy(xt[s][:, :, :], flip[s][:, 0:C].rearrange("p (h c) -> p h c", h=CH)).then_inc(s_row, 1)

            def step(t, s, k, last):
                if not last:
                    turn(t + 1, 1 - s)
                dve.wait_ge(s_gate, done(t))
                dve.tensor_tensor(row(score, t), gp[s][:, 0:X].unsqueeze(1), bg[:, :].unsqueeze(1), ALU.add).then_inc(s_gated, 1)
            turn(0, 0)
            tiles(dve, step)
            dve.wait_ge(s_gated, done(T - 1))
            link = Chain(dve, s_lchain)
            wide = lambda a: a.unsqueeze(2).to_broadcast([P, T, X])
            link(dve.tensor_reduce(best[:, :], score[:, :, :], AX.X, ALU.max))
            dve.tensor_tensor(equal[:, :, :], score[:, :, :], wide(best[:, :]), ALU.subtract).then_inc(s_diff, 1)
            dve.wait_ge(s_exp, 1)
            link(dve.tensor_reduce(best[:, :], score[:, :, :], AX.X, ALU.add))
            link(dve.reciprocal(best[:, :], best[:, :]))
            link(dve.tensor_tensor(score[:, :, :], score[:, :, :], wide(best[:, :]), ALU.mult))
            first_best(dve, m, link, score, m.prob[:, :, 0], key[:, :], equal)
            sort_vector(dve, m, link, key[:, :], onehot, count, small6, m.psum[0], pos[:, :], m.fown[:, 0:FBLK1],
                        s_counts, s_totals, X, T, FBLK1)
            dve.tensor_copy(m.fpos[:, 0:T], pos[:, :]).then_inc(s_pos, 1)

        @block.tensor
        def _(pe):
            opened(pe, s_flipped, s_hid, s_gate)
            pe.wait_ge(s_w, 64)

            def flips(t, s):
                pe.wait_ge(s_copied, done(t))
                pe.wait_ge(s_row, freed(t))
                for h in range(CH):
                    ins = pe.transpose(flip[s][:, h * P:h * P + P], xs[s][:, h * P:h * P + P], m.ident[:, :])
                ins.then_inc(s_flipped, 1)

            def hidden(t, s):
                pe.wait_ge(s_row, done(t))
                pe.wait_ge(s_gelu, freed(t))
                hidden_turned(pe, hp[s], m.f1_w1, xt[s]).then_inc(s_hid, 1)

            def gates(t, s):
                pe.wait_ge(s_gelu, done(t))
                pe.wait_ge(s_gated, freed(t))
                for q in range(HC):
                    ins = pe.matmul(gp[s][:, 0:X], hs[s][:, q, :], wg[:, q, :], start=q == 0, stop=q == HC - 1)
                ins.then_inc(s_gate, 1)

            flips(0, 0)
            hidden(0, 0)
            flips(1, 1)

            def step(t, s, k, last):
                hidden(t + 1, 1 - s)
                if not last:
                    flips(t + 2, s)
                gates(t, s)
            tiles(pe, step, T - 1)
            gates(T - 1, (T - 1) % 2)
            sort_tensor(pe, m, small6, m.psum[0], s_counts, s_totals, X)

        @block.gpsimd
        def _(pool):
            pool.wait_ge(s_pos, 1)

            def step(t, s, k, last):
                pool.wait_ge(s_staged, done(t))
                landed(pool, s_sent[s], k)
                pool.tensor_copy(ps[s][:, :], m.fpos[:, bass.ds(t, 1)]).then_inc(s_pcopy, 1)
                pool.wait_ge(s_pcopy, t + 1)
                pool.sem_inc(s_issue, 1)
                pool.indirect_dma_start(out=d.xs1, out_offset=bass.IndirectOffsetOnAxis(ap=ps[s][:, 0:1], axis=0),
                                        in_=xs[s][:, :], in_offset=None).then_inc(s_sent[s], 16)
            tiles(pool, step, peel=True)
            for s in range(SLOTS):
                pool.wait_ge(s_sent[s], 16 * ((T - s + 1) // 2))



def phase_experts1(nc, m, d):
    s_w, s_flipped, s_row, s_hid, s_gelu, s_y, s_out = m.sems("ex1", "w flipped row hid gelu y out")
    s_load, s_store = m.sems("ex1", "load0 load1"), m.sems("ex1", "store0 store1")
    with ExitStack() as mem, nc.Block() as block:
        sb = lambda name, shape, dt=F32: mem.enter_context(nc.sbuf_tensor("ex1_" + name, shape, dt))
        wd = sb("wd", [P, X, HC, C])
        bd = sb("bd", [P, X, C])
        xin = [sb(f"xin{s}", [P, C]) for s in range(SLOTS)]
        xt = [sb(f"xt{s}", [P, CH, P]) for s in range(SLOTS)]
        hs = [sb(f"hs{s}", [P, HC, P]) for s in range(SLOTS)]
        ys = [sb(f"ys{s}", [P, C]) for s in range(SLOTS)]
        flip, yp, hp = m.psum[0:2], m.psum[2:4], [m.psum[4:6], m.psum[6:8]]
        loop = lambda eng, step: tiles(eng, step, FBLK1)

        @block.sync
        def _(sp):
            sp.dma_start(bd[:, :, :].rearrange("p e c -> p (e c)"),
                         d.f1_bd.rearrange("e c -> (e c)").rearrange("(a c) -> a c", a=1).to_broadcast([P, X * C])).then_inc(s_w, 16)
            for e in range(X):
                sp.dma_start(wd[:, e, :, :], d.f1_wd[e, :, :].rearrange("(q p) o -> p q o", p=P)).then_inc(s_w, 16)

            def step(j, s, k, last):
                sp.wait_ge(s_out, done(j))
                sp.dma_start(d.ys1[bass.ds(j * P, P), :], ys[s][:, :]).then_inc(s_store[s], 16)
            loop(sp, step)
            for s in range(SLOTS):
                sp.wait_ge(s_store[s], 16 * ((FBLK1 - s + 1) // 2))

        @block.gpsimd
        def _(pool):
            def step(j, s, k, last):
                pool.wait_ge(s_flipped, freed(j))
                pool.dma_start(xin[s][:, :], d.xs1[bass.ds(j * P, P), :]).then_inc(s_load[s], 16)
            loop(pool, step)

        @block.scalar
        def _(act):
            opened(act, s_gelu)

            def step(j, s, k, last):
                act.wait_ge(s_hid, done(j))
                act.wait_ge(s_y, freed(j))
                for q in range(HC):
                    ins = act.activation(hs[s][:, q, :], hp[s][q // 4][:, q % 4 * P:q % 4 * P + P], ACT.Gelu, bias=m.f1_b1[:, q:q + 1])
                ins.then_inc(s_gelu, 1)
            loop(act, step)

        @block.vector
        def _(dve):
            opened(dve, s_row, s_out)
            dve.wait_ge(s_w, 16 * (X + 1))

            def turn(j, s):
                dve.wait_ge(s_flipped, done(j))
                dve.wait_ge(s_hid, freed(j))
                dve.tensor_copy(xt[s][:, :, :], flip[s][:, 0:C].rearrange("p (h c) -> p h c", h=CH)).then_inc(s_row, 1)

            def result(j, s, k):
                e = dve.value_load(m.fown[0:1, bass.ds(j, 1)], min_val=0, max_val=X - 1)
                dve.wait_ge(s_y, done(j))
                landed(dve, s_store[s], k)
                dve.tensor_tensor(ys[s][:, :].unsqueeze(1), yp[s][:, 0:C].unsqueeze(1), bd[:, bass.ds(e, 1), :], ALU.add).then_inc(s_out, 1)
            turn(0, 0)
            turn(1, 1)

            def step(j, s, k, last):
                if not last:
                    turn(j + 2, s)
                result(j, s, k)
            tiles(dve, step, FBLK1 - 1, peel=True)
            result(FBLK1 - 1, (FBLK1 - 1) % 2, (FBLK1 - 1) // 2)

        @block.tensor
        def _(pe):
            opened(pe, s_flipped, s_hid, s_y)

            def flips(j, s, k):
                pe.wait_ge(s_load[s], 16 * k + 16)
                pe.wait_ge(s_row, freed(j))
                for h in range(CH):
                    ins = pe.transpose(flip[s][:, h * P:h * P + P], xin[s][:, h * P:h * P + P], m.ident[:, :])
                ins.then_inc(s_flipped, 1)

            def hidden(j, s):
                pe.wait_ge(s_row, done(j))
                pe.wait_ge(s_gelu, freed(j))
                hidden_turned(pe, hp[s], m.f1_w1, xt[s]).then_inc(s_hid, 1)

            def result(j, s):
                e = pe.value_load(m.fown[0:1, bass.ds(j, 1)], min_val=0, max_val=X - 1)
                pe.wait_ge(s_gelu, done(j))
                pe.wait_ge(s_out, freed(j))
                for q in range(HC):
                    ins = pe.matmul(yp[s][:, 0:C], hs[s][:, q, :], wd[:, bass.ds(e, 1), q, :], start=q == 0, stop=q == HC - 1)
                ins.then_inc(s_y, 1)

            flips(0, 0, 0)
            hidden(0, 0)
            flips(1, 1, 0)
            pe.wait_ge(s_w, 16 * (X + 1))

            def step(j, s, k, last):
                hidden(j + 1, 1 - s)
                if not last:
                    flips(j + 2, s, k + 1)
                result(j, s)
            tiles(pe, step, FBLK1 - 1)
            result(FBLK1 - 1, (FBLK1 - 1) % 2)



class Tensors:
    pass


def build(nc, d):
    dram = lambda name, rows, width: nc.dram_tensor(name, (rows, width), F32, kind="Internal").ap()
    d.support = dram("support", T * P, C)
    d.rec = dram("records", P * EBLK, 4)
    d.xs0, d.ys0 = dram("tokens0", FBLK0 * P, C), dram("results0", FBLK0 * P, C)
    d.xs1, d.ys1 = dram("tokens1", FBLK1 * P, C), dram("results1", FBLK1 * P, C)
    d.graph = dram("graph", T * P, C)
    with ExitStack() as whole:
        m = Machine(nc, whole)
        m.x = m.sb("x", [P, T, C])
        m.ident = m.sb("ident", [P, P])
        m.earlier = m.sb("earlier", [P, P])
        m.ones = m.sb("ones", [P, P])
        m.zeros = m.sb("zeros", [P, C])
        m.iota = m.sb("iota", [P, EBLK])
        m.lastmask = m.sb("lastmask", [P, 1])
        m.small_int = m.sb("small_int", [P, 32], I32)
        m.fpos = m.sb("fpos", [P, 2 * T], I32)
        m.fown = m.sb("fown", [P, FBLK0], I32)
        m.prob = m.sb("prob", [P, T, 2])
        with m.scope():
            m.rec = m.sb("rec", [P, ECOLS, 4])
            m.epos = m.sb("epos", [P, ECOLS], I32)
            m.eowner = m.sb("eowner", [P, EBLK], I32)
            m.buf_rec = [m.sb(f"buf_rec{h}", [P, EBUF * 4]) for h in range(2)]
            m.buf_pos = [m.sb(f"buf_pos{h}", [P, EBUF], I32) for h in range(2)]
            m.mix = m.sb("mix", [P, T, C])
            m.s_copied, m.s_issue = m.sems("edges", "copied issue")
            m.s_sent = m.sems("edges", "sent0 sent1")
            with m.scope():
                m.xn = m.sb("xn", [P, T, C])
                phase_start(nc, m, d)
                m.xnT = m.sb("xnT", [P, CH, T * P])
                m.bd = m.sb("bd", [P, CH, KVW])
                phase_support_kv(nc, m, d, (0, 144))
                phase_attend(nc, m, d, (144, 256))
            phase_mlp(nc, m, d, (256, ECOLS))
            phase_aggregate(nc, m, d)
        with m.scope():
            w1 = m.sb("ffn0_w1", [P, X, CH, HID])
            m.s_w1 = m.sem("ffn0_w1")
            phase_route0(nc, m, d, w1)
            phase_experts0(nc, m, d, w1)
        phase_combine(nc, m, "cmb0", d.ys0, 2)
        m.recycle()
        with m.scope():
            m.xnT = m.sb("xnT1", [P, CH, T * P])
            m.mixer = m.sb("mixer", [P, CH, C])
            phase_project1(nc, m, d)
            phase_graph1(nc, m, d)
        m.f1_w1 = m.sb("f1_w1", [P, CH, HID])
        m.f1_b1 = m.sb("f1_b1", [P, HC])
        phase_route1(nc, m, d)
        phase_experts1(nc, m, d)
        phase_combine(nc, m, "cmb1", d.ys1, 1)
        s_out = m.sem("out")
        with nc.Block() as block:
            @block.sync
            def _(sp):
                full = (T - 1) * P
                sp.dma_start(d.out[0:full, :].rearrange("(t p) c -> p t c", p=P), m.x[:, 0:T - 1, :]).then_inc(s_out, 16)
                sp.dma_start(d.out[full:N, :], m.x[0:LAST, T - 1, :]).then_inc(s_out, 16)
                sp.wait_ge(s_out, 32)


def kernel(x, src, dst, edge_weight, L0_gnn_A, L0_gnn_B, L0_gnn_bn_weight, L0_gnn_bn_bias, L0_mix_Wqkv, L0_mix_ln1_g,
           L0_mix_ln1_b, L0_mix_W1, L0_mix_b1, L0_mix_W2, L0_mix_b2, L0_mix_ln2_g, L0_mix_ln2_b, L0_ffn_Wg, L0_ffn_bg,
           L0_ffn_W1, L0_ffn_b1, L0_ffn_W2, L0_ffn_b2, L1_gnn_weight, L1_gnn_attn_l, L1_gnn_attn_r, L1_mix_wq,
           L1_mix_wk, L1_mix_wv, L1_mix_wo, L1_mix_bo, L1_mix_ln_k_g, L1_mix_ln_k_b, L1_mix_ln_v_g, L1_mix_ln_v_b,
           L1_ffn_W1, L1_ffn_b1, L1_ffn_Wg, L1_ffn_bg, L1_ffn_Wd, L1_ffn_bd):
    import numpy as np
    from concourse import bacc
    from concourse.bass_utils import run_bass_kernel_spmd

    laid = {
        "ends": np.transpose(np.reshape(np.stack([src[:N], dst[:N]], -1)[:(T - 1) * P], (T - 1, P, 2)), (1, 0, 2)),
        "ends_last": np.stack([src[(T - 1) * P:N], dst[(T - 1) * P:N]], -1),
        "x": x, "src": src, "dst": dst, "edge_weight": edge_weight,
        "A": L0_gnn_A, "B": L0_gnn_B, "bn_w": L0_gnn_bn_weight, "bn_b": L0_gnn_bn_bias,
        "wqkv": np.transpose(L0_mix_Wqkv), "ln1_g": L0_mix_ln1_g, "ln1_b": L0_mix_ln1_b,
        "mw1": np.transpose(L0_mix_W1), "mb1": np.transpose(np.reshape(L0_mix_b1, (CH, P))), "mw2": np.transpose(L0_mix_W2), "mb2": L0_mix_b2,
        "ln2_g": L0_mix_ln2_g, "ln2_b": L0_mix_ln2_b,
        "f0_wg": np.transpose(L0_ffn_Wg), "f0_bg": L0_ffn_bg,
        "f0_w1": np.transpose(L0_ffn_W1, (0, 2, 1)), "f0_b1": np.transpose(np.reshape(L0_ffn_b1, (X, HC, P)), (2, 0, 1)),
        "f0_w2": np.transpose(L0_ffn_W2, (0, 2, 1)), "f0_b2": L0_ffn_b2,
        "g_w": L1_gnn_weight, "g_al": L1_gnn_attn_l, "g_ar": L1_gnn_attn_r,
        "wq": L1_mix_wq, "wk": np.transpose(L1_mix_wk), "wv": np.transpose(L1_mix_wv), "wo": np.transpose(L1_mix_wo),
        "bo": L1_mix_bo, "k_g": L1_mix_ln_k_g, "k_b": L1_mix_ln_k_b, "v_g": L1_mix_ln_v_g, "v_b": L1_mix_ln_v_b,
        "f1_w1": L1_ffn_W1, "f1_b1": np.transpose(np.reshape(L1_ffn_b1, (HC, P))), "f1_wg": L1_ffn_Wg, "f1_bg": L1_ffn_bg, "f1_wd": L1_ffn_Wd,
        "f1_bd": L1_ffn_bd,
    }
    nc = bacc.Bacc("TRN2", target_bir_lowering=False, num_devices=1)
    d = Tensors()
    arrays = {}
    for name, a in laid.items():
        arrays["in_" + name] = a = np.ascontiguousarray(a)
        ap = nc.dram_tensor("in_" + name, a.shape, mybir.dt.from_np(a.dtype), kind="ExternalInput").ap()
        d.__dict__[name] = ap
    d.out = nc.dram_tensor("out", (N, C), F32, kind="ExternalOutput").ap()
    build(nc, d)
    r = run_bass_kernel_spmd(nc, [arrays], core_ids=[0])
    return r.results[0]["out"]
```

```python
import concourse.bass as bass
from concourse import mybir
from contextlib import ExitStack, contextmanager

F32 = mybir.dt.float32
I32 = mybir.dt.int32
U32 = mybir.dt.uint32
ALU = mybir.AluOpType
ACT = mybir.ActivationFunctionType
AX = mybir.AxisListType

P = 128
N = 3125
C = 256
CH = C // P
T = -(-N // P)
LAST = N - (T - 1) * P
E = 50000
EROWS = 125
ECOLS = E // EROWS
EBUF = 8
GB = 16
X = 8
HID = 1024
HC = HID // P
H0, D0 = 8, 32
H1, D1 = 4, 64
KVW = P + 4
GROW = C + 2 * H1
SLOTS = 2


def blocks_for(rows, buckets):
    return (rows + buckets * (P - 1)) // P


EBLK = -(-blocks_for(P * ECOLS, T) // GB) * GB
FBLK0 = blocks_for(2 * T * P, X)
FBLK1 = blocks_for(T * P, X)
FAR = 1 << 20


def done(t):
    return t + 1 + SLOTS


def freed(t):
    return t + 1


def opened(eng, *sems):
    for s in sems:
        eng.sem_inc(s, SLOTS)


def tiles(eng, step, n=T, peel=False, slots=SLOTS):
    loops = (n - 1) // slots
    if peel:
        for s in range(slots):
            step(s, s, 0, False)
    with eng.Fori(int(peel), loops) as k:
        for s in range(slots):
            step(k * slots + s, s, k, False)
    for t in range(loops * slots, n):
        step(t, t % slots, t // slots, t == n - 1)


class Chain:

    def __init__(self, eng, sem, start=0):
        self.eng, self.sem, self.value = eng, sem, start

    def __call__(self, ins):
        self.value = self.value + 1
        ins.then_inc(self.sem, 1)
        self.eng.wait_ge(self.sem, self.value)


def landed(eng, sem, k, dmas=1):
    if not isinstance(k, int) or k > 0:
        eng.wait_ge(sem, k * (16 * dmas))


def row(ap, t):
    return ap[:, bass.ds(t, 1)] if not isinstance(t, int) else ap[:, t:t + 1]


class Machine:

    def __init__(self, nc, ctx):
        self.nc, self.ctx, self.used = nc, ctx, []
        self.psum = [ctx.enter_context(nc.psum_tensor(f"bank{i}", [P, 512], F32)) for i in range(8)]

    def sb(self, name, shape, dt=F32):
        return self.ctx.enter_context(self.nc.sbuf_tensor(name, shape, dt))

    def sem(self, name):
        self.used.append(self.nc.alloc_semaphore(name))
        return self.used[-1]

    @contextmanager
    def scope(self):
        outer = self.ctx
        with ExitStack() as self.ctx:
            yield
        self.ctx = outer

    def recycle(self):
        self.nc.clear_and_free_semaphores(self.used)
        self.nc.all_engine_barrier()
        self.used = []

    def sems(self, phase, names):
        return [self.sem(f"{phase}_{n}") for n in names.split()]



def row_stats(dve, x, stats, t, s_stats):
    return dve.bn_stats(row(stats, t), row(x, t)).then_inc(s_stats, 1)


def stats_vector(dve, link, m, stats, s_var, s_std):
    even, odd = stats[:, :, 0:3], stats[:, :, 3:6]
    dif, dev, var = (m.scratch[:, i, :] for i in range(3))
    dve.tensor_tensor(dif, even[:, :, 1], odd[:, :, 1], ALU.subtract)
    dve.tensor_tensor(dev, even[:, :, 2], odd[:, :, 2], ALU.add)
    link(dve.tensor_tensor(m.mean[:, :], even[:, :, 1], odd[:, :, 1], ALU.add))
    dve.tensor_scalar(m.mean[:, :], m.mean[:, :], 0.5, None, ALU.mult)
    dve.scalar_tensor_tensor(out=var, in0=dif, scalar=0.25, in1=dif, op0=ALU.mult, op1=ALU.mult)
    link(dve.tensor_scalar(dev, dev, 1.0 / C, 1e-5, ALU.mult, ALU.add))
    dve.tensor_tensor(var, var, dev, ALU.add).then_inc(s_var, 1)
    dve.wait_ge(s_std, 1)
    link(dve.reciprocal(m.rstd[:, :], m.scratch[:, 3, :]))


def stats_scalar(act, m, s_var, s_std):
    act.wait_ge(s_var, 1)
    act.activation(m.scratch[:, 3, :], m.scratch[:, 2, :], ACT.Sqrt).then_inc(s_std, 1)


def normalise(dve, m, out, t, x=None):
    return dve.tensor_scalar(out, row(m.x if x is None else x, t), m.mean[:, bass.ds(t, 1)], m.rstd[:, bass.ds(t, 1)],
                             ALU.subtract, ALU.mult)



def sort_vector(dve, m, link, key, onehot, count, small, psum, pos, s_counts, s_totals, buckets, cols):
    oh = onehot[:, 0:buckets * cols].rearrange("p (b c) -> p b c", b=buckets)
    cn = count[:, 0:buckets * cols].rearrange("p (b c) -> p b c", b=buckets)
    link(dve.tensor_tensor(oh, key.unsqueeze(1).to_broadcast([P, buckets, cols]),
                           m.iota[:, 0:buckets].unsqueeze(2).to_broadcast([P, buckets, cols]), ALU.is_equal))
    link(dve.tensor_tensor_scan(count[:, 0:buckets * cols], onehot[:, 0:buckets * cols],
                                onehot[:, 0:buckets * cols], 0.0, ALU.add, ALU.max))
    own, before, base, full, blk, end = (small[:, i, 0:buckets] for i in range(6))
    link(dve.memset(before, 0.0))
    link(dve.tensor_copy(small[:, 1, 1:buckets], cn[:, 0:buckets - 1, cols - 1]))
    dve.tensor_tensor(own, cn[:, :, cols - 1], before, ALU.subtract).then_inc(s_counts, 1)
    dve.wait_ge(s_totals, 1)
    link(dve.tensor_scalar(full, psum[:, 64:64 + buckets], float(P - 1), None, ALU.add))
    whole = m.small_int[:, 0:buckets]
    link(dve.tensor_copy(whole, full))
    link(dve.tensor_scalar(whole, whole, 7, None, ALU.arith_shift_right))
    link(dve.tensor_copy(blk, whole))
    link(dve.tensor_tensor_scan(end, blk, blk, 0.0, ALU.add, ALU.max))
    link(dve.tensor_tensor(base, end, blk, ALU.subtract))
    link(dve.tensor_scalar(base, base, float(P), -1.0, ALU.mult, ALU.add))
    link(dve.tensor_tensor(base, base, before, ALU.subtract))
    link(dve.tensor_tensor(base, base, psum[:, 0:buckets], ALU.add))
    for b in range(buckets):
        ins = dve.scalar_tensor_tensor(out=cn[:, b, :], in0=cn[:, b, :], scalar=base[:, b:b + 1],
                                       in1=oh[:, b, :], op0=ALU.add, op1=ALU.mult)
    link(ins)
    link(dve.tensor_reduce(pos, count[:, 0:buckets * cols].rearrange("p (b c) -> p c b", b=buckets),
                           AX.X, ALU.add))


def sort_owner(dve, m, link, end, tmp, owner, buckets, nblk):
    link(dve.memset(tmp, 0.0))
    for b in range(buckets - 1):
        link(dve.scalar_tensor_tensor(out=tmp, in0=m.iota[:, 0:nblk], scalar=end[:, b:b + 1], in1=tmp,
                                      op0=ALU.is_ge, op1=ALU.add))
    link(dve.tensor_copy(owner, tmp))


PICK = 5


def invert_vector(dve, m, link, pos, value, work, whole, hi_hot, lo_hot, psum, cols, nblk, s_hot, s_placed):
    lo, hi, ids, none = (work[:, i, :] for i in range(4))
    lo, hi, ids, none = lo[:, 0:cols], hi[:, 0:cols], ids[:, 0:nblk], none[:, 0:nblk]
    link(dve.tensor_copy(whole[:, 0, :], pos))
    dve.tensor_scalar(whole[:, 1, :], whole[:, 0, :], P - 1, None, ALU.bitwise_and)
    link(dve.tensor_scalar(whole[:, 2, :], whole[:, 0, :], 7, None, ALU.arith_shift_right))
    dve.tensor_copy(lo, whole[:, 1, :])
    link(dve.tensor_copy(hi, whole[:, 2, :]))
    link(dve.tensor_tensor(hi_hot, m.iota[:, 0:nblk].unsqueeze(1).to_broadcast([P, cols, nblk]),
                           hi.unsqueeze(2).to_broadcast([P, cols, nblk]), ALU.is_equal))
    link(dve.tensor_tensor(hi_hot, hi_hot, value.unsqueeze(2).to_broadcast([P, cols, nblk]), ALU.mult))
    opened(dve, s_hot)

    def step(g, s, k, last):
        dve.wait_ge(s_placed, freed(g))
        dve.tensor_tensor(lo_hot[s][:, :, :], m.iota[:, 0:P].unsqueeze(1).to_broadcast([P, PICK, P]),
                          lo[:, bass.ds(g * PICK, PICK)].unsqueeze(2).to_broadcast([P, PICK, P]), ALU.is_equal).then_inc(s_hot, 1)
    tiles(dve, step, cols // PICK)
    dve.wait_ge(s_placed, done(cols // PICK - 1))
    link(dve.tensor_scalar(ids, psum[:, 0:nblk], -1.0, None, ALU.add))
    link(dve.tensor_scalar(none, ids, 0.0, float(FAR), ALU.is_lt, ALU.mult))
    link(dve.tensor_tensor(m.dest[:, 0:nblk], ids, none, ALU.add))
    link(dve.tensor_scalar(none, ids, float(T * P), -float(T * P), ALU.is_ge, ALU.mult))
    link(dve.tensor_tensor(ids, ids, none, ALU.add))
    link(dve.tensor_scalar(m.token[:, 0:nblk], ids, 0.0, None, ALU.max))


def invert_tensor(pe, m, hi_hot, lo_hot, psum, cols, nblk, s_hot, s_placed):
    opened(pe, s_placed)
    pe.matmul(psum[:, 0:nblk], m.zeros[:, 0:P], m.zeros[:, 0:nblk], start=True, stop=False)

    def step(g, s, k, last):
        pe.wait_ge(s_hot, done(g))
        for u in range(PICK):
            ins = pe.matmul(psum[:, 0:nblk], lo_hot[s][:, u, :], hi_hot[:, bass.ds(g * PICK + u, 1), :],
                            start=False, stop=last and u == PICK - 1)
        ins.then_inc(s_placed, 1)
    tiles(pe, step, cols // PICK)


def sort_tensor(pe, m, small, psum, s_counts, s_totals, buckets):
    pe.wait_ge(s_counts, 1)
    pe.matmul(psum[:, 0:buckets], m.earlier[:, :], small[:, 0, 0:buckets], start=True, stop=True)
    pe.matmul(psum[:, 64:64 + buckets], m.ones[:, :], small[:, 0, 0:buckets], start=True, stop=True)\
      .then_inc(s_totals, 1)



def phase_start(nc, m, d):
    s_load, s_const, s_pad = m.sems("start", "load const pad")
    s_edge, s_eload, s_edges, s_counts, s_totals, s_rec, s_wchain = m.sems("start", "edge eload edges counts totals rec wchain")
    with ExitStack() as mem, nc.Block() as block:
        sb = lambda name, shape, dt=F32: mem.enter_context(nc.sbuf_tensor(name, shape, dt))
        onehot = sb("st_onehot", [P, ECOLS * T])
        count = sb("st_count", [P, ECOLS * T])
        small = sb("st_small", [P, 6, 32])
        src_i = sb("st_src", [P, ECOLS], I32)
        dst_i = sb("st_dst", [P, ECOLS], I32)
        w = sb("st_w", [P, ECOLS])
        key = sb("st_key", [P, ECOLS])
        pos = sb("st_pos", [P, ECOLS])
        pos_i = sb("st_pos_i", [P, ECOLS], I32)
        lo_i = sb("st_lo_i", [P, ECOLS], I32)
        zrec = sb("st_zrec", [P, EBLK * 4])

        @block.gpsimd
        def _(pool):
            c = Chain(pool, s_const)
            c(pool.memset(m.ones[:, :], 1.0))
            c(pool.memset(m.zeros[:, :], 0.0))
            c(pool.iota(m.iota[:, :], [[1, EBLK]], base=0, channel_multiplier=0, allow_small_or_imprecise_dtypes=True))
            c(pool.affine_select(out=m.ident[:, :], in_=m.zeros[:, 0:P], compare_op=ALU.not_equal, fill=1.0,
                                 base=0, pattern=[[-1, P]], channel_multiplier=1))
            c(pool.affine_select(out=m.earlier[:, :], in_=m.zeros[:, 0:P], compare_op=ALU.is_ge, fill=1.0,
                                 base=0, pattern=[[-1, P]], channel_multiplier=1))
            c(pool.affine_select(out=m.lastmask[:, :], in_=m.ones[:, 0:1], compare_op=ALU.is_ge, fill=0.0,
                                 base=LAST - 1, pattern=[[0, 1]], channel_multiplier=-1))
            c(pool.iota(m.row2[:, :, :], [[P, T], [T * P, 2]], base=1, channel_multiplier=1, allow_small_or_imprecise_dtypes=True))
            c(pool.iota(m.row1[:, :], [[P, T]], base=1, channel_multiplier=1, allow_small_or_imprecise_dtypes=True))
            pool.memset(zrec[:, :], 0.0).then_inc(s_rec, 1)

        @block.sync
        def _(sp):
            sp.wait_ge(s_edge, 4)
            sp.dma_start(src_i[0:EROWS, :], d.src.rearrange("(p c) -> p c", p=EROWS)).then_inc(s_edges, 16)
            sp.dma_start(dst_i[0:EROWS, :], d.dst.rearrange("(p c) -> p c", p=EROWS)).then_inc(s_edges, 16)
            sp.dma_start(w[0:EROWS, :], d.edge_weight.rearrange("(p c) -> p c", p=EROWS)).then_inc(s_edges, 16)
            sp.wait_ge(s_rec, 1)
            sp.dma_start(d.rec.rearrange("(p j) r -> p (j r)", p=P), zrec[:, :]).then_inc(s_eload, 16)
            sp.wait_ge(s_eload, 16)
            sp.wait_ge(s_load, 32)

        @block.scalar
        def _(act):
            act.wait_ge(s_pad, 1)
            full = (T - 1) * P
            act.dma_start(m.x[:, 0:T - 1, :], d.x[0:full, :].rearrange("(t p) c -> p t c", p=P)).then_inc(s_load, 16)
            act.dma_start(m.x[0:LAST, T - 1, :], d.x[full:N, :]).then_inc(s_load, 16)

        @block.vector
        def _(dve):
            dve.memset(src_i[:, :], 0).then_inc(s_edge, 1)
            dve.memset(dst_i[:, :], 0).then_inc(s_edge, 1)
            dve.memset(w[:, :], 0.0).then_inc(s_edge, 1)
            dve.memset(m.rec[:, :, :], 0.0).then_inc(s_edge, 1)
            dve.memset(m.x[:, T - 1, :], 0.0).then_inc(s_pad, 1)
            dve.wait_ge(s_const, 8)
            dve.wait_ge(s_edges, 48)
            link = Chain(dve, s_wchain)
            link(dve.tensor_scalar(lo_i[:, :], src_i[:, :], 7, None, ALU.arith_shift_right))
            link(dve.tensor_copy(key[:, :], lo_i[:, :]))
            link(dve.tensor_scalar(lo_i[:, :], src_i[:, :], P - 1, None, ALU.bitwise_and))
            dve.tensor_copy(m.rec[:, :, 0], lo_i[:, :])
            dve.tensor_copy(m.rec[:, :, 1], w[:, :])
            link(dve.tensor_copy(m.rec.bitcast(I32)[:, :, 2], dst_i[:, :]))
            sort_vector(dve, m, link, key[:, :], onehot, count, small, m.psum[0], pos[:, :], s_counts, s_totals, T, ECOLS)
            link(dve.tensor_copy(m.eend[:, :], small[:, 5, 0:T]))
            link(dve.tensor_copy(pos_i[:, :], pos[:, :]))
            link(dve.tensor_scalar(lo_i[:, :], pos_i[:, :], P - 1, None, ALU.bitwise_and))
            link(dve.tensor_scalar(pos_i[:, :], pos_i[:, :], 7, None, ALU.arith_shift_right))
            link(dve.tensor_scalar(pos[:, :], lo_i[:, :], float(EBLK), None, ALU.mult))
            link(dve.tensor_tensor(m.epos[:, :], pos[:, :], pos_i[:, :], ALU.add))

        @block.tensor
        def _(pe):
            pe.wait_ge(s_const, 8)
            sort_tensor(pe, m, small, m.psum[0], s_counts, s_totals, T)


def scatter_edges(pool, m, d, first, last):
    s_copied, s_sent, s_issue = m.s_copied, m.s_sent, m.s_issue
    step = 2 * EBUF

    def both(k):
        for h in range(2):
            col = k * step + h * EBUF
            landed(pool, s_sent[h], k, EBUF)
            pool.tensor_copy(m.buf_rec[h][:, :], m.rec[:, bass.ds(col, EBUF), :].rearrange("p c r -> p (c r)"))
            pool.tensor_copy(m.buf_pos[h][:, :], m.epos[:, bass.ds(col, EBUF)]).then_inc(s_copied, 1)
            pool.wait_ge(s_copied, k * 2 + h + 1)
            pool.sem_inc(s_issue, 1)
            for u in range(EBUF):
                pool.indirect_dma_start(out=d.rec, out_offset=bass.IndirectOffsetOnAxis(ap=m.buf_pos[h][:, u:u + 1], axis=0),
                                        in_=m.buf_rec[h][:, 4 * u:4 * u + 4], in_offset=None).then_inc(s_sent[h], 16)

    if first == 0:
        both(0)
    with pool.Fori(max(first // step, 1), last // step) as k:
        both(k)
    for h in range(2):
        pool.wait_ge(s_sent[h], last // step * 16 * EBUF)



QUATERNION = [[(0, 1), (1, 1), (2, 1), (3, 1)],
              [(1, -1), (0, 1), (3, 1), (2, -1)],
              [(2, -1), (3, -1), (0, 1), (1, 1)],
              [(3, -1), (2, 1), (1, -1), (0, 1)]]


def phase_support_kv(nc, m, d, share):
    (s_w, s_built, s_chain, s_copied, s_flipped, s_row, s_rowall, s_proj, s_kmin, s_kexp, s_k, s_v, s_kv, s_sup,
     s_kept, s_stats, s_var, s_std) = m.sems(
        "skv", "w built chain copied flipped row rowall proj kmin kexp k v kv sup kept stats var std")
    s_store = m.sems("skv", "store0 store1")
    with ExitStack() as mem, nc.Block() as block:
        sb = lambda name, shape, dt=F32: mem.enter_context(nc.sbuf_tensor("skv_" + name, shape, dt))
        w = sb("w", [P, CH, 3 * C])
        ab = sb("ab", [P, 2, P])
        g = w[:, :, 2 * C:3 * C]
        stats = sb("stats", [P, T, 6])
        xs = [sb(f"xs{s}", [P, C]) for s in range(SLOTS)]
        xt = [sb(f"xt{s}", [P, CH, P]) for s in range(SLOTS)]
        sup = [sb(f"sup{s}", [P, C]) for s in range(SLOTS)]
        kmin = [sb(f"kmin{s}", [P, C]) for s in range(SLOTS)]
        kexp = [sb(f"kexp{s}", [P, C]) for s in range(SLOTS)]
        ks = [sb(f"ks{s}", [P, C]) for s in range(SLOTS)]
        vs = [sb(f"vs{s}", [P, CH, KVW]) for s in range(SLOTS)]
        flip, kp, vsp, kv = m.psum[0:2], m.psum[2:4], m.psum[4:6], m.psum[6:8]

        @block.sync
        def _(sp):
            sp.dma_start(w[:, :, 0:2 * C], d.wqkv[:, C:3 * C].rearrange("(h p) o -> p h o", p=P)).then_inc(s_w, 16)
            for b in range(4):
                sp.dma_start(ab[32 * b:32 * b + 32, 0, :], d.A).then_inc(s_w, 16)
                sp.dma_start(ab[32 * b:32 * b + 32, 1, :], d.B).then_inc(s_w, 16)

            def step(t, s, k, last):
                sp.wait_ge(s_sup, done(t))
                sp.dma_start(d.support[bass.ds(t * P, P), :], sup[s][:, :]).then_inc(s_store[s], 16)
            tiles(sp, step)
            for s in range(SLOTS):
                sp.wait_ge(s_store[s], 16 * ((T - s + 1) // 2))

        @block.gpsimd
        def _(pool):
            scatter_edges(pool, m, d, *share)

        @block.scalar
        def _(act):
            opened(act, s_kept, s_rowall, s_v, s_kexp, s_sup)
            stats_scalar(act, m, s_var, s_std)

            def keep(t, s):
                act.wait_ge(s_copied, done(t))
                act.activation(row(m.xn, t), xs[s][:, :].unsqueeze(1), ACT.Copy).then_inc(s_kept, 1)

            def step(t, s, k, last):
                if not last:
                    keep(t + 1, 1 - s)
                act.wait_ge(s_row, done(t))
                act.activation(m.xnT[:, :, bass.ds(t * P, P)], xt[s][:, :, :], ACT.Copy).then_inc(s_rowall, 1)
                act.wait_ge(s_kmin, done(t))
                act.activation(kexp[s][:, :], kmin[s][:, :], ACT.Exp).then_inc(s_kexp, 1)
                act.wait_ge(s_kv, freed(t))
                act.activation(vs[s][:, :, 0:P], vsp[s][:, 0:C].rearrange("p (h c) -> p h c", h=CH),
                               ACT.Copy).then_inc(s_v, 1)
                landed(act, s_store[s], k)
                act.activation(sup[s][:, :], vsp[s][:, C:2 * C], ACT.Copy).then_inc(s_sup, 1)

            keep(0, 0)
            tiles(act, step, peel=True)

        @block.vector
        def _(dve):
            link = Chain(dve, s_chain)
            opened(dve, s_copied, s_row, s_kmin, s_k)
            with dve.Fori(0, T) as t:
                row_stats(dve, m.x, stats, t, s_stats)
            dve.wait_ge(s_stats, T)
            stats_vector(dve, link, m, stats[:, :, :], s_var, s_std)

            def norm(t, s):
                dve.wait_ge(s_flipped, freed(t))
                dve.wait_ge(s_kept, freed(t))
                normalise(dve, m, xs[s][:, :].unsqueeze(1), t).then_inc(s_copied, 1)

            norm(0, 0)
            for s in range(SLOTS):
                link(dve.memset(vs[s][:, :, P:KVW], 1.0))
            link(dve.memset(g, 0.0))
            link(dve.memset(m.bd[:, :, :], 0.0))
            dve.wait_ge(s_w, 16 * 9)
            for b in range(4):
                for c, (part, sign) in enumerate(QUATERNION[b]):
                    q = slice(32 * b, 32 * b + 32)
                    out = slice(32 * c, 32 * c + 32)
                    src = slice(32 * part, 32 * part + 32)
                    dve.tensor_scalar(g[q, 0, out], ab[q, 0, src], float(sign), None, ALU.mult)
                    dve.tensor_scalar(g[q, 1, P + 32 * c:P + 32 * c + 32], ab[q, 0, src], float(sign), None, ALU.mult)
                    ins = dve.tensor_scalar(g[q, 0, P + 32 * c:P + 32 * c + 32], ab[q, 1, src], float(sign), None, ALU.mult)
            ins.then_inc(s_built, 1)

            def turn(t, s):
                dve.wait_ge(s_flipped, done(t))
                dve.wait_ge(s_proj, freed(t))
                dve.wait_ge(s_rowall, freed(t))
                dve.tensor_copy(xt[s][:, :, :], flip[s][:, 0:C].rearrange("p (h c) -> p h c", h=CH)).then_inc(s_row, 1)

            def step(t, s, k, last):
                if not last:
                    norm(t + 1, 1 - s)
                dve.wait_ge(s_proj, done(t))
                dve.wait_ge(s_kexp, freed(t))
                dve.tensor_scalar(kmin[s][:, :], kp[s][:, 0:C], 0.0, None, ALU.min).then_inc(s_kmin, 1)
                if not last:
                    turn(t + 1, 1 - s)
                dve.wait_ge(s_kexp, done(t))
                dve.wait_ge(s_kv, freed(t))
                if last:
                    link(dve.tensor_copy(vs[s][:, :, P:KVW], m.lastmask[:, 0:1].unsqueeze(1).to_broadcast([P, CH, 4])))
                dve.scalar_tensor_tensor(out=ks[s][:, :], in0=kp[s][:, 0:C], scalar=0.0, in1=kexp[s][:, :],
                                         op0=ALU.max, op1=ALU.add).then_inc(s_k, 1)

            turn(0, 0)
            tiles(dve, step)
            dve.wait_ge(s_kv, done(T - 1))
            for h in range(CH):
                for i in range(4):
                    q = slice(D0 * i, D0 * i + D0)
                    dve.tensor_copy(m.bd[q, h, q], kv[h][q, q])
                    ins = dve.tensor_copy(m.bd[q, h, P + i:P + i + 1], kv[h][q, P:P + 1])
            link(ins)

        @block.tensor
        def _(pe):
            opened(pe, s_flipped, s_proj, s_kv)
            for h in range(CH):
                pe.matmul(kv[h][:, 0:KVW], m.zeros[:, 0:P], m.zeros[:, 0:KVW], start=True, stop=False)

            def flips(t, s):
                pe.wait_ge(s_copied, done(t))
                pe.wait_ge(s_row, freed(t))
                for h in range(CH):
                    ins = pe.transpose(flip[s][:, h * P:h * P + P], xs[s][:, h * P:h * P + P], m.ident[:, :])
                ins.then_inc(s_flipped, 1)

            def step(t, s, k, last):
                pe.wait_ge(s_row, done(t))
                pe.wait_ge(s_k, freed(t))
                pe.wait_ge(s_v, freed(t))
                pe.wait_ge(s_sup, freed(t))
                for h in range(CH):
                    pe.matmul(kp[s][:, 0:C], xt[s][:, h, :], w[:, h, 0:C], start=h == 0, stop=h == CH - 1)
                for h in range(CH):
                    ins = pe.matmul(vsp[s][:, :], xt[s][:, h, :], w[:, h, C:3 * C], start=h == 0, stop=h == CH - 1)
                ins.then_inc(s_proj, 1)
                if not last:
                    flips(t + 1, 1 - s)
                pe.wait_ge(s_k, done(t))
                pe.wait_ge(s_v, done(t))
                for h in range(CH):
                    ins = pe.matmul(kv[h][:, 0:KVW], ks[s][:, h * P:h * P + P], vs[s][:, h, :],
                                    start=False, stop=last)
                ins.then_inc(s_kv, 1)

            flips(0, 0)
            pe.wait_ge(s_w, 16 * 9)
            pe.wait_ge(s_built, 1)
            tiles(pe, step)



def phase_attend(nc, m, d, share):
    s_w, s_q, s_qmin, s_qexp, s_qs, s_att, s_out, s_chain, s_owner = m.sems("att", "w q qmin qexp qs att out chain owner")
    with ExitStack() as mem, nc.Block() as block:
        sb = lambda name, shape, dt=F32: mem.enter_context(nc.sbuf_tensor("att_" + name, shape, dt))
        wq = sb("wq", [P, CH, C])
        owner = sb("owner", [P, EBLK])
        qmin = [sb(f"qmin{s}", [P, C]) for s in range(SLOTS)]
        qexp = [sb(f"qexp{s}", [P, C]) for s in range(SLOTS)]
        qs = [sb(f"qs{s}", [P, CH, P]) for s in range(SLOTS)]
        z = [sb(f"z{s}", [P, CH, 4]) for s in range(SLOTS)]
        part = [sb(f"part{s}", [P, C]) for s in range(SLOTS)]
        qp, ap = m.psum[0:2], m.psum[2:4]

        @block.sync
        def _(sp):
            sp.dma_start(wq[:, :, :], d.wqkv[:, 0:C].rearrange("(h p) o -> p h o", p=P)).then_inc(s_w, 16)
            for e in range(X):
                sp.dma_start(m.w1[:, e, :, :], d.f0_w1[e, :, :].rearrange("(h p) o -> p h o", p=P)).then_inc(m.s_w1, 16)

        @block.gpsimd
        def _(pool):
            scatter_edges(pool, m, d, *share)

        @block.scalar
        def _(act):
            opened(act, s_qexp)

            def step(t, s, k, last):
                act.wait_ge(s_qmin, done(t))
                act.wait_ge(s_qs, freed(t))
                act.activation(qexp[s][:, :], qmin[s][:, :], ACT.Exp).then_inc(s_qexp, 1)
            tiles(act, step)

        @block.vector
        def _(dve):
            opened(dve, s_qmin, s_qs, s_out)
            sort_owner(dve, m, Chain(dve, s_owner), m.eend[:, :], owner[:, :], m.eowner[:, :], T, EBLK)

            def low(t, s):
                dve.wait_ge(s_q, done(t))
                dve.wait_ge(s_qexp, freed(t))
                dve.tensor_scalar(qmin[s][:, :], qp[s][:, 0:C], 0.0, None, ALU.min).then_inc(s_qmin, 1)

            def step(t, s, k, last):
                dve.wait_ge(s_qexp, done(t))
                dve.wait_ge(s_att, freed(t))
                dve.scalar_tensor_tensor(out=qs[s][:, :, :].rearrange("p h c -> p (h c)"), in0=qp[s][:, 0:C],
                                         scalar=0.0, in1=qexp[s][:, :], op0=ALU.max, op1=ALU.add).then_inc(s_qs, 1)
                if not last:
                    low(t + 1, 1 - s)
                dve.wait_ge(s_att, done(t))
                link = Chain(dve, s_chain, t * 3)
                a = ap[s][:, 0:CH * KVW].rearrange("p (h c) -> p h c", h=CH)
                link(dve.tensor_scalar(z[s][:, :, :], a[:, :, P:KVW], 1e-6, None, ALU.add))
                link(dve.reciprocal(z[s][:, :, :], z[s][:, :, :]))
                for h in range(CH):
                    ins = dve.tensor_tensor(part[s][:, h * P:h * P + P].rearrange("p (i c) -> p i c", c=D0),
                                            a[:, h, 0:P].rearrange("p (i c) -> p i c", c=D0),
                                            z[s][:, h, :].unsqueeze(2).to_broadcast([P, 4, D0]), ALU.mult)
                link(ins)
                dve.tensor_tensor(row(m.mix, t), part[s][:, :].unsqueeze(1), row(m.xn, t), ALU.add).then_inc(s_out, 1)

            low(0, 0)
            tiles(dve, step)

        @block.tensor
        def _(pe):
            opened(pe, s_q, s_att)

            def queries(t, s):
                pe.wait_ge(s_qs, freed(t))
                for o in range(CH):
                    for h in range(CH):
                        ins = pe.matmul(qp[s][:, o * P:o * P + P], wq[:, h, o * P:o * P + P],
                                        m.xnT[:, h, bass.ds(t * P, P)], start=h == 0, stop=h == CH - 1)
                ins.then_inc(s_q, 1)

            def step(t, s, k, last):
                if not last:
                    queries(t + 1, 1 - s)
                pe.wait_ge(s_qs, done(t))
                pe.wait_ge(s_out, freed(t))
                for h in range(CH):
                    ins = pe.matmul(ap[s][:, h * KVW:h * KVW + KVW], qs[s][:, h, :], m.bd[:, h, :],
                                    start=True, stop=True)
                ins.then_inc(s_att, 1)

            pe.wait_ge(s_w, 16)
            queries(0, 0)
            tiles(pe, step)



def phase_mlp(nc, m, d, share):
    s_w, s_normed, s_flipped, s_row, s_hid, s_gelu, s_y, s_out, s_wchain, s_tchain, s_last = m.sems(
        "mlp", "w normed flipped row hid gelu y out wchain tchain last")
    s_stats1, s_var1, s_std1, s_stats2, s_var2, s_std2 = m.sems("mlp", "stats1 var1 std1 stats2 var2 std2")
    with ExitStack() as mem, nc.Block() as block:
        sb = lambda name, shape, dt=F32: mem.enter_context(nc.sbuf_tensor("mlp_" + name, shape, dt))
        w1 = sb("w1", [P, CH, C])
        w2 = sb("w2", [P, CH, C])
        b1 = sb("b1", [P, CH])
        b2 = sb("b2", [1, C])
        gb = sb("gb", [P, 4, C])
        stats = sb("stats", [P, T, 6])
        raw = [sb(f"raw{s}", [P, C]) for s in range(SLOTS)]
        xs = [sb(f"xs{s}", [P, C]) for s in range(SLOTS)]
        xt = [sb(f"xt{s}", [P, CH, P]) for s in range(SLOTS)]
        hs = [sb(f"hs{s}", [P, CH, P]) for s in range(SLOTS)]
        flip, hp, yp = m.psum[0:2], m.psum[2:4], m.psum[4:6]
        NW = 4 + 4

        @block.sync
        def _(sp):
            for i, v in enumerate((d.ln1_g, d.ln1_b, d.ln2_g, d.ln2_b)):
                sp.dma_start(gb[:, i, :], v.rearrange("(a c) -> a c", a=1).to_broadcast([P, C])).then_inc(s_w, 16)
            sp.dma_start(w1[:, :, :], d.mw1.rearrange("(h p) o -> p h o", p=P)).then_inc(s_w, 16)
            sp.dma_start(w2[:, :, :], d.mw2.rearrange("(h p) o -> p h o", p=P)).then_inc(s_w, 16)
            sp.dma_start(b1[:, :], d.mb1).then_inc(s_w, 16)
            sp.dma_start(b2[:, :], d.mb2.rearrange("(a c) -> a c", a=1)).then_inc(s_w, 16)

        @block.gpsimd
        def _(pool):
            scatter_edges(pool, m, d, *share)

        @block.scalar
        def _(act):
            opened(act, s_gelu)
            stats_scalar(act, m, s_var1, s_std1)

            def step(t, s, k, last):
                act.wait_ge(s_hid, done(t))
                act.wait_ge(s_y, freed(t))
                for h in range(CH):
                    ins = act.activation(hs[s][:, h, :], hp[s][:, h * P:h * P + P], ACT.Gelu, bias=b1[:, h:h + 1])
                ins.then_inc(s_gelu, 1)

            act.wait_ge(s_w, 16 * NW)
            tiles(act, step)
            stats_scalar(act, m, s_var2, s_std2)

        @block.vector
        def _(dve):
            link = Chain(dve, s_wchain)
            opened(dve, s_normed, s_row, s_out)
            with dve.Fori(0, T) as t:
                row_stats(dve, m.mix, stats, t, s_stats1)
            dve.wait_ge(s_stats1, T)
            stats_vector(dve, link, m, stats[:, :, :], s_var1, s_std1)
            dve.wait_ge(s_w, 16 * NW)

            def norm(t, s):
                chain = Chain(dve, s_tchain, t * 2)
                chain(normalise(dve, m, raw[s][:, :].unsqueeze(1), t, m.mix))
                chain(dve.tensor_tensor(raw[s][:, :], raw[s][:, :], gb[:, 0, :], ALU.mult))
                dve.wait_ge(s_flipped, freed(t))
                dve.tensor_tensor(xs[s][:, :], raw[s][:, :], gb[:, 1, :], ALU.add).then_inc(s_normed, 1)

            def turn(t, s):
                dve.wait_ge(s_flipped, done(t))
                dve.wait_ge(s_hid, freed(t))
                dve.tensor_copy(xt[s][:, :, :], flip[s][:, 0:C].rearrange("p (h c) -> p h c", h=CH)).then_inc(s_row, 1)

            def step(t, s, k, last):
                if not last:
                    norm(t + 1, 1 - s)
                    turn(t + 1, 1 - s)
                dve.wait_ge(s_y, done(t))
                dve.wait_ge(s_normed, done(t))
                dve.tensor_tensor(row(m.mix, t), yp[s][:, 0:C].unsqueeze(1), xs[s][:, :].unsqueeze(1), ALU.add).then_inc(s_out, 1)
                dve.wait_ge(s_out, done(t))
                row_stats(dve, m.mix, stats, t, s_stats2)

            norm(0, 0)
            turn(0, 0)
            tiles(dve, step)
            dve.wait_ge(s_stats2, T)
            stats_vector(dve, link, m, stats[:, :, :], s_var2, s_std2)
            with dve.Fori(0, T) as t:
                normalise(dve, m, row(m.mix, t), t, m.mix).then_inc(s_last, 1)
            dve.wait_ge(s_last, T)
            link(dve.tensor_tensor(m.mix[:, :, :], m.mix[:, :, :], gb[:, 2:3, :].to_broadcast([P, T, C]), ALU.mult))
            link(dve.tensor_tensor(m.mix[:, :, :], m.mix[:, :, :], gb[:, 3:4, :].to_broadcast([P, T, C]), ALU.add))
            link(dve.tensor_tensor(m.x[:, :, :], m.x[:, :, :], m.mix[:, :, :], ALU.add))

        @block.tensor
        def _(pe):
            opened(pe, s_flipped, s_hid, s_y)

            def flips(t, s):
                pe.wait_ge(s_normed, done(t))
                pe.wait_ge(s_row, freed(t))
                for h in range(CH):
                    ins = pe.transpose(flip[s][:, h * P:h * P + P], xs[s][:, h * P:h * P + P], m.ident[:, :])
                ins.then_inc(s_flipped, 1)

            def step(t, s, k, last):
                pe.wait_ge(s_row, done(t))
                pe.wait_ge(s_gelu, freed(t))
                for o in range(CH):
                    for h in range(CH):
                        ins = pe.matmul(hp[s][:, o * P:o * P + P], w1[:, h, o * P:o * P + P], xt[s][:, h, :],
                                        start=h == 0, stop=h == CH - 1)
                ins.then_inc(s_hid, 1)
                if not last:
                    flips(t + 1, 1 - s)
                pe.wait_ge(s_out, freed(t))
                pe.matmul(yp[s][:, 0:C], m.ones[0:1, :], b2[:, :], start=True, stop=False)
                pe.wait_ge(s_gelu, done(t))
                for h in range(CH):
                    ins = pe.matmul(yp[s][:, 0:C], hs[s][:, h, :], w2[:, h, :], start=False, stop=h == CH - 1)
                ins.then_inc(s_y, 1)

            pe.wait_ge(s_w, 16 * NW)
            flips(0, 0)
            tiles(pe, step)



def phase_aggregate(nc, m, d):
    s_rec, s_idx, s_issue, s_hot, s_sum, s_add, s_zero, s_wchain = m.sems("agg", "rec idx issue hot sum add zero wchain")
    s_mean, s_dev, s_sq, s_var, s_vare, s_sd, s_aff, s_tanh = m.sems("agg", "mean dev sq var vare sd aff tanh")
    s_masked, s_stats = m.sems("agg", "masked stats")
    s_row = m.sems("agg", " ".join(f"row{u}" for u in range(GB)))
    HALF = GB // 2
    GROUP = 8
    PART = 5
    parts = [slice(t, t + PART) for t in range(0, T, PART)]
    OH, AHEAD = 4, 3
    with ExitStack() as mem, nc.Block() as block:
        sb = lambda name, shape, dt=F32: mem.enter_context(nc.sbuf_tensor("agg_" + name, shape, dt))
        acc = sb("acc", [P, T, C])
        tmp = m.mix
        recs = sb("recs", [P, EBLK, 4])
        bn = sb("bn", [P, 2, C])
        stat = sb("stat", [P, 4, C])
        rows = [sb(f"rows{u}", [P, C]) for u in range(GB)]
        idx = [sb(f"idx{h}", [P, HALF], I32) for h in range(2)]
        hot = [sb(f"hot{u}", [P, P]) for u in range(OH)]
        bank = m.psum[0:OH]

        @block.sync
        def _(sp):
            sp.dma_start(recs[:, :, :].rearrange("p j r -> p (j r)"), d.rec.rearrange("(p j) r -> p (j r)", p=P)).then_inc(s_rec, 16)
            sp.dma_start(bn[:, 0, :], d.bn_w.rearrange("(a c) -> a c", a=1).to_broadcast([P, C])).then_inc(s_rec, 16)
            sp.dma_start(bn[:, 1, :], d.bn_b.rearrange("(a c) -> a c", a=1).to_broadcast([P, C])).then_inc(s_rec, 16)


        @block.gpsimd
        def _(pool):
            with pool.Fori(0, EBLK // GB) as k:
                for h in range(2):
                    pool.wait_ge(s_idx, k * 2 + h + 1)
                    pool.sem_inc(s_issue, 1)
                    for u in range(HALF):
                        v = h * HALF + u
                        pool.indirect_dma_start(out=rows[v][:, :], out_offset=None, in_=d.support,
                                                in_offset=bass.IndirectOffsetOnAxis(ap=idx[h][:, u:u + 1], axis=0))\
                            .then_inc(s_row[v], 16)

        @block.vector
        def _(dve):
            dve.memset(acc[:, :, :], 0.0).then_inc(s_zero, 1)
            dve.sem_inc(s_add, OH)
            dve.wait_ge(s_zero, 1)
            dve.wait_ge(s_rec, 48)

            def weigh(j, u):
                dve.wait_ge(s_sum, j + 1 + GB - OH)
                dve.tensor_scalar(hot[u % OH][:, :], m.iota[:, 0:P], recs[:, bass.ds(j, 1), 0], recs[:, bass.ds(j, 1), 1],
                                  ALU.is_equal, ALU.mult).then_inc(s_hot, 1)

            def owners(j):
                _, tile = nc.values_load_multi_w_load_instructions(m.eowner[0:1, bass.ds(j, GROUP)], [mybir.EngineType.DVE],
                                                                   min_val=0, max_val=T - 1)
                return tile

            def add(j, u, owner):
                dve.wait_ge(s_sum, j + GB + 1)
                dve.wait_ge(s_add, j + OH)
                a = acc[:, bass.ds(owner, 1), :]
                dve.tensor_tensor(a, a, bank[u % OH][:, 0:C].unsqueeze(1), ALU.add).then_inc(s_add, 1)

            for u in range(AHEAD):
                weigh(u, u)
            with dve.Fori(0, EBLK // GROUP - 1) as k:
                tile = owners(k * GROUP)
                for u in range(GROUP):
                    weigh(k * GROUP + u + AHEAD, u + AHEAD)
                    add(k * GROUP + u, u, tile[u])
            tile = owners(EBLK - GROUP)
            for u in range(GROUP):
                if u + AHEAD < GROUP:
                    weigh(EBLK - GROUP + u + AHEAD, u + AHEAD)
                add(EBLK - GROUP + u, u, tile[u])
            link = Chain(dve, s_wchain)
            dve.wait_ge(s_add, EBLK + OH)
            mean, var, gain, shift = (stat[:, i, :] for i in range(4))
            dve.tensor_reduce(mean, acc[:, :, :].rearrange("p t c -> p c t"), AX.X, ALU.add).then_inc(s_mean, 1)
            dve.wait_ge(s_mean, 2)
            link(dve.tensor_scalar(mean, m.psum[4][:, 0:C], 1.0 / N, None, ALU.mult))
            for g in parts:
                dve.tensor_tensor(acc[:, g, :], acc[:, g, :], stat[:, 0:1, :].to_broadcast([P, PART, C]),
                                  ALU.subtract).then_inc(s_dev, 1)
            dve.wait_ge(s_sq, len(parts))
            dve.tensor_scalar(tmp[:, T - 1, :], tmp[:, T - 1, :], m.lastmask[:, 0:1], None, ALU.mult).then_inc(s_masked, 1)
            dve.wait_ge(s_var, 1)
            dve.tensor_scalar(var, m.psum[5][:, 0:C], 1.0 / N, 1e-5, ALU.mult, ALU.add).then_inc(s_vare, 1)
            dve.wait_ge(s_sd, 1)
            link(dve.reciprocal(gain, shift))
            link(dve.tensor_tensor(gain, gain, bn[:, 0, :], ALU.mult))

            def add_out(i):
                g = parts[i]
                dve.wait_ge(s_tanh, i + 1)
                link(dve.tensor_tensor(m.x[:, g, :], m.x[:, g, :], tmp[:, g, :], ALU.add))
                for t in range(g.start, g.stop):
                    row_stats(dve, m.x, m.stats, t, s_stats)

            for i, g in enumerate(parts):
                link(dve.tensor_tensor(acc[:, g, :], acc[:, g, :], stat[:, 2:3, :].to_broadcast([P, PART, C]), ALU.mult))
                dve.tensor_tensor(acc[:, g, :], acc[:, g, :], bn[:, 1:2, :].to_broadcast([P, PART, C]), ALU.add).then_inc(s_aff, 1)
                if i > 0:
                    add_out(i - 1)
            add_out(len(parts) - 1)
            dve.wait_ge(s_stats, T)

        @block.scalar
        def _(act):
            act.wait_ge(s_rec, 48)
            with act.Fori(0, EBLK // GB) as k:
                for h in range(2):
                    col = k * GB + h * HALF
                    act.wait_ge(s_sum, col + HALF)
                    act.activation(idx[h][:, :], recs.bitcast(I32)[:, bass.ds(col, HALF), 2], ACT.Copy).then_inc(s_idx, 1)
            for i, g in enumerate(parts):
                act.wait_ge(s_dev, i + 1)
                act.activation(tmp[:, g, :], acc[:, g, :], ACT.Square).then_inc(s_sq, 1)
            act.wait_ge(s_vare, 1)
            act.activation(stat[:, 3, :], stat[:, 1, :], ACT.Sqrt).then_inc(s_sd, 1)
            for i, g in enumerate(parts):
                act.wait_ge(s_aff, i + 1)
                act.activation(tmp[:, g, :], acc[:, g, :], ACT.Tanh).then_inc(s_tanh, 1)

        @block.tensor
        def _(pe):
            pe.sem_inc(s_sum, GB)
            with pe.Fori(0, EBLK // GB) as k:
                for u in range(GB):
                    j = k * GB + u
                    pe.wait_ge(s_hot, j + 1)
                    pe.wait_ge(s_row[u], k * 16 + 16)
                    pe.wait_ge(s_add, j + 1)
                    pe.matmul(bank[u % OH][:, 0:C], hot[u % OH][:, :], rows[u][:, :], start=True, stop=True)\
                      .then_inc(s_sum, 1)

            pe.wait_ge(s_mean, 1)
            pe.matmul(m.psum[4][:, 0:C], m.ones[:, :], stat[:, 0, :], start=True, stop=True).then_inc(s_mean, 1)
            for i, g in enumerate(parts):
                if i < len(parts) - 1:
                    pe.wait_ge(s_sq, i + 1)
                else:
                    pe.wait_ge(s_masked, 1)
                for t in range(g.start, g.stop):
                    ins = pe.matmul(m.psum[5][:, 0:C], m.ones[:, :], tmp[:, t, :], start=t == 0, stop=t == T - 1)
            ins.then_inc(s_var, 1)


def first_best(dve, m, link, score, best, place, tmp):
    wide = lambda a: a.unsqueeze(2).to_broadcast([P, T, X])
    link(dve.tensor_reduce(best, score[:, :, :], AX.X, ALU.max))
    link(dve.tensor_tensor(tmp[:, :, :], score[:, :, :], wide(best), ALU.is_lt))
    link(dve.scalar_tensor_tensor(out=tmp[:, :, :], in0=tmp[:, :, :], scalar=float(X),
                                  in1=m.iota[:, 0:X].unsqueeze(1).to_broadcast([P, T, X]), op0=ALU.mult, op1=ALU.add))
    link(dve.tensor_reduce(place, tmp[:, :, :], AX.X, ALU.min))



def phase_route0(nc, m, d, w2):
    s_w, s_copied, s_flipped, s_row, s_gate, s_gated, s_wchain, s_diff, s_exp, s_counts, s_totals, \
        s_hot, s_placed, s_lchain = m.sems(
            "rt0", "w copied flipped row gate gated wchain diff exp counts totals hot placed lchain")
    s_var, s_std = m.sems("rt0", "var std")
    s_kept = m.sems("rt0", "kept0 kept1")
    K = 2
    with ExitStack() as mem, nc.Block() as block:
        sb = lambda name, shape, dt=F32: mem.enter_context(nc.sbuf_tensor("rt0_" + name, shape, dt))
        small6 = sb("small6", [P, 6, 32])
        wg = sb("wg", [P, CH, X])
        bg = sb("bg", [P, X])
        xs = [sb(f"xs{s}", [P, C]) for s in range(SLOTS)]
        xt = [sb(f"xt{s}", [P, CH, P]) for s in range(SLOTS)]
        score = sb("score", [P, T, X])
        equal = sb("equal", [P, T, X])
        top = sb("top", [P, T, K])
        key = sb("key", [P, T, K])
        onehot = sb("onehot", [P, K * T * X])
        count = sb("count", [P, K * T * X])
        pos = sb("pos", [P, T * K])
        work = sb("work", [P, 4, max(K * T, FBLK0)])
        whole = sb("whole", [P, 3, K * T], I32)
        hi_hot = sb("hi_hot", [P, K * T, FBLK0])
        lo_hot = [sb(f"lo_hot{s}", [P, PICK, P]) for s in range(SLOTS)]
        flip, gp = m.psum[0:2], m.psum[2:4]

        @block.sync
        def _(sp):
            sp.dma_start(wg[:, :, :], d.f0_wg.rearrange("(h p) e -> p h e", p=P)).then_inc(s_w, 16)
            sp.dma_start(bg[:, :], d.f0_bg.rearrange("(a c) -> a c", a=1).to_broadcast([P, X])).then_inc(s_w, 16)
            for e in range(X):
                sp.dma_start(w2[:, e, :, :], d.f0_w2[e, :, :].rearrange("(h p) o -> p h o", p=P)).then_inc(m.s_w2, 16)

            def keep(t, s, k, last):
                sp.wait_ge(s_copied, done(t))
                sp.dma_start(d.normed0[bass.ds(t * P, P), :], xs[s][:, :]).then_inc(s_kept[s], 16)
            tiles(sp, keep)
            for s in range(SLOTS):
                sp.wait_ge(s_kept[s], 16 * ((T - s + 1) // 2))

        @block.scalar
        def _(act):
            stats_scalar(act, m, s_var, s_std)
            act.wait_ge(s_diff, 1)
            act.activation(m.prob[:, :, 1], top[:, :, 1], ACT.Exp).then_inc(s_exp, 1)

        @block.vector
        def _(dve):
            link = Chain(dve, s_wchain)
            stats_vector(dve, link, m, m.stats[:, :, :], s_var, s_std)
            dve.wait_ge(s_w, 32)
            opened(dve, s_copied, s_row, s_gated)

            def norm(t, s, uses):
                dve.wait_ge(s_flipped, freed(t))
                landed(dve, s_kept[s], uses)
                normalise(dve, m, xs[s][:, :].unsqueeze(1), t).then_inc(s_copied, 1)

            def turn(t, s):
                dve.wait_ge(s_flipped, done(t))
                dve.wait_ge(s_gate, freed(t))
                dve.tensor_copy(xt[s][:, :, :], flip[s][:, 0:C].rearrange("p (h c) -> p h c", h=CH)).then_inc(s_row, 1)

            def step(t, s, k, last):
                if not last:
                    norm(t + 1, 1 - s, k + s)
                    turn(t + 1, 1 - s)
                dve.wait_ge(s_gate, done(t))
                dve.tensor_tensor(row(score, t), gp[s][:, 0:X].unsqueeze(1), bg[:, :].unsqueeze(1), ALU.add).then_inc(s_gated, 1)

            norm(0, 0, 0)
            turn(0, 0)
            tiles(dve, step, peel=True)
            dve.wait_ge(s_gated, done(T - 1))
            link = Chain(dve, s_lchain)
            first_best(dve, m, link, score, top[:, :, 0], key[:, :, 0], equal)
            link(dve.tensor_tensor(equal[:, :, :], m.iota[:, 0:X].unsqueeze(1).to_broadcast([P, T, X]),
                                   key[:, :, 0].unsqueeze(2).to_broadcast([P, T, X]), ALU.is_equal))
            link(dve.scalar_tensor_tensor(out=score[:, :, :], in0=equal[:, :, :], scalar=-3e38, in1=score[:, :, :],
                                          op0=ALU.mult, op1=ALU.add))
            first_best(dve, m, link, score, top[:, :, 1], key[:, :, 1], equal)
            dve.tensor_tensor(top[:, :, 1], top[:, :, 1], top[:, :, 0], ALU.subtract).then_inc(s_diff, 1)
            dve.wait_ge(s_exp, 1)
            link(dve.tensor_scalar(m.prob[:, :, 0], m.prob[:, :, 1], 1.0, None, ALU.add))
            link(dve.reciprocal(m.prob[:, :, 0], m.prob[:, :, 0]))
            link(dve.tensor_tensor(m.prob[:, :, 1], m.prob[:, :, 1], m.prob[:, :, 0], ALU.mult))
            sort_vector(dve, m, link, key[:, :, :].rearrange("p t k -> p (t k)"), onehot, count, small6, m.psum[4],
                        pos[:, :], s_counts, s_totals, X, K * T)
            invert_vector(dve, m, link, pos[:, :], m.row2[:, :, :].rearrange("p t k -> p (t k)"), work, whole, hi_hot[:, :, :], lo_hot, m.psum[5],
                          K * T, FBLK0, s_hot, s_placed)
            sort_owner(dve, m, link, small6[:, 5, :], count[:, 0:FBLK0], m.fown[:, 0:FBLK0], X, FBLK0)

        @block.tensor
        def _(pe):
            opened(pe, s_flipped, s_gate)
            pe.wait_ge(s_w, 32)

            def flips(t, s):
                pe.wait_ge(s_copied, done(t))
                pe.wait_ge(s_row, freed(t))
                for h in range(CH):
                    ins = pe.transpose(flip[s][:, h * P:h * P + P], xs[s][:, h * P:h * P + P], m.ident[:, :])
                ins.then_inc(s_flipped, 1)

            def step(t, s, k, last):
                pe.wait_ge(s_row, done(t))
                pe.wait_ge(s_gated, freed(t))
                for h in range(CH):
                    ins = pe.matmul(gp[s][:, 0:X], xt[s][:, h, :], wg[:, h, :], start=h == 0, stop=h == CH - 1)
                ins.then_inc(s_gate, 1)
                if not last:
                    flips(t + 1, 1 - s)

            flips(0, 0)
            tiles(pe, step)
            sort_tensor(pe, m, small6, m.psum[4], s_counts, s_totals, X)
            invert_tensor(pe, m, hi_hot, lo_hot, m.psum[5], K * T, FBLK0, s_hot, s_placed)


def hidden_turned(pe, hp, w1, xt):
    for q in range(HC):
        for h in range(CH):
            ins = pe.matmul(hp[q // 4][:, q % 4 * P:q % 4 * P + P], w1[:, h, q * P:q * P + P], xt[:, h, :],
                            start=h == 0, stop=h == CH - 1)
    return ins


def gather(pool, m, rows, xin, slot, j, s_token, s_gather, s_load):
    pool.tensor_copy(slot[:, :], m.token[:, bass.ds(j, 1)]).then_inc(s_token, 1)
    pool.wait_ge(s_token, j + 1)
    pool.sem_inc(s_gather, 1)
    pool.indirect_dma_start(out=xin[:, :], out_offset=None, in_=rows,
                            in_offset=bass.IndirectOffsetOnAxis(ap=slot[:, 0:1], axis=0)).then_inc(s_load, 16)


def results(pool, m, rows, k, ys, slot, j, s_slot, s_issue, s_store):
    pool.tensor_copy(slot[:, :], m.dest[:, bass.ds(j, 1)]).then_inc(s_slot, 1)
    pool.wait_ge(s_slot, j + 1)
    pool.sem_inc(s_issue, 1)
    pool.indirect_dma_start(out=rows, out_offset=bass.IndirectOffsetOnAxis(ap=slot[:, 0:1], axis=0), in_=ys[:, :],
                            in_offset=None, bounds_check=k * T * P - 1, oob_is_err=False).then_inc(s_store, 16)



def phase_experts(nc, m, name, nblk, normed, out, K, function, w2, b2_rows, s_w2, b1_rows=None):
    s_w, s_flipped, s_row, s_hid, s_held, s_y, s_out, s_picked = m.sems(name, "w flipped row hid held y out picked")
    s_slot, s_issue, s_token, s_gather = m.sems(name, "slot issue token gather")
    s_load, s_store = m.sems(name, "load0 load1"), m.sems(name, "store0 store1")
    own = b1_rows is not None
    with ExitStack() as mem, nc.Block() as block:
        sb = lambda what, shape, dt=F32: mem.enter_context(nc.sbuf_tensor(name + "_" + what, shape, dt))
        b2 = sb("b2", [P, X, C])
        xin = [sb(f"xin{s}", [P, C]) for s in range(SLOTS)]
        token = [sb(f"token{s}", [P, 1], I32) for s in range(SLOTS)]
        slot = [sb(f"slot{s}", [P, 1], I32) for s in range(SLOTS)]
        xt = [sb(f"xt{s}", [P, CH, P]) for s in range(SLOTS)]
        hs = [sb(f"hs{s}", [P, HC, P]) for s in range(SLOTS)]
        ys = [sb(f"ys{s}", [P, C]) for s in range(SLOTS)]
        if own:
            b1_all = sb("b1_all", [P, X, HC])
            w1 = [sb(f"w1{s}", [P, CH, HID]) for s in range(SLOTS)]
            b1 = [sb(f"b1{s}", [P, HC]) for s in range(SLOTS)]
        else:
            w1, b1 = [m.f1_w1] * SLOTS, [m.f1_b1] * SLOTS
        flip, yp, hp = m.psum[0:2], m.psum[2:4], [m.psum[4:6], m.psum[6:8]]
        NW = 2 if own else 1

        @block.sync
        def _(sp):
            if own:
                sp.dma_start(b1_all[:, :, :], b1_rows).then_inc(s_w, 16)
            sp.dma_start(b2[:, :, :].rearrange("p e c -> p (e c)"),
                         b2_rows.rearrange("e c -> (e c)").rearrange("(a c) -> a c", a=1).to_broadcast([P, X * C])).then_inc(s_w, 16)

        @block.gpsimd
        def _(pool):
            fetch = lambda j, s: gather(pool, m, normed, xin[s], token[s], j, s_token, s_gather, s_load[s])
            send = lambda j, s: results(pool, m, out, K, ys[s], slot[s], j, s_slot, s_issue, s_store[s])
            fetch(0, 0)
            fetch(1, 1)

            def step(j, s, k, last):
                if not last:
                    pool.wait_ge(s_row, done(j))
                    fetch(j + 2, s)
                if not isinstance(j, int) or j > 0:
                    pool.wait_ge(s_out, done(j - 1))
                    send(j - 1, 1 - s)
            tiles(pool, step, nblk - 1, peel=True)
            pool.wait_ge(s_out, done(nblk - 1))
            send(nblk - 2, (nblk - 2) % 2)
            send(nblk - 1, (nblk - 1) % 2)
            for s in range(SLOTS):
                pool.wait_ge(s_store[s], 16 * ((nblk - s + 1) // 2))

        @block.scalar
        def _(act):
            opened(act, s_held)

            def step(j, s, k, last):
                act.wait_ge(s_hid, done(j))
                act.wait_ge(s_y, freed(j))
                for q in range(HC):
                    ins = act.activation(hs[s][:, q, :], hp[s][q // 4][:, q % 4 * P:q % 4 * P + P], function, bias=b1[s][:, q:q + 1])
                ins.then_inc(s_held, 1)
            tiles(act, step, nblk)

        @block.vector
        def _(dve):
            opened(dve, s_row, s_out, s_picked)
            dve.wait_ge(s_w, 16 * NW)
            if own:
                dve.wait_ge(m.s_w1, 16 * X)

            def turn(j, s):
                dve.wait_ge(s_flipped, done(j))
                dve.wait_ge(s_hid, freed(j))
                dve.tensor_copy(xt[s][:, :, :], flip[s][:, 0:C].rearrange("p (h c) -> p h c", h=CH)).then_inc(s_row, 1)

            def pick(j, s):
                if own:
                    e = dve.value_load(m.fown[0:1, bass.ds(j, 1)], min_val=0, max_val=X - 1)
                    dve.wait_ge(s_hid, freed(j))
                    dve.wait_ge(s_held, freed(j))
                    dve.tensor_copy(b1[s][:, :].unsqueeze(1), b1_all[:, bass.ds(e, 1), :])
                    dve.tensor_copy(w1[s][:, :, :].unsqueeze(1), m.w1[:, bass.ds(e, 1), :, :]).then_inc(s_picked, 1)

            def result(j, s, k):
                e = dve.value_load(m.fown[0:1, bass.ds(j, 1)], min_val=0, max_val=X - 1)
                dve.wait_ge(s_y, done(j))
                landed(dve, s_store[s], k)
                dve.tensor_tensor(ys[s][:, :].unsqueeze(1), yp[s][:, 0:C].unsqueeze(1), b2[:, bass.ds(e, 1), :], ALU.add).then_inc(s_out, 1)

            for j in range(2):
                pick(j, j)
                turn(j, j)

            def step(j, s, k, last):
                if not last:
                    turn(j + 2, s)
                    pick(j + 2, s)
                result(j, s, k)
            tiles(dve, step, nblk - 1, peel=True)
            result(nblk - 1, (nblk - 1) % 2, (nblk - 1) // 2)

        @block.tensor
        def _(pe):
            opened(pe, s_flipped, s_hid, s_y)

            def flips(j, s, k):
                pe.wait_ge(s_load[s], 16 * k + 16)
                pe.wait_ge(s_row, freed(j))
                for h in range(CH):
                    ins = pe.transpose(flip[s][:, h * P:h * P + P], xin[s][:, h * P:h * P + P], m.ident[:, :])
                ins.then_inc(s_flipped, 1)

            def hidden(j, s):
                pe.wait_ge(s_row, done(j))
                pe.wait_ge(s_held, freed(j))
                if own:
                    pe.wait_ge(s_picked, done(j))
                hidden_turned(pe, hp[s], w1[s], xt[s]).then_inc(s_hid, 1)

            def result(j, s):
                e = pe.value_load(m.fown[0:1, bass.ds(j, 1)], min_val=0, max_val=X - 1)
                pe.wait_ge(s_held, done(j))
                pe.wait_ge(s_out, freed(j))
                for q in range(HC):
                    ins = pe.matmul(yp[s][:, 0:C], hs[s][:, q, :], w2[:, bass.ds(e, 1), q, :], start=q == 0, stop=q == HC - 1)
                ins.then_inc(s_y, 1)

            flips(0, 0, 0)
            hidden(0, 0)
            flips(1, 1, 0)
            pe.wait_ge(s_w2, 16 * X)

            def step(j, s, k, last):
                hidden(j + 1, 1 - s)
                if not last:
                    flips(j + 2, s, k + 1)
                result(j, s)
            tiles(pe, step, nblk - 1)
            result(nblk - 1, (nblk - 1) % 2)



def phase_combine(nc, m, name, results, K, stats_too):
    GROUP = 5
    s_chain, s_stats, s_wchain, s_var, s_std = m.sems(name, "chain stats wchain var std")
    s_y = m.sems(name, " ".join(f"y{g}" for g in range(T // GROUP)))
    with ExitStack() as mem, nc.Block() as block:
        sb = lambda n, shape, dt=F32: mem.enter_context(nc.sbuf_tensor(name + n, shape, dt))
        y = sb("y", [P, K, T, C])
        stats = sb("stats", [P, T, 6])
        by_tile = results.rearrange("(k t p) c -> p k t c", k=K, p=P)

        @block.sync
        def _(sp):
            for g, s in enumerate(s_y):
                for k in range(K):
                    sp.dma_start(y[:, k, g * GROUP:(g + 1) * GROUP, :], by_tile[:, k, g * GROUP:(g + 1) * GROUP, :]).then_inc(s, 16)

        @block.scalar
        def _(act):
            if stats_too:
                stats_scalar(act, m, s_var, s_std)

        @block.vector
        def _(dve):
            for g, s in enumerate(s_y):
                dve.wait_ge(s, 16 * K)
                with dve.Fori(0, GROUP) as i:
                    t = i + g * GROUP
                    link = Chain(dve, s_chain, t * K)
                    for k in range(K):
                        link(dve.scalar_tensor_tensor(out=row(m.x, t), in0=y[:, k, bass.ds(t, 1), :],
                                                      scalar=m.prob[:, bass.ds(t, 1), k], in1=row(m.x, t), op0=ALU.mult, op1=ALU.add))
                    if stats_too:
                        row_stats(dve, m.x, stats, t, s_stats)
            if stats_too:
                dve.wait_ge(s_stats, T)
                stats_vector(dve, Chain(dve, s_wchain), m, stats[:, :, :], s_var, s_std)




def phase_project1(nc, m, d):
    s_w, s_normed, s_flipped, s_row, s_rowall, s_proj, s_xt, s_chain, s_var, s_std, s_centred, s_gain, s_kv, s_block, \
        s_r, s_rheld, s_m, s_built = m.sems(
            "pr1", "w normed flipped row rowall proj xt chain var std centred gain kv block r rheld m built")
    s_store = m.sems("pr1", "store0 store1")
    s_fold = m.sem("pr1_fold")
    s_wchain, s_gchain = m.sems("pr1", "wchain gchain")
    G = 2 * H1
    with ExitStack() as mem, nc.Block() as block:
        sb = lambda name, shape, dt=F32: mem.enter_context(nc.sbuf_tensor("pr1_" + name, shape, dt))
        w = sb("w", [P, CH, 2 * C + GROW])
        attn = sb("attn", [P, 2, C])
        scaled = [sb(f"scaled{u}", [P, CH, C]) for u in range(2)]
        wo = sb("wo", [P, CH, C])
        wq = sb("wq", [P, CH, C])
        gb = sb("gb", [P, 2, G * D1])
        xs = [sb(f"xs{s}", [P, C]) for s in range(SLOTS)]
        xt = [sb(f"xt{s}", [P, CH, P]) for s in range(SLOTS)]
        gr = [sb(f"gr{s}", [P, GROW]) for s in range(SLOTS)]
        stats = [sb(f"stats{s}", [P, G, 6]) for s in range(SLOTS)]
        mean = [sb(f"mean{s}", [P, G]) for s in range(SLOTS)]
        dif = [sb(f"dif{s}", [P, G]) for s in range(SLOTS)]
        var = [sb(f"var{s}", [P, G]) for s in range(SLOTS)]
        std = [sb(f"std{s}", [P, G]) for s in range(SLOTS)]
        kn = [sb(f"kn{s}", [P, G * D1]) for s in range(SLOTS)]
        kv = [sb(f"kv{s}", [P, G * D1]) for s in range(SLOTS)]
        bd = sb("bd", [P, CH, P])
        r_ = sb("r", [P, CH, C])
        flip, kvp, grp, acc = m.psum[0:2], m.psum[2:4], m.psum[4:6], m.psum[6:8]
        NW = 7 + 2 * G

        @block.sync
        def _(sp):
            for i, a in enumerate((d.wk, d.wv, d.g_w)):
                sp.dma_start(w[:, :, i * C:i * C + C], a.rearrange("(h p) o -> p h o", p=P)).then_inc(s_w, 16)
            for u, a in enumerate((d.g_al, d.g_ar)):
                sp.dma_start(attn[:, u, :], a.rearrange("h c -> (h c)").rearrange("(a c) -> a c", a=1).to_broadcast([P, C])).then_inc(s_w, 16)
            sp.dma_start(wo[:, :, :], d.wo.rearrange("(h p) o -> p h o", p=P)).then_inc(s_w, 16)
            sp.dma_start(wq[:, :, :], d.wq.rearrange("(h p) o -> p h o", p=P)).then_inc(s_w, 16)
            for i, pair in enumerate(((d.k_g, d.v_g), (d.k_b, d.v_b))):
                for g in range(G):
                    v = pair[g // H1]
                    sp.dma_start(gb[:, i, g * D1:g * D1 + D1], v.rearrange("(a c) -> a c", a=1).to_broadcast([P, D1])).then_inc(s_w, 16)

            def step(t, s, k, last):
                sp.wait_ge(s_xt, done(t))
                sp.dma_start(d.graph[bass.ds(t * P, P), :], gr[s][:, :]).then_inc(s_store[s], 16)
            tiles(sp, step)
            for s in range(SLOTS):
                sp.wait_ge(s_store[s], 16 * ((T - s + 1) // 2))

        @block.gpsimd
        def _(pool):
            opened(pool, s_gain)
            pool.wait_ge(s_w, 16 * NW)

            def step(t, s, k, last):
                pool.wait_ge(s_centred, done(t))
                pool.wait_ge(s_kv, freed(t))
                pool.tensor_tensor(kv[s][:, :], kn[s][:, :], gb[:, 0, :], ALU.mult).then_inc(s_gchain, 1)
                pool.wait_ge(s_gchain, t + 1)
                ins = pool.tensor_tensor(kv[s][:, :], kv[s][:, :], gb[:, 1, :], ALU.add)
                if last:
                    ins.then_inc(s_gchain, 1)
                    pool.wait_ge(s_gchain, T + 1)
                    ins = pool.tensor_tensor(kv[s][:, 0:C], kv[s][:, 0:C], m.lastmask[:, 0:1].to_broadcast([P, C]), ALU.mult)
                ins.then_inc(s_gain, 1)
            tiles(pool, step)

        @block.scalar
        def _(act):
            opened(act, s_rowall, s_xt, s_std)

            def step(t, s, k, last):
                act.wait_ge(s_row, done(t))
                act.activation(m.xnT[:, :, bass.ds(t * P, P)], xt[s][:, :, :], ACT.Copy).then_inc(s_rowall, 1)
                act.wait_ge(s_var, done(t))
                act.activation(std[s][:, :], var[s][:, :], ACT.Sqrt).then_inc(s_std, 1)
                act.wait_ge(s_proj, done(t))
                landed(act, s_store[s], k)
                act.activation(gr[s][:, :], grp[s][:, 0:GROW], ACT.Copy).then_inc(s_xt, 1)
            tiles(act, step, peel=True)

        @block.vector
        def _(dve):
            opened(dve, s_normed, s_row, s_var, s_centred)
            wlink = Chain(dve, s_wchain)
            wlink(dve.memset(bd[:, :, :], 0.0))

            def norm(t, s):
                dve.wait_ge(s_flipped, freed(t))
                normalise(dve, m, xs[s][:, :].unsqueeze(1), t).then_inc(s_normed, 1)

            def turn(t, s):
                dve.wait_ge(s_flipped, done(t))
                dve.wait_ge(s_proj, freed(t))
                dve.wait_ge(s_rowall, freed(t))
                dve.tensor_copy(xt[s][:, :, :], flip[s][:, 0:C].rearrange("p (h c) -> p h c", h=CH)).then_inc(s_row, 1)

            def step(t, s, k, last):
                dve.wait_ge(s_proj, done(t))
                link = Chain(dve, s_chain, t * 4)
                for g in range(G):
                    ins = dve.bn_stats(stats[s][:, g, :], kvp[s][:, g * D1:g * D1 + D1])
                link(ins)
                even, odd = stats[s][:, :, 0:3], stats[s][:, :, 3:6]
                dve.tensor_tensor(dif[s][:, :], even[:, :, 1], odd[:, :, 1], ALU.subtract)
                dve.tensor_tensor(var[s][:, :], even[:, :, 2], odd[:, :, 2], ALU.add)
                link(dve.tensor_tensor(mean[s][:, :], even[:, :, 1], odd[:, :, 1], ALU.add))
                dve.tensor_scalar(mean[s][:, :], mean[s][:, :], 0.5, None, ALU.mult)
                dve.scalar_tensor_tensor(out=dif[s][:, :], in0=dif[s][:, :], scalar=0.25, in1=dif[s][:, :], op0=ALU.mult, op1=ALU.mult)
                link(dve.tensor_scalar(var[s][:, :], var[s][:, :], 1.0 / D1, 1e-5, ALU.mult, ALU.add))
                dve.tensor_tensor(var[s][:, :], var[s][:, :], dif[s][:, :], ALU.add).then_inc(s_var, 1)
                if not last:
                    norm(t + 2, s)
                dve.wait_ge(s_std, done(t))
                link(dve.reciprocal(std[s][:, :], std[s][:, :]))
                dve.wait_ge(s_gain, freed(t))
                for g in range(G):
                    q = slice(g * D1, g * D1 + D1)
                    ins = dve.tensor_scalar(kn[s][:, q], kvp[s][:, q], mean[s][:, g:g + 1], std[s][:, g:g + 1],
                                            ALU.subtract, ALU.mult)
                ins.then_inc(s_centred, 1)
                if not last:
                    turn(t + 2, s)

            for t in range(2):
                norm(t, t)
            for t in range(2):
                turn(t, t)
            dve.wait_ge(s_w, 16 * NW)
            for u in range(2):
                ins = dve.tensor_tensor(scaled[u][:, :, :], w[:, :, 2 * C:3 * C], attn[:, u:u + 1, :].to_broadcast([P, CH, C]), ALU.mult)
            wlink(ins)
            for u in range(2):
                ins = dve.tensor_reduce(w[:, :, 3 * C + u * H1:3 * C + (u + 1) * H1],
                                        scaled[u][:, :, :].rearrange("p k (h c) -> p k h c", h=H1), AX.X, ALU.add)
            ins.then_inc(s_fold, 1)
            tiles(dve, step, T - 1)
            step(T - 1, (T - 1) % 2, (T - 1) // 2, True)
            dve.wait_ge(s_kv, done(T - 1))
            for h in range(CH):
                for i in range(P // D1):
                    q = slice(D1 * i, D1 * i + D1)
                    ins = dve.tensor_scalar(bd[q, h, q], acc[h][q, q], 1.0 / N, None, ALU.mult)
            ins.then_inc(s_block, 1)
            dve.wait_ge(s_r, 1)
            for h in range(CH):
                ins = dve.tensor_copy(r_[:, h, :], m.psum[h][:, 0:C])
            ins.then_inc(s_rheld, 1)
            dve.wait_ge(s_m, 1)
            for h in range(CH):
                ins = dve.tensor_copy(m.mixer[:, h, :], m.psum[2 + h][:, 0:C])
            wlink(ins)

        @block.tensor
        def _(pe):
            opened(pe, s_flipped, s_proj, s_kv)
            for h in range(CH):
                pe.matmul(acc[h][:, 0:P], m.zeros[:, 0:P], m.zeros[:, 0:P], start=True, stop=False)

            def flips(t, s):
                pe.wait_ge(s_normed, done(t))
                pe.wait_ge(s_row, freed(t))
                for h in range(CH):
                    ins = pe.transpose(flip[s][:, h * P:h * P + P], xs[s][:, h * P:h * P + P], m.ident[:, :])
                ins.then_inc(s_flipped, 1)

            def project(t, s):
                pe.wait_ge(s_row, done(t))
                pe.wait_ge(s_centred, freed(t))
                pe.wait_ge(s_xt, freed(t))
                for h in range(CH):
                    pe.matmul(kvp[s][:, :], xt[s][:, h, :], w[:, h, 0:2 * C], start=h == 0, stop=h == CH - 1)
                for h in range(CH):
                    ins = pe.matmul(grp[s][:, 0:GROW], xt[s][:, h, :], w[:, h, 2 * C:2 * C + GROW], start=h == 0, stop=h == CH - 1)
                ins.then_inc(s_proj, 1)

            def products(t, s, last):
                pe.wait_ge(s_gain, done(t))
                for h in range(CH):
                    v = C + h * P
                    ins = pe.matmul(acc[h][:, 0:P], kv[s][:, v:v + P], kv[s][:, h * P:h * P + P], start=False, stop=last)
                ins.then_inc(s_kv, 1)

            flips(0, 0)
            flips(1, 1)
            pe.wait_ge(s_w, 16 * NW)
            pe.wait_ge(s_fold, 1)
            project(0, 0)

            def step(t, s, k, last):
                project(t + 1, 1 - s)
                if not last:
                    flips(t + 2, s)
                if not isinstance(t, int) or t > 0:
                    products(t - 1, 1 - s, False)
            tiles(pe, step, T - 1, peel=True)
            products(T - 2, (T - 2) % 2, False)
            products(T - 1, (T - 1) % 2, True)
            pe.wait_ge(s_block, 1)
            for h in range(CH):
                ins = pe.matmul(m.psum[h][:, 0:C], bd[:, h, :], wo[:, h, :], start=True, stop=True)
            ins.then_inc(s_r, 1)
            pe.wait_ge(s_rheld, 1)
            for c in range(CH):
                for h in range(CH):
                    ins = pe.matmul(m.psum[2 + c][:, 0:C], wq[:, h, c * P:c * P + P], r_[:, h, :], start=h == 0, stop=h == CH - 1)
            ins.then_inc(s_m, 1)




def phase_graph1(nc, m, d):
    s_w, s_copied, s_y, s_out, s_idx, s_pcopy, s_issue, s_moved, s_chain, s_exp, s_exped = m.sems(
        "gr1", "w copied y out idx pcopy issue moved chain exp exped")
    GOT = 4
    s_got = m.sems("gr1", " ".join(f"got{s}" for s in range(GOT)))
    s_stats, s_var, s_std = m.sems("gr1", "stats var std")
    with ExitStack() as mem, nc.Block() as block:
        sb = lambda name, shape, dt=F32: mem.enter_context(nc.sbuf_tensor("gr1_" + name, shape, dt))
        bo = sb("bo", [1, C])
        idx = sb("idx", [P, T, 2], I32)
        ps = [sb(f"ps{s}", [P, 2], I32) for s in range(GOT)]
        got = [sb(f"got{s}", [P, 2, GROW]) for s in range(GOT)]
        source = sb("source", [P, T, H1])
        dest = sb("dest", [P, T, GROW])
        prod = sb("prod", [P, T, C])
        logit = sb("logit", [P, T, H1])
        tmp = sb("tmp", [P, T, H1])
        one = sb("one", [P, T])
        mean = sb("mean", [P, T, D1])
        xt = [sb(f"xt{s}", [P, CH, P]) for s in range(SLOTS)]
        stats = sb("stats", [P, T, 6])
        yp = m.psum[0:2]

        @block.sync
        def _(sp):
            sp.dma_start(bo[:, :], d.bo.rearrange("(a c) -> a c", a=1)).then_inc(s_w, 16)
            sp.wait_ge(s_idx, 1)
            sp.dma_start(idx[:, 0:T - 1, :], d.ends).then_inc(s_w, 16)
            sp.dma_start(idx[0:LAST, T - 1, :], d.ends_last).then_inc(s_w, 16)
            for e in range(X):
                sp.dma_start(m.wd[:, e, :, :], d.f1_wd[e, :, :].rearrange("(q p) o -> p q o", p=P)).then_inc(m.s_wd, 16)

        @block.gpsimd
        def _(pool):
            pool.memset(idx[:, :, :], 0).then_inc(s_idx, 1)
            pool.wait_ge(s_w, 48)

            def step(t, s, k, last):
                pool.wait_ge(s_moved, t + 1)
                pool.tensor_copy(ps[s][:, :].unsqueeze(1), row(idx, t)).then_inc(s_pcopy, 1)
                pool.wait_ge(s_pcopy, t + 1)
                pool.sem_inc(s_issue, 1)
                for u in range(2):
                    pool.indirect_dma_start(out=got[s][:, u, :], out_offset=None, in_=d.graph,
                                            in_offset=bass.IndirectOffsetOnAxis(ap=ps[s][:, u:u + 1], axis=0)).then_inc(s_got[s], 16)
            tiles(pool, step, slots=GOT)

        @block.scalar
        def _(act):
            opened(act, s_copied)
            act.sem_inc(s_moved, GOT)

            def step(t, s, k, last):
                act.wait_ge(s_y, freed(t))
                act.activation(xt[s % SLOTS][:, :, :], m.xnT[:, :, bass.ds(t * P, P)], ACT.Copy).then_inc(s_copied, 1)
                act.wait_ge(s_got[s], k * 32 + 32)
                act.activation(row(source, t), got[s][:, 0:1, C:C + H1], ACT.Copy)
                act.activation(row(dest, t), got[s][:, 1:2, :], ACT.Copy).then_inc(s_moved, 1)
            tiles(act, step, slots=GOT)
            act.wait_ge(s_exp, 1)
            act.activation(tmp[:, :, :], logit[:, :, :], ACT.Exp).then_inc(s_exped, 1)
            stats_scalar(act, m, s_var, s_std)

        @block.tensor
        def _(pe):
            opened(pe, s_y)
            pe.wait_ge(s_w, 48)

            def step(t, s, k, last):
                pe.wait_ge(s_copied, done(t))
                pe.wait_ge(s_out, freed(t))
                pe.matmul(yp[s][:, 0:C], m.ones[0:1, :], bo[:, :], start=True, stop=False)
                for h in range(CH):
                    ins = pe.matmul(yp[s][:, 0:C], xt[s][:, h, :], m.mixer[:, h, :], start=False, stop=h == CH - 1)
                ins.then_inc(s_y, 1)
            tiles(pe, step)

        @block.vector
        def _(dve):
            opened(dve, s_out)

            def step(t, s, k, last):
                dve.wait_ge(s_y, done(t))
                dve.tensor_tensor(row(m.x, t), yp[s][:, 0:C].unsqueeze(1), row(m.x, t), ALU.add).then_inc(s_out, 1)
            tiles(dve, step)
            dve.wait_ge(s_out, done(T - 1))
            link = Chain(dve, s_chain)
            dve.wait_ge(s_moved, T + GOT)
            link(dve.tensor_tensor(logit[:, :, :], source[:, :, :], dest[:, :, C + H1:GROW], ALU.add))
            link(dve.scalar_tensor_tensor(out=logit[:, :, :], in0=logit[:, :, :], scalar=0.01, in1=logit[:, :, :], op0=ALU.mult, op1=ALU.max))
            link(dve.tensor_reduce(one[:, :], logit[:, :, :], AX.X, ALU.max))
            dve.tensor_tensor(logit[:, :, :], logit[:, :, :], one[:, :].unsqueeze(2).to_broadcast([P, T, H1]), ALU.subtract).then_inc(s_exp, 1)
            dve.wait_ge(s_exped, 1)
            link(dve.tensor_reduce(one[:, :], tmp[:, :, :], AX.X, ALU.add))
            link(dve.reciprocal(one[:, :], one[:, :]))
            link(dve.tensor_tensor(logit[:, :, :], tmp[:, :, :], one[:, :].unsqueeze(2).to_broadcast([P, T, H1]), ALU.mult))
            link(dve.tensor_tensor(prod[:, :, :].rearrange("p t (h c) -> p t h c", h=H1),
                                   dest[:, :, 0:C].rearrange("p t (h c) -> p t h c", h=H1),
                                   logit[:, :, :].unsqueeze(3).to_broadcast([P, T, H1, D1]), ALU.mult))
            link(dve.tensor_reduce(mean[:, :, :], prod[:, :, :].rearrange("p t (h c) -> p t c h", h=H1), AX.X, ALU.add))
            x4 = m.x[:, :, :].rearrange("p t (h c) -> p t h c", h=H1)
            link(dve.tensor_tensor(x4, x4, mean[:, :, :].unsqueeze(2).to_broadcast([P, T, H1, D1]), ALU.add))
            with dve.Fori(0, T) as t:
                row_stats(dve, m.x, stats, t, s_stats)
            dve.wait_ge(s_stats, T)
            stats_vector(dve, link, m, stats[:, :, :], s_var, s_std)



def phase_route1(nc, m, d):
    s_copied, s_flipped, s_row, s_hid, s_gelu, s_gate, s_gated, s_wchain, s_diff, s_exp, s_counts, s_totals, \
        s_hot, s_placed, s_lchain, s_w = m.sems(
            "rt1", "copied flipped row hid gelu gate gated wchain diff exp counts totals hot placed lchain w")
    s_kept = m.sems("rt1", "kept0 kept1")
    with ExitStack() as mem, nc.Block() as block:
        sb = lambda name, shape, dt=F32: mem.enter_context(nc.sbuf_tensor("rt1_" + name, shape, dt))
        small6 = sb("small6", [P, 6, 32])
        wg = sb("wg", [P, HC, X])
        bg = sb("bg", [P, X])
        xs = [sb(f"xs{s}", [P, C]) for s in range(SLOTS)]
        xt = [sb(f"xt{s}", [P, CH, P]) for s in range(SLOTS)]
        hs = [sb(f"hs{s}", [P, HC, P]) for s in range(SLOTS)]
        score = sb("score", [P, T, X])
        equal = sb("equal", [P, T, X])
        best = sb("best", [P, T])
        key = sb("key", [P, T])
        onehot = sb("onehot", [P, max(T, FBLK1) * X])
        count = sb("count", [P, max(T, FBLK1) * X])
        pos = sb("pos", [P, T])
        work = sb("work", [P, 4, max(T, FBLK1)])
        whole = sb("whole", [P, 3, T], I32)
        hi_hot = sb("hi_hot", [P, T, FBLK1])
        lo_hot = [sb(f"lo_hot{s}", [P, PICK, P]) for s in range(SLOTS)]
        flip, gp, hp = m.psum[0:2], m.psum[2:4], [m.psum[4:6], m.psum[6:8]]

        @block.sync
        def _(sp):
            sp.dma_start(m.f1_w1[:, :, :], d.f1_w1.rearrange("(h p) o -> p h o", p=P)).then_inc(s_w, 16)
            sp.dma_start(m.f1_b1[:, :], d.f1_b1).then_inc(s_w, 16)
            sp.dma_start(wg[:, :, :], d.f1_wg.rearrange("(q p) e -> p q e", p=P)).then_inc(s_w, 16)
            sp.dma_start(bg[:, :], d.f1_bg.rearrange("(a c) -> a c", a=1).to_broadcast([P, X])).then_inc(s_w, 16)

            def keep(t, s, k, last):
                sp.wait_ge(s_copied, done(t))
                sp.dma_start(d.normed1[bass.ds(t * P, P), :], xs[s][:, :]).then_inc(s_kept[s], 16)
            tiles(sp, keep)
            for s in range(SLOTS):
                sp.wait_ge(s_kept[s], 16 * ((T - s + 1) // 2))

        @block.scalar
        def _(act):
            opened(act, s_gelu)
            act.wait_ge(s_w, 64)

            def step(t, s, k, last):
                act.wait_ge(s_hid, done(t))
                act.wait_ge(s_gate, freed(t))
                for q in range(HC):
                    ins = act.activation(hs[s][:, q, :], hp[s][q // 4][:, q % 4 * P:q % 4 * P + P], ACT.Gelu, bias=m.f1_b1[:, q:q + 1])
                ins.then_inc(s_gelu, 1)
            tiles(act, step)
            act.wait_ge(s_diff, 1)
            act.activation(score[:, :, :], equal[:, :, :], ACT.Exp).then_inc(s_exp, 1)

        @block.vector
        def _(dve):
            opened(dve, s_copied, s_row, s_gated)
            dve.wait_ge(s_w, 64)

            def norm(t, s, uses):
                dve.wait_ge(s_flipped, freed(t))
                landed(dve, s_kept[s], uses)
                normalise(dve, m, xs[s][:, :].unsqueeze(1), t).then_inc(s_copied, 1)

            def turn(t, s):
                dve.wait_ge(s_flipped, done(t))
                dve.wait_ge(s_hid, freed(t))
                dve.tensor_copy(xt[s][:, :, :], flip[s][:, 0:C].rearrange("p (h c) -> p h c", h=CH)).then_inc(s_row, 1)

            def step(t, s, k, last):
                if not last:
                    norm(t + 2, s, k + 1)
                    turn(t + 2, s)
                dve.wait_ge(s_gate, done(t))
                dve.tensor_tensor(row(score, t), gp[s][:, 0:X].unsqueeze(1), bg[:, :].unsqueeze(1), ALU.add).then_inc(s_gated, 1)
            norm(0, 0, 0)
            norm(1, 1, 0)
            turn(0, 0)
            turn(1, 1)
            tiles(dve, step, T - 1)
            step(T - 1, (T - 1) % 2, 0, True)
            dve.wait_ge(s_gated, done(T - 1))
            link = Chain(dve, s_lchain)
            wide = lambda a: a.unsqueeze(2).to_broadcast([P, T, X])
            link(dve.tensor_reduce(best[:, :], score[:, :, :], AX.X, ALU.max))
            dve.tensor_tensor(equal[:, :, :], score[:, :, :], wide(best[:, :]), ALU.subtract).then_inc(s_diff, 1)
            dve.wait_ge(s_exp, 1)
            link(dve.tensor_reduce(best[:, :], score[:, :, :], AX.X, ALU.add))
            link(dve.reciprocal(best[:, :], best[:, :]))
            link(dve.tensor_tensor(score[:, :, :], score[:, :, :], wide(best[:, :]), ALU.mult))
            first_best(dve, m, link, score, m.prob[:, :, 0], key[:, :], equal)
            sort_vector(dve, m, link, key[:, :], onehot, count, small6, m.psum[0], pos[:, :], s_counts, s_totals, X, T)
            invert_vector(dve, m, link, pos[:, :], m.row1[:, :], work, whole, hi_hot[:, :, :], lo_hot, m.psum[1],
                          T, FBLK1, s_hot, s_placed)
            sort_owner(dve, m, link, small6[:, 5, :], count[:, 0:FBLK1], m.fown[:, 0:FBLK1], X, FBLK1)

        @block.tensor
        def _(pe):
            opened(pe, s_flipped, s_hid, s_gate)
            pe.wait_ge(s_w, 64)

            def flips(t, s):
                pe.wait_ge(s_copied, done(t))
                pe.wait_ge(s_row, freed(t))
                for h in range(CH):
                    ins = pe.transpose(flip[s][:, h * P:h * P + P], xs[s][:, h * P:h * P + P], m.ident[:, :])
                ins.then_inc(s_flipped, 1)

            def hidden(t, s):
                pe.wait_ge(s_row, done(t))
                pe.wait_ge(s_gelu, freed(t))
                hidden_turned(pe, hp[s], m.f1_w1, xt[s]).then_inc(s_hid, 1)

            def gates(t, s):
                pe.wait_ge(s_gelu, done(t))
                pe.wait_ge(s_gated, freed(t))
                for q in range(HC):
                    ins = pe.matmul(gp[s][:, 0:X], hs[s][:, q, :], wg[:, q, :], start=q == 0, stop=q == HC - 1)
                ins.then_inc(s_gate, 1)

            flips(0, 0)
            hidden(0, 0)
            flips(1, 1)

            def step(t, s, k, last):
                hidden(t + 1, 1 - s)
                if not last:
                    flips(t + 2, s)
                gates(t, s)
            tiles(pe, step, T - 1)
            gates(T - 1, (T - 1) % 2)
            sort_tensor(pe, m, small6, m.psum[0], s_counts, s_totals, X)
            invert_tensor(pe, m, hi_hot, lo_hot, m.psum[1], T, FBLK1, s_hot, s_placed)



class Tensors:
    pass


def build(nc, d):
    dram = lambda name, rows, width: nc.dram_tensor(name, (rows, width), F32, kind="Internal").ap()
    d.support = dram("support", T * P, C)
    d.rec = dram("records", P * EBLK, 4)
    d.normed0, d.results0 = dram("normed0", T * P, C), dram("results0", 2 * T * P, C)
    d.normed1, d.results1 = dram("normed1", T * P, C), dram("results1", T * P, C)
    d.graph = dram("graph", T * P, GROW)
    with ExitStack() as whole:
        m = Machine(nc, whole)
        m.x = m.sb("x", [P, T, C])
        m.ident = m.sb("ident", [P, P])
        m.earlier = m.sb("earlier", [P, P])
        m.ones = m.sb("ones", [P, P])
        m.zeros = m.sb("zeros", [P, C])
        m.iota = m.sb("iota", [P, EBLK])
        m.lastmask = m.sb("lastmask", [P, 1])
        m.small_int = m.sb("small_int", [P, 32], I32)
        m.fown = m.sb("fown", [P, FBLK0], I32)
        m.prob = m.sb("prob", [P, T, 2])
        m.mean = m.sb("mean", [P, T])
        m.rstd = m.sb("rstd", [P, T])
        m.scratch = m.sb("scratch", [P, 4, T])
        m.stats = m.sb("stats", [P, T, 6])
        m.row1 = m.sb("row1", [P, T])
        m.row2 = m.sb("row2", [P, T, 2])
        m.token = m.sb("token", [P, FBLK0], I32)
        m.dest = m.sb("dest", [P, FBLK0], I32)
        with m.scope():
            m.w1 = m.sb("ffn0_w1", [P, X, CH, HID])
            m.s_w1, m.s_w2 = m.sems("ffn0", "w1 w2")
            with m.scope():
                m.rec = m.sb("rec", [P, ECOLS, 4])
                m.epos = m.sb("epos", [P, ECOLS], I32)
                m.eowner = m.sb("eowner", [P, EBLK], I32)
                m.eend = m.sb("eend", [P, T])
                m.buf_rec = [m.sb(f"buf_rec{h}", [P, EBUF * 4]) for h in range(2)]
                m.buf_pos = [m.sb(f"buf_pos{h}", [P, EBUF], I32) for h in range(2)]
                m.s_copied, m.s_issue = m.sems("edges", "copied issue")
                m.s_sent = m.sems("edges", "sent0 sent1")
                phase_start(nc, m, d)
                m.mix = m.sb("mix", [P, T, C])
                with m.scope():
                    m.xn = m.sb("xn", [P, T, C])
                    m.xnT = m.sb("xnT", [P, CH, T * P])
                    m.bd = m.sb("bd", [P, CH, KVW])
                    phase_support_kv(nc, m, d, (0, 144))
                    phase_attend(nc, m, d, (144, 240))
                phase_mlp(nc, m, d, (240, ECOLS))
                phase_aggregate(nc, m, d)
            w2 = m.sb("ffn0_w2", [P, X, HC, C])
            phase_route0(nc, m, d, w2)
            phase_experts(nc, m, "ex0", FBLK0, d.normed0, d.results0, 2, ACT.Relu, w2, d.f0_b2, m.s_w2, d.f0_b1)
        phase_combine(nc, m, "cmb0", d.results0, 2, True)
        m.recycle()
        m.f1_w1 = m.sb("f1_w1", [P, CH, HID])
        m.f1_b1 = m.sb("f1_b1", [P, HC])
        m.wd = m.sb("f1_wd", [P, X, HC, C])
        m.s_wd = m.sem("f1_wd")
        with m.scope():
            m.xnT = m.sb("xnT1", [P, CH, T * P])
            m.mixer = m.sb("mixer", [P, CH, C])
            phase_project1(nc, m, d)
            phase_graph1(nc, m, d)
        phase_route1(nc, m, d)
        phase_experts(nc, m, "ex1", FBLK1, d.normed1, d.results1, 1, ACT.Gelu, m.wd, d.f1_bd, m.s_wd)
        phase_combine(nc, m, "cmb1", d.results1, 1, False)
        s_out = m.sem("out")
        with nc.Block() as block:
            @block.sync
            def _(sp):
                full = (T - 1) * P
                sp.dma_start(d.out[0:full, :].rearrange("(t p) c -> p t c", p=P), m.x[:, 0:T - 1, :]).then_inc(s_out, 16)
                sp.dma_start(d.out[full:N, :], m.x[0:LAST, T - 1, :]).then_inc(s_out, 16)
                sp.wait_ge(s_out, 32)


def kernel(x, src, dst, edge_weight, L0_gnn_A, L0_gnn_B, L0_gnn_bn_weight, L0_gnn_bn_bias, L0_mix_Wqkv, L0_mix_ln1_g,
           L0_mix_ln1_b, L0_mix_W1, L0_mix_b1, L0_mix_W2, L0_mix_b2, L0_mix_ln2_g, L0_mix_ln2_b, L0_ffn_Wg, L0_ffn_bg,
           L0_ffn_W1, L0_ffn_b1, L0_ffn_W2, L0_ffn_b2, L1_gnn_weight, L1_gnn_attn_l, L1_gnn_attn_r, L1_mix_wq,
           L1_mix_wk, L1_mix_wv, L1_mix_wo, L1_mix_bo, L1_mix_ln_k_g, L1_mix_ln_k_b, L1_mix_ln_v_g, L1_mix_ln_v_b,
           L1_ffn_W1, L1_ffn_b1, L1_ffn_Wg, L1_ffn_bg, L1_ffn_Wd, L1_ffn_bd):
    import numpy as np
    from concourse import bacc
    from concourse.bass_utils import run_bass_kernel_spmd

    laid = {
        "ends": np.transpose(np.reshape(np.stack([src[:N], dst[:N]], -1)[:(T - 1) * P], (T - 1, P, 2)), (1, 0, 2)),
        "ends_last": np.stack([src[(T - 1) * P:N], dst[(T - 1) * P:N]], -1),
        "x": x, "src": src, "dst": dst, "edge_weight": edge_weight,
        "A": L0_gnn_A, "B": L0_gnn_B, "bn_w": L0_gnn_bn_weight, "bn_b": L0_gnn_bn_bias,
        "wqkv": np.transpose(L0_mix_Wqkv), "ln1_g": L0_mix_ln1_g, "ln1_b": L0_mix_ln1_b,
        "mw1": np.transpose(L0_mix_W1), "mb1": np.transpose(np.reshape(L0_mix_b1, (CH, P))), "mw2": np.transpose(L0_mix_W2), "mb2": L0_mix_b2,
        "ln2_g": L0_mix_ln2_g, "ln2_b": L0_mix_ln2_b,
        "f0_wg": np.transpose(L0_ffn_Wg), "f0_bg": L0_ffn_bg,
        "f0_w1": np.transpose(L0_ffn_W1, (0, 2, 1)), "f0_b1": np.transpose(np.reshape(L0_ffn_b1, (X, HC, P)), (2, 0, 1)),
        "f0_w2": np.transpose(L0_ffn_W2, (0, 2, 1)), "f0_b2": L0_ffn_b2,
        "g_w": L1_gnn_weight, "g_al": L1_gnn_attn_l, "g_ar": L1_gnn_attn_r,
        "wq": L1_mix_wq, "wk": np.transpose(L1_mix_wk), "wv": np.transpose(L1_mix_wv), "wo": np.transpose(L1_mix_wo),
        "bo": L1_mix_bo, "k_g": L1_mix_ln_k_g, "k_b": L1_mix_ln_k_b, "v_g": L1_mix_ln_v_g, "v_b": L1_mix_ln_v_b,
        "f1_w1": L1_ffn_W1, "f1_b1": np.transpose(np.reshape(L1_ffn_b1, (HC, P))), "f1_wg": L1_ffn_Wg, "f1_bg": L1_ffn_bg, "f1_wd": L1_ffn_Wd,
        "f1_bd": L1_ffn_bd,
    }
    nc = bacc.Bacc("TRN2", target_bir_lowering=False, num_devices=1)
    d = Tensors()
    arrays = {}
    for name, a in laid.items():
        arrays["in_" + name] = a = np.ascontiguousarray(a)
        ap = nc.dram_tensor("in_" + name, a.shape, mybir.dt.from_np(a.dtype), kind="ExternalInput").ap()
        d.__dict__[name] = ap
    d.out = nc.dram_tensor("out", (N, C), F32, kind="ExternalOutput").ap()
    build(nc, d)
    r = run_bass_kernel_spmd(nc, [arrays], core_ids=[0])
    return r.results[0]["out"]
```

```python
import concourse.bass as bass
from concourse import mybir
from contextlib import ExitStack, contextmanager

F32 = mybir.dt.float32
I32 = mybir.dt.int32
BF16 = mybir.dt.bfloat16
ALU = mybir.AluOpType
ACT = mybir.ActivationFunctionType
AX = mybir.AxisListType

P = 128
N = 3125
C = 256
CH = C // P
T = -(-N // P)
LAST = N - (T - 1) * P
E = 50000
EBUF = 14
ESTEP = 2 * EBUF
ECOLS = -(-E // (P * ESTEP)) * ESTEP
EROWS = E // ECOLS
ELAST = E - EROWS * ECOLS
GB = 16
PICK = 5
X = 8
HID = 1024
HC = HID // P
H0, D0 = 8, 32
H1, D1 = 4, 64
KVW = P + 4
GROW = C + 2 * H1
SLOTS = 2


def blocks_for(rows, buckets):
    return (rows + buckets * (P - 1)) // P


EBLK = -(-blocks_for(P * ECOLS, T) // GB) * GB
FBLK0 = blocks_for(2 * T * P, X)
FBLK1 = blocks_for(T * P, X)
FAR = 1 << 20


def done(t):
    return t + 1 + SLOTS


def freed(t):
    return t + 1


def opened(eng, *sems):
    for s in sems:
        eng.sem_inc(s, SLOTS)


def tiles(eng, step, n=T, peel=False, slots=SLOTS):
    loops = (n - 1) // slots
    if peel:
        for s in range(slots):
            step(s, s, 0, False)
    with eng.Fori(int(peel), loops) as k:
        for s in range(slots):
            step(k * slots + s, s, k, False)
    for t in range(loops * slots, n):
        step(t, t % slots, t // slots, t == n - 1)


def each_tile(eng, step, group=5):
    with eng.Fori(0, T // group) as k:
        for u in range(group):
            step(k * group + u)


class Chain:

    def __init__(self, eng, sem, start=0):
        self.eng, self.sem, self.value = eng, sem, start

    def __call__(self, ins):
        self.value = self.value + 1
        ins.then_inc(self.sem, 1)
        self.eng.wait_ge(self.sem, self.value)


def landed(eng, sem, k, dmas=1):
    if not isinstance(k, int) or k > 0:
        eng.wait_ge(sem, k * (16 * dmas))


def row(ap, t):
    return ap[:, bass.ds(t, 1)] if not isinstance(t, int) else ap[:, t:t + 1]


class Machine:

    def __init__(self, nc, ctx):
        self.nc, self.ctx, self.used = nc, ctx, []
        self.psum = [ctx.enter_context(nc.psum_tensor(f"bank{i}", [P, 512], F32)) for i in range(8)]

    def sb(self, name, shape, dt=F32):
        return self.ctx.enter_context(self.nc.sbuf_tensor(name, shape, dt))

    def sem(self, name):
        self.used.append(self.nc.alloc_semaphore(name))
        return self.used[-1]

    @contextmanager
    def scope(self):
        outer = self.ctx
        with ExitStack() as self.ctx:
            yield
        self.ctx = outer

    def recycle(self):
        self.nc.clear_and_free_semaphores(self.used)
        self.nc.all_engine_barrier()
        self.used = []

    def sems(self, phase, names):
        return [self.sem(f"{phase}_{n}") for n in names.split()]



def row_stats(dve, x, stats, t, s_stats):
    return dve.bn_stats(row(stats, t), row(x, t)).then_inc(s_stats, 1)


def stats_vector(dve, link, m, stats, s_var, s_std):
    even, odd = stats[:, :, 0:3], stats[:, :, 3:6]
    dif, dev, var = (m.scratch[:, i, :] for i in range(3))
    dve.tensor_tensor(dif, even[:, :, 1], odd[:, :, 1], ALU.subtract)
    dve.tensor_tensor(dev, even[:, :, 2], odd[:, :, 2], ALU.add)
    link(dve.tensor_tensor(m.mean[:, :], even[:, :, 1], odd[:, :, 1], ALU.add))
    dve.tensor_scalar(m.mean[:, :], m.mean[:, :], 0.5, None, ALU.mult)
    dve.scalar_tensor_tensor(out=var, in0=dif, scalar=0.25, in1=dif, op0=ALU.mult, op1=ALU.mult)
    link(dve.tensor_scalar(dev, dev, 1.0 / C, 1e-5, ALU.mult, ALU.add))
    dve.tensor_tensor(var, var, dev, ALU.add).then_inc(s_var, 1)
    dve.wait_ge(s_std, 1)
    link(dve.reciprocal(m.rstd[:, :], m.scratch[:, 3, :]))


def stats_scalar(act, m, s_var, s_std):
    act.wait_ge(s_var, 1)
    act.activation(m.scratch[:, 3, :], m.scratch[:, 2, :], ACT.Sqrt).then_inc(s_std, 1)


def normalise(dve, m, out, t, x=None):
    return dve.tensor_scalar(out, row(m.x if x is None else x, t), m.mean[:, bass.ds(t, 1)], m.rstd[:, bass.ds(t, 1)],
                             ALU.subtract, ALU.mult)



def sort_vector(dve, m, link, key, onehot, count, small, psum, pos, s_counts, s_totals, buckets, cols):
    oh = onehot[:, 0:buckets * cols].rearrange("p (b c) -> p b c", b=buckets)
    cn = count[:, 0:buckets * cols].rearrange("p (b c) -> p b c", b=buckets)
    link(dve.tensor_tensor(oh, key.unsqueeze(1).to_broadcast([P, buckets, cols]),
                           m.iota[:, 0:buckets].unsqueeze(2).to_broadcast([P, buckets, cols]), ALU.is_equal))
    link(dve.tensor_tensor_scan(count[:, 0:buckets * cols], onehot[:, 0:buckets * cols],
                                onehot[:, 0:buckets * cols], 0.0, ALU.add, ALU.max))
    own, before, base, full, blk, end = (small[:, i, 0:buckets] for i in range(6))
    link(dve.memset(before, 0.0))
    link(dve.tensor_copy(small[:, 1, 1:buckets], cn[:, 0:buckets - 1, cols - 1]))
    dve.tensor_tensor(own, cn[:, :, cols - 1], before, ALU.subtract).then_inc(s_counts, 1)
    dve.wait_ge(s_totals, 1)
    link(dve.tensor_scalar(full, psum[:, 64:64 + buckets], float(P - 1), None, ALU.add))
    whole = m.small_int[:, 0:buckets]
    link(dve.tensor_copy(whole, full))
    link(dve.tensor_scalar(whole, whole, 7, None, ALU.arith_shift_right))
    link(dve.tensor_copy(blk, whole))
    link(dve.tensor_tensor_scan(end, blk, blk, 0.0, ALU.add, ALU.max))
    link(dve.tensor_tensor(base, end, blk, ALU.subtract))
    link(dve.tensor_scalar(base, base, float(P), -1.0, ALU.mult, ALU.add))
    link(dve.tensor_tensor(base, base, before, ALU.subtract))
    link(dve.tensor_tensor(base, base, psum[:, 0:buckets], ALU.add))
    for b in range(buckets):
        ins = dve.scalar_tensor_tensor(out=cn[:, b, :], in0=cn[:, b, :], scalar=base[:, b:b + 1],
                                       in1=oh[:, b, :], op0=ALU.add, op1=ALU.mult)
    link(ins)
    link(dve.tensor_reduce(pos, count[:, 0:buckets * cols].rearrange("p (b c) -> p c b", b=buckets),
                           AX.X, ALU.add))


def sort_owner(dve, m, link, end, tmp, owner, buckets, nblk):
    link(dve.memset(tmp, 0.0))
    for b in range(buckets - 1):
        link(dve.scalar_tensor_tensor(out=tmp, in0=m.iota[:, 0:nblk], scalar=end[:, b:b + 1], in1=tmp,
                                      op0=ALU.is_ge, op1=ALU.add))
    link(dve.tensor_copy(owner, tmp))


def invert_vector(dve, m, link, pos, value, work, whole, hi_hot, lo_hot, psum, cols, nblk, s_hot, s_placed):
    lo, hi, ids, none = (work[:, i, :] for i in range(4))
    lo, hi, ids, none = lo[:, 0:cols], hi[:, 0:cols], ids[:, 0:nblk], none[:, 0:nblk]
    link(dve.tensor_copy(whole[:, 0, :], pos))
    dve.tensor_scalar(whole[:, 1, :], whole[:, 0, :], P - 1, None, ALU.bitwise_and)
    link(dve.tensor_scalar(whole[:, 2, :], whole[:, 0, :], 7, None, ALU.arith_shift_right))
    dve.tensor_copy(lo, whole[:, 1, :])
    link(dve.tensor_copy(hi, whole[:, 2, :]))
    high, low = hi_hot[:, :, 0:nblk], hi_hot[:, :, nblk:2 * nblk]
    link(dve.tensor_tensor(low, m.iota[:, 0:nblk].unsqueeze(1).to_broadcast([P, cols, nblk]),
                           hi.unsqueeze(2).to_broadcast([P, cols, nblk]), ALU.is_equal))
    link(dve.tensor_tensor(high, low, value.unsqueeze(2).to_broadcast([P, cols, nblk]), ALU.mult))
    link(dve.tensor_scalar(low, low, m.number[:, 0:1], None, ALU.mult))
    opened(dve, s_hot)

    def step(g, s, k, last):
        dve.wait_ge(s_placed, freed(g))
        dve.tensor_tensor(lo_hot[s][:, :, :], m.iota[:, 0:P].unsqueeze(1).to_broadcast([P, PICK, P]),
                          lo[:, bass.ds(g * PICK, PICK)].unsqueeze(2).to_broadcast([P, PICK, P]), ALU.is_equal).then_inc(s_hot, 1)
    tiles(dve, step, cols // PICK)
    dve.wait_ge(s_placed, done(cols // PICK - 1))
    link(dve.tensor_scalar(ids, psum[:, 0:nblk], float(P), -1.0, ALU.mult, ALU.add))
    link(dve.tensor_tensor(ids, ids, psum[:, nblk:2 * nblk], ALU.add))
    link(dve.tensor_scalar(none, ids, 0.0, float(FAR), ALU.is_lt, ALU.mult))
    link(dve.tensor_tensor(m.dest[:, 0:nblk], ids, none, ALU.add))
    link(dve.tensor_scalar(none, ids, float(T * P), -float(T * P), ALU.is_ge, ALU.mult))
    link(dve.tensor_tensor(ids, ids, none, ALU.add))
    link(dve.tensor_scalar(m.token[:, 0:nblk], ids, 0.0, None, ALU.max))


def invert_tensor(pe, m, hi_hot, lo_hot, psum, cols, nblk, s_hot, s_placed):
    opened(pe, s_placed)
    pe.matmul(psum[:, 0:2 * nblk], m.zeros[:, 0:P], m.zeros[:, 0:2 * nblk], start=True, stop=False)

    def step(g, s, k, last):
        pe.wait_ge(s_hot, done(g))
        for u in range(PICK):
            ins = pe.matmul(psum[:, 0:2 * nblk], lo_hot[s][:, u, :], hi_hot[:, bass.ds(g * PICK + u, 1), :],
                            start=False, stop=last and u == PICK - 1)
        ins.then_inc(s_placed, 1)
    tiles(pe, step, cols // PICK)


def sort_tensor(pe, m, small, psum, s_counts, s_totals, buckets):
    pe.wait_ge(s_counts, 1)
    pe.matmul(psum[:, 0:buckets], m.earlier[:, :], small[:, 0, 0:buckets], start=True, stop=True)
    pe.matmul(psum[:, 64:64 + buckets], m.ones[:, :], small[:, 0, 0:buckets], start=True, stop=True)\
      .then_inc(s_totals, 1)



def phase_start(nc, m, d):
    s_load, s_const, s_pad = m.sems("start", "load const pad")
    s_edge, s_eload, s_edges, s_counts, s_totals, s_rec, s_wchain = m.sems("start", "edge eload edges counts totals rec wchain")
    with ExitStack() as mem, nc.Block() as block:
        sb = lambda name, shape, dt=F32: mem.enter_context(nc.sbuf_tensor(name, shape, dt))
        onehot = sb("st_onehot", [P, ECOLS * T])
        count = sb("st_count", [P, ECOLS * T])
        small = sb("st_small", [P, 6, 32])
        src_i = sb("st_src", [P, ECOLS], I32)
        dst_i = sb("st_dst", [P, ECOLS], I32)
        w = sb("st_w", [P, ECOLS])
        key = sb("st_key", [P, ECOLS])
        pos = sb("st_pos", [P, ECOLS])
        pos_i = sb("st_pos_i", [P, ECOLS], I32)
        lo_i = sb("st_lo_i", [P, ECOLS], I32)
        zrec = sb("st_zrec", [P, EBLK * 4])

        @block.gpsimd
        def _(pool):
            c = Chain(pool, s_const)
            c(pool.memset(m.ones[:, :], 1.0))
            c(pool.memset(m.zeros[:, :], 0.0))
            c(pool.iota(m.iota[:, :], [[1, EBLK]], base=0, channel_multiplier=0, allow_small_or_imprecise_dtypes=True))
            c(pool.affine_select(out=m.ident[:, :], in_=m.zeros[:, 0:P], compare_op=ALU.not_equal, fill=1.0,
                                 base=0, pattern=[[-1, P]], channel_multiplier=1))
            c(pool.affine_select(out=m.earlier[:, :], in_=m.zeros[:, 0:P], compare_op=ALU.is_ge, fill=1.0,
                                 base=0, pattern=[[-1, P]], channel_multiplier=1))
            c(pool.affine_select(out=m.lastmask[:, :], in_=m.ones[:, 0:1], compare_op=ALU.is_ge, fill=0.0,
                                 base=LAST - 1, pattern=[[0, 1]], channel_multiplier=-1))
            c(pool.iota(m.tile2[:, :, :], [[1, T], [T, 2]], base=0, channel_multiplier=0, allow_small_or_imprecise_dtypes=True))
            c(pool.iota(m.number[:, :], [[0, 1]], base=1, channel_multiplier=1, allow_small_or_imprecise_dtypes=True))
            pool.memset(zrec[:, :], 0.0).then_inc(s_rec, 1)

        @block.sync
        def _(sp):
            sp.wait_ge(s_edge, 4)
            for tile, edges in ((src_i, d.src), (dst_i, d.dst), (w, d.edge_weight)):
                full = EROWS * ECOLS
                sp.dma_start(tile[0:EROWS, :], edges[0:full].rearrange("(p c) -> p c", p=EROWS)).then_inc(s_edges, 16)
                sp.dma_start(tile[EROWS:EROWS + 1, 0:ELAST], edges[full:E].rearrange("(p c) -> p c", p=1)).then_inc(s_edges, 16)
            sp.wait_ge(s_rec, 1)
            sp.dma_start(d.rec.rearrange("(p j) r -> p (j r)", p=P), zrec[:, :]).then_inc(s_eload, 16)
            sp.wait_ge(s_eload, 16)
            sp.wait_ge(s_load, 32)

        @block.scalar
        def _(act):
            act.wait_ge(s_pad, 1)
            act.wait_ge(s_edges, 96)
            full = (T - 1) * P
            act.dma_start(m.x[:, 0:T - 1, :], d.x[0:full, :].rearrange("(t p) c -> p t c", p=P)).then_inc(s_load, 16)
            act.dma_start(m.x[0:LAST, T - 1, :], d.x[full:N, :]).then_inc(s_load, 16)

        @block.vector
        def _(dve):
            dve.memset(src_i[:, :], 0).then_inc(s_edge, 1)
            dve.memset(dst_i[:, :], 0).then_inc(s_edge, 1)
            dve.memset(w[:, :], 0.0).then_inc(s_edge, 1)
            dve.memset(m.rec[:, :, :], 0.0).then_inc(s_edge, 1)
            dve.memset(m.x[:, T - 1, :], 0.0).then_inc(s_pad, 1)
            dve.wait_ge(s_const, 8)
            dve.wait_ge(s_edges, 96)
            link = Chain(dve, s_wchain)
            link(dve.tensor_scalar(lo_i[:, :], src_i[:, :], 7, None, ALU.arith_shift_right))
            link(dve.tensor_copy(key[:, :], lo_i[:, :]))
            link(dve.tensor_scalar(lo_i[:, :], src_i[:, :], P - 1, None, ALU.bitwise_and))
            dve.tensor_copy(m.rec[:, :, 0], lo_i[:, :])
            dve.tensor_copy(m.rec[:, :, 1], w[:, :])
            link(dve.tensor_copy(m.rec.bitcast(I32)[:, :, 2], dst_i[:, :]))
            sort_vector(dve, m, link, key[:, :], onehot, count, small, m.psum[0], pos[:, :], s_counts, s_totals, T, ECOLS)
            link(dve.tensor_copy(m.eend[:, :], small[:, 5, 0:T]))
            link(dve.tensor_copy(pos_i[:, :], pos[:, :]))
            link(dve.tensor_scalar(lo_i[:, :], pos_i[:, :], P - 1, None, ALU.bitwise_and))
            link(dve.tensor_scalar(pos_i[:, :], pos_i[:, :], 7, None, ALU.arith_shift_right))
            link(dve.tensor_scalar(pos[:, :], lo_i[:, :], float(EBLK), None, ALU.mult))
            link(dve.tensor_tensor(m.epos[:, :], pos[:, :], pos_i[:, :], ALU.add))

        @block.tensor
        def _(pe):
            pe.wait_ge(s_const, 8)
            sort_tensor(pe, m, small, m.psum[0], s_counts, s_totals, T)


def scatter_edges(pool, m, d, first, last):
    s_copied, s_sent, s_issue = m.s_copied, m.s_sent, m.s_issue

    def both(k):
        for h in range(2):
            col = k * ESTEP + h * EBUF
            landed(pool, s_sent[h], k, EBUF)
            pool.tensor_copy(m.buf_rec[h][:, :], m.rec[:, bass.ds(col, EBUF), :].rearrange("p c r -> p (c r)"))
            pool.tensor_copy(m.buf_pos[h][:, :], m.epos[:, bass.ds(col, EBUF)]).then_inc(s_copied, 1)
            pool.wait_ge(s_copied, k * 2 + h + 1)
            pool.sem_inc(s_issue, 1)
            for u in range(EBUF):
                pool.indirect_dma_start(out=d.rec, out_offset=bass.IndirectOffsetOnAxis(ap=m.buf_pos[h][:, u:u + 1], axis=0),
                                        in_=m.buf_rec[h][:, 4 * u:4 * u + 4], in_offset=None).then_inc(s_sent[h], 16)

    if first == 0:
        both(0)
    with pool.Fori(max(first // ESTEP, 1), last // ESTEP) as k:
        both(k)
    for h in range(2):
        pool.wait_ge(s_sent[h], last // ESTEP * 16 * EBUF)


def load_experts(sp, m, d, first, last):
    for e in range(first, last):
        sp.dma_start(m.w1[:, e, :, :], d.f0_w1[e, :, :].rearrange("(h p) o -> p h o", p=P)).then_inc(m.s_w1, 16)



QUATERNION = [[(0, 1), (1, 1), (2, 1), (3, 1)],
              [(1, -1), (0, 1), (3, 1), (2, -1)],
              [(2, -1), (3, -1), (0, 1), (1, 1)],
              [(3, -1), (2, 1), (1, -1), (0, 1)]]


def phase_support_kv(nc, m, d, share):
    (s_w, s_built, s_chain, s_copied, s_flipped, s_row, s_rowall, s_proj, s_kmin, s_kexp, s_k, s_v, s_kv, s_sup,
     s_kept, s_stats, s_var, s_std) = m.sems(
        "skv", "w built chain copied flipped row rowall proj kmin kexp k v kv sup kept stats var std")
    s_store = m.sems("skv", "store0 store1")
    with ExitStack() as mem, nc.Block() as block:
        sb = lambda name, shape, dt=F32: mem.enter_context(nc.sbuf_tensor("skv_" + name, shape, dt))
        w = sb("w", [P, CH, 3 * C])
        ab = sb("ab", [P, 2, P])
        g = w[:, :, 2 * C:3 * C]
        stats = sb("stats", [P, T, 6])
        xs = [sb(f"xs{s}", [P, C]) for s in range(SLOTS)]
        xt = [sb(f"xt{s}", [P, CH, P]) for s in range(SLOTS)]
        sup = [sb(f"sup{s}", [P, C]) for s in range(SLOTS)]
        kmin = [sb(f"kmin{s}", [P, C]) for s in range(SLOTS)]
        kexp = [sb(f"kexp{s}", [P, C]) for s in range(SLOTS)]
        ks = [sb(f"ks{s}", [P, C]) for s in range(SLOTS)]
        vs = [sb(f"vs{s}", [P, CH, KVW]) for s in range(SLOTS)]
        flip, kp, vsp, kv = m.psum[0:2], m.psum[2:4], m.psum[4:6], m.psum[6:8]

        @block.sync
        def _(sp):
            sp.dma_start(w[:, :, 0:2 * C], d.wqkv[:, C:3 * C].rearrange("(h p) o -> p h o", p=P)).then_inc(s_w, 16)
            for b in range(4):
                sp.dma_start(ab[32 * b:32 * b + 32, 0, :], d.A).then_inc(s_w, 16)
                sp.dma_start(ab[32 * b:32 * b + 32, 1, :], d.B).then_inc(s_w, 16)
            load_experts(sp, m, d, 0, 3)

            def step(t, s, k, last):
                sp.wait_ge(s_sup, done(t))
                sp.dma_start(d.support[bass.ds(t * P, P), :], sup[s][:, :]).then_inc(s_store[s], 16)
            tiles(sp, step)
            for s in range(SLOTS):
                sp.wait_ge(s_store[s], 16 * ((T - s + 1) // 2))

        @block.gpsimd
        def _(pool):
            scatter_edges(pool, m, d, *share)

        @block.scalar
        def _(act):
            opened(act, s_kept, s_rowall, s_v, s_kexp, s_sup)
            stats_scalar(act, m, s_var, s_std)

            def keep(t, s):
                act.wait_ge(s_copied, done(t))
                act.activation(row(m.xn, t), xs[s][:, :].unsqueeze(1), ACT.Copy).then_inc(s_kept, 1)

            def step(t, s, k, last):
                if not last:
                    keep(t + 1, 1 - s)
                act.wait_ge(s_row, done(t))
                act.activation(m.xnT[:, :, bass.ds(t * P, P)], xt[s][:, :, :], ACT.Copy).then_inc(s_rowall, 1)
                act.wait_ge(s_kmin, done(t))
                act.activation(kexp[s][:, :], kmin[s][:, :], ACT.Exp).then_inc(s_kexp, 1)
                act.wait_ge(s_kv, freed(t))
                act.activation(vs[s][:, :, 0:P], vsp[s][:, 0:C].rearrange("p (h c) -> p h c", h=CH),
                               ACT.Copy).then_inc(s_v, 1)
                landed(act, s_store[s], k)
                act.activation(sup[s][:, :], vsp[s][:, C:2 * C], ACT.Copy).then_inc(s_sup, 1)

            keep(0, 0)
            tiles(act, step, peel=True)

        @block.vector
        def _(dve):
            link = Chain(dve, s_chain)
            opened(dve, s_copied, s_row, s_kmin, s_k)
            each_tile(dve, lambda t: row_stats(dve, m.x, stats, t, s_stats))
            dve.wait_ge(s_stats, T)
            stats_vector(dve, link, m, stats[:, :, :], s_var, s_std)

            def norm(t, s):
                dve.wait_ge(s_flipped, freed(t))
                dve.wait_ge(s_kept, freed(t))
                normalise(dve, m, xs[s][:, :].unsqueeze(1), t).then_inc(s_copied, 1)

            norm(0, 0)
            for s in range(SLOTS):
                link(dve.memset(vs[s][:, :, P:KVW], 1.0))
            link(dve.memset(g, 0.0))
            link(dve.memset(m.bd[:, :, :], 0.0))
            dve.wait_ge(s_w, 16 * 9)
            for b in range(4):
                for c, (part, sign) in enumerate(QUATERNION[b]):
                    q = slice(32 * b, 32 * b + 32)
                    out = slice(32 * c, 32 * c + 32)
                    src = slice(32 * part, 32 * part + 32)
                    dve.tensor_scalar(g[q, 0, out], ab[q, 0, src], float(sign), None, ALU.mult)
                    dve.tensor_scalar(g[q, 1, P + 32 * c:P + 32 * c + 32], ab[q, 0, src], float(sign), None, ALU.mult)
                    ins = dve.tensor_scalar(g[q, 0, P + 32 * c:P + 32 * c + 32], ab[q, 1, src], float(sign), None, ALU.mult)
            ins.then_inc(s_built, 1)

            def turn(t, s):
                dve.wait_ge(s_flipped, done(t))
                dve.wait_ge(s_proj, freed(t))
                dve.wait_ge(s_rowall, freed(t))
                dve.tensor_copy(xt[s][:, :, :], flip[s][:, 0:C].rearrange("p (h c) -> p h c", h=CH)).then_inc(s_row, 1)

            def step(t, s, k, last):
                if not last:
                    norm(t + 1, 1 - s)
                dve.wait_ge(s_proj, done(t))
                dve.wait_ge(s_kexp, freed(t))
                dve.tensor_scalar(kmin[s][:, :], kp[s][:, 0:C], 0.0, None, ALU.min).then_inc(s_kmin, 1)
                if not last:
                    turn(t + 1, 1 - s)
                dve.wait_ge(s_kexp, done(t))
                dve.wait_ge(s_kv, freed(t))
                if last:
                    link(dve.tensor_copy(vs[s][:, :, P:KVW], m.lastmask[:, 0:1].unsqueeze(1).to_broadcast([P, CH, 4])))
                dve.scalar_tensor_tensor(out=ks[s][:, :], in0=kp[s][:, 0:C], scalar=0.0, in1=kexp[s][:, :],
                                         op0=ALU.max, op1=ALU.add).then_inc(s_k, 1)

            turn(0, 0)
            tiles(dve, step)
            dve.wait_ge(s_kv, done(T - 1))
            for h in range(CH):
                for i in range(4):
                    q = slice(D0 * i, D0 * i + D0)
                    dve.tensor_copy(m.bd[q, h, q], kv[h][q, q])
                    ins = dve.tensor_copy(m.bd[q, h, P + i:P + i + 1], kv[h][q, P:P + 1])
            link(ins)

        @block.tensor
        def _(pe):
            opened(pe, s_flipped, s_proj, s_kv)
            for h in range(CH):
                pe.matmul(kv[h][:, 0:KVW], m.zeros[:, 0:P], m.zeros[:, 0:KVW], start=True, stop=False)

            def flips(t, s):
                pe.wait_ge(s_copied, done(t))
                pe.wait_ge(s_row, freed(t))
                for h in range(CH):
                    ins = pe.transpose(flip[s][:, h * P:h * P + P], xs[s][:, h * P:h * P + P], m.ident[:, :])
                ins.then_inc(s_flipped, 1)

            def step(t, s, k, last):
                pe.wait_ge(s_row, done(t))
                pe.wait_ge(s_k, freed(t))
                pe.wait_ge(s_v, freed(t))
                pe.wait_ge(s_sup, freed(t))
                for h in range(CH):
                    pe.matmul(kp[s][:, 0:C], xt[s][:, h, :], w[:, h, 0:C], start=h == 0, stop=h == CH - 1)
                for h in range(CH):
                    ins = pe.matmul(vsp[s][:, :], xt[s][:, h, :], w[:, h, C:3 * C], start=h == 0, stop=h == CH - 1)
                ins.then_inc(s_proj, 1)
                if not last:
                    flips(t + 1, 1 - s)
                pe.wait_ge(s_k, done(t))
                pe.wait_ge(s_v, done(t))
                for h in range(CH):
                    ins = pe.matmul(kv[h][:, 0:KVW], ks[s][:, h * P:h * P + P], vs[s][:, h, :],
                                    start=False, stop=last)
                ins.then_inc(s_kv, 1)

            flips(0, 0)
            pe.wait_ge(s_w, 16 * 9)
            pe.wait_ge(s_built, 1)
            tiles(pe, step)



def phase_attend(nc, m, d, share):
    s_w, s_q, s_qmin, s_qexp, s_qs, s_att, s_out, s_chain, s_owner = m.sems("att", "w q qmin qexp qs att out chain owner")
    with ExitStack() as mem, nc.Block() as block:
        sb = lambda name, shape, dt=F32: mem.enter_context(nc.sbuf_tensor("att_" + name, shape, dt))
        wq = sb("wq", [P, CH, C])
        owner = sb("owner", [P, EBLK])
        qmin = [sb(f"qmin{s}", [P, C]) for s in range(SLOTS)]
        qexp = [sb(f"qexp{s}", [P, C]) for s in range(SLOTS)]
        qs = [sb(f"qs{s}", [P, CH, P]) for s in range(SLOTS)]
        z = [sb(f"z{s}", [P, CH, 4]) for s in range(SLOTS)]
        part = [sb(f"part{s}", [P, C]) for s in range(SLOTS)]
        qp, ap = m.psum[0:2], m.psum[2:4]

        @block.sync
        def _(sp):
            sp.dma_start(wq[:, :, :], d.wqkv[:, 0:C].rearrange("(h p) o -> p h o", p=P)).then_inc(s_w, 16)
            load_experts(sp, m, d, 3, 6)

        @block.gpsimd
        def _(pool):
            scatter_edges(pool, m, d, *share)

        @block.scalar
        def _(act):
            opened(act, s_qexp)

            def step(t, s, k, last):
                act.wait_ge(s_qmin, done(t))
                act.wait_ge(s_qs, freed(t))
                act.activation(qexp[s][:, :], qmin[s][:, :], ACT.Exp).then_inc(s_qexp, 1)
            tiles(act, step)

        @block.vector
        def _(dve):
            opened(dve, s_qmin, s_qs, s_out)
            sort_owner(dve, m, Chain(dve, s_owner), m.eend[:, :], owner[:, :], m.eowner[:, :], T, EBLK)

            def low(t, s):
                dve.wait_ge(s_q, done(t))
                dve.wait_ge(s_qexp, freed(t))
                dve.tensor_scalar(qmin[s][:, :], qp[s][:, 0:C], 0.0, None, ALU.min).then_inc(s_qmin, 1)

            def step(t, s, k, last):
                dve.wait_ge(s_qexp, done(t))
                dve.wait_ge(s_att, freed(t))
                dve.scalar_tensor_tensor(out=qs[s][:, :, :].rearrange("p h c -> p (h c)"), in0=qp[s][:, 0:C],
                                         scalar=0.0, in1=qexp[s][:, :], op0=ALU.max, op1=ALU.add).then_inc(s_qs, 1)
                if not last:
                    low(t + 1, 1 - s)
                dve.wait_ge(s_att, done(t))
                link = Chain(dve, s_chain, t * 3)
                a = ap[s][:, 0:CH * KVW].rearrange("p (h c) -> p h c", h=CH)
                link(dve.tensor_scalar(z[s][:, :, :], a[:, :, P:KVW], 1e-6, None, ALU.add))
                link(dve.reciprocal(z[s][:, :, :], z[s][:, :, :]))
                for h in range(CH):
                    ins = dve.tensor_tensor(part[s][:, h * P:h * P + P].rearrange("p (i c) -> p i c", c=D0),
                                            a[:, h, 0:P].rearrange("p (i c) -> p i c", c=D0),
                                            z[s][:, h, :].unsqueeze(2).to_broadcast([P, 4, D0]), ALU.mult)
                link(ins)
                dve.tensor_tensor(row(m.mix, t), part[s][:, :].unsqueeze(1), row(m.xn, t), ALU.add).then_inc(s_out, 1)

            low(0, 0)
            tiles(dve, step)

        @block.tensor
        def _(pe):
            opened(pe, s_q, s_att)

            def queries(t, s):
                pe.wait_ge(s_qs, freed(t))
                for o in range(CH):
                    for h in range(CH):
                        ins = pe.matmul(qp[s][:, o * P:o * P + P], wq[:, h, o * P:o * P + P],
                                        m.xnT[:, h, bass.ds(t * P, P)], start=h == 0, stop=h == CH - 1)
                ins.then_inc(s_q, 1)

            def step(t, s, k, last):
                if not last:
                    queries(t + 1, 1 - s)
                pe.wait_ge(s_qs, done(t))
                pe.wait_ge(s_out, freed(t))
                for h in range(CH):
                    ins = pe.matmul(ap[s][:, h * KVW:h * KVW + KVW], qs[s][:, h, :], m.bd[:, h, :],
                                    start=True, stop=True)
                ins.then_inc(s_att, 1)

            pe.wait_ge(s_w, 16)
            queries(0, 0)
            tiles(pe, step)



def phase_mlp(nc, m, d, share):
    s_w, s_normed, s_flipped, s_row, s_hid, s_gelu, s_y, s_out, s_wchain, s_tchain, s_last = m.sems(
        "mlp", "w normed flipped row hid gelu y out wchain tchain last")
    s_stats1, s_var1, s_std1, s_stats2, s_var2, s_std2 = m.sems("mlp", "stats1 var1 std1 stats2 var2 std2")
    with ExitStack() as mem, nc.Block() as block:
        sb = lambda name, shape, dt=F32: mem.enter_context(nc.sbuf_tensor("mlp_" + name, shape, dt))
        w1 = sb("w1", [P, CH, C])
        w2 = sb("w2", [P, CH, C])
        b1 = sb("b1", [P, CH])
        b2 = sb("b2", [1, C])
        gb = sb("gb", [P, 4, C])
        stats = sb("stats", [P, T, 6])
        raw = [sb(f"raw{s}", [P, C]) for s in range(SLOTS)]
        xs = [sb(f"xs{s}", [P, C]) for s in range(SLOTS)]
        xt = [sb(f"xt{s}", [P, CH, P]) for s in range(SLOTS)]
        hs = [sb(f"hs{s}", [P, CH, P]) for s in range(SLOTS)]
        flip, hp, yp = m.psum[0:2], m.psum[2:4], m.psum[4:6]
        NW = 4 + 4

        @block.sync
        def _(sp):
            for i, v in enumerate((d.ln1_g, d.ln1_b, d.ln2_g, d.ln2_b)):
                sp.dma_start(gb[:, i, :], v.rearrange("(a c) -> a c", a=1).to_broadcast([P, C])).then_inc(s_w, 16)
            sp.dma_start(w1[:, :, :], d.mw1.rearrange("(h p) o -> p h o", p=P)).then_inc(s_w, 16)
            sp.dma_start(w2[:, :, :], d.mw2.rearrange("(h p) o -> p h o", p=P)).then_inc(s_w, 16)
            sp.dma_start(b1[:, :], d.mb1).then_inc(s_w, 16)
            sp.dma_start(b2[:, :], d.mb2.rearrange("(a c) -> a c", a=1)).then_inc(s_w, 16)
            load_experts(sp, m, d, 6, X)

        @block.gpsimd
        def _(pool):
            scatter_edges(pool, m, d, *share)

        @block.scalar
        def _(act):
            opened(act, s_gelu)
            stats_scalar(act, m, s_var1, s_std1)

            def step(t, s, k, last):
                act.wait_ge(s_hid, done(t))
                act.wait_ge(s_y, freed(t))
                for h in range(CH):
                    ins = act.activation(hs[s][:, h, :], hp[s][:, h * P:h * P + P], ACT.Gelu, bias=b1[:, h:h + 1])
                ins.then_inc(s_gelu, 1)

            act.wait_ge(s_w, 16 * NW)
            tiles(act, step)
            stats_scalar(act, m, s_var2, s_std2)

        @block.vector
        def _(dve):
            link = Chain(dve, s_wchain)
            opened(dve, s_normed, s_row, s_out)
            each_tile(dve, lambda t: row_stats(dve, m.mix, stats, t, s_stats1))
            dve.wait_ge(s_stats1, T)
            stats_vector(dve, link, m, stats[:, :, :], s_var1, s_std1)
            dve.wait_ge(s_w, 16 * NW)

            def norm(t, s):
                chain = Chain(dve, s_tchain, t * 2)
                chain(normalise(dve, m, raw[s][:, :].unsqueeze(1), t, m.mix))
                chain(dve.tensor_tensor(raw[s][:, :], raw[s][:, :], gb[:, 0, :], ALU.mult))
                dve.wait_ge(s_flipped, freed(t))
                dve.tensor_tensor(xs[s][:, :], raw[s][:, :], gb[:, 1, :], ALU.add).then_inc(s_normed, 1)

            def turn(t, s):
                dve.wait_ge(s_flipped, done(t))
                dve.wait_ge(s_hid, freed(t))
                dve.tensor_copy(xt[s][:, :, :], flip[s][:, 0:C].rearrange("p (h c) -> p h c", h=CH)).then_inc(s_row, 1)

            def step(t, s, k, last):
                if not last:
                    norm(t + 1, 1 - s)
                    turn(t + 1, 1 - s)
                dve.wait_ge(s_y, done(t))
                dve.wait_ge(s_normed, done(t))
                dve.tensor_tensor(row(m.mix, t), yp[s][:, 0:C].unsqueeze(1), xs[s][:, :].unsqueeze(1), ALU.add).then_inc(s_out, 1)
                dve.wait_ge(s_out, done(t))
                row_stats(dve, m.mix, stats, t, s_stats2)

            norm(0, 0)
            turn(0, 0)
            tiles(dve, step)
            dve.wait_ge(s_stats2, T)
            stats_vector(dve, link, m, stats[:, :, :], s_var2, s_std2)
            each_tile(dve, lambda t: normalise(dve, m, row(m.mix, t), t, m.mix).then_inc(s_last, 1))
            dve.wait_ge(s_last, T)
            link(dve.tensor_tensor(m.mix[:, :, :], m.mix[:, :, :], gb[:, 2:3, :].to_broadcast([P, T, C]), ALU.mult))
            link(dve.tensor_tensor(m.mix[:, :, :], m.mix[:, :, :], gb[:, 3:4, :].to_broadcast([P, T, C]), ALU.add))
            link(dve.tensor_tensor(m.x[:, :, :], m.x[:, :, :], m.mix[:, :, :], ALU.add))

        @block.tensor
        def _(pe):
            opened(pe, s_flipped, s_hid, s_y)

            def flips(t, s):
                pe.wait_ge(s_normed, done(t))
                pe.wait_ge(s_row, freed(t))
                for h in range(CH):
                    ins = pe.transpose(flip[s][:, h * P:h * P + P], xs[s][:, h * P:h * P + P], m.ident[:, :])
                ins.then_inc(s_flipped, 1)

            def step(t, s, k, last):
                pe.wait_ge(s_row, done(t))
                pe.wait_ge(s_gelu, freed(t))
                for o in range(CH):
                    for h in range(CH):
                        ins = pe.matmul(hp[s][:, o * P:o * P + P], w1[:, h, o * P:o * P + P], xt[s][:, h, :],
                                        start=h == 0, stop=h == CH - 1)
                ins.then_inc(s_hid, 1)
                if not last:
                    flips(t + 1, 1 - s)
                pe.wait_ge(s_out, freed(t))
                pe.matmul(yp[s][:, 0:C], m.ones[0:1, :], b2[:, :], start=True, stop=False)
                pe.wait_ge(s_gelu, done(t))
                for h in range(CH):
                    ins = pe.matmul(yp[s][:, 0:C], hs[s][:, h, :], w2[:, h, :], start=False, stop=h == CH - 1)
                ins.then_inc(s_y, 1)

            pe.wait_ge(s_w, 16 * NW)
            flips(0, 0)
            tiles(pe, step)



def phase_aggregate(nc, m, d):
    s_rec, s_idx, s_issue, s_hot, s_sum, s_add, s_zero, s_wchain = m.sems("agg", "rec idx issue hot sum add zero wchain")
    s_mean, s_dev, s_sq, s_var, s_vare, s_sd, s_aff, s_tanh = m.sems("agg", "mean dev sq var vare sd aff tanh")
    s_masked, s_stats, s_whole = m.sems("agg", "masked stats whole")
    s_row = m.sems("agg", " ".join(f"row{u}" for u in range(GB)))
    HALF = GB // 2
    GROUP = 8
    PART = 5
    parts = [slice(t, t + PART) for t in range(0, T, PART)]
    OH, AHEAD = 4, 3
    with ExitStack() as mem, nc.Block() as block:
        sb = lambda name, shape, dt=F32: mem.enter_context(nc.sbuf_tensor("agg_" + name, shape, dt))
        acc = sb("acc", [P, T, C])
        tmp = m.mix
        recs = sb("recs", [P, EBLK, 4])
        bn = sb("bn", [P, 2, C])
        stat = sb("stat", [P, 4, C])
        rows = [sb(f"rows{u}", [P, C]) for u in range(GB)]
        idx = [sb(f"idx{h}", [P, HALF], I32) for h in range(2)]
        hot = [sb(f"hot{u}", [P, P]) for u in range(OH)]
        bank = m.psum[0:OH]

        @block.sync
        def _(sp):
            sp.dma_start(recs[:, :, :].rearrange("p j r -> p (j r)"), d.rec.rearrange("(p j) r -> p (j r)", p=P)).then_inc(s_rec, 16)
            sp.dma_start(bn[:, 0, :], d.bn_w.rearrange("(a c) -> a c", a=1).to_broadcast([P, C])).then_inc(s_rec, 16)
            sp.dma_start(bn[:, 1, :], d.bn_b.rearrange("(a c) -> a c", a=1).to_broadcast([P, C])).then_inc(s_rec, 16)

        @block.gpsimd
        def _(pool):
            with pool.Fori(0, EBLK // GB) as k:
                for h in range(2):
                    pool.wait_ge(s_idx, k * 2 + h + 1)
                    pool.sem_inc(s_issue, 1)
                    for u in range(HALF):
                        v = h * HALF + u
                        pool.indirect_dma_start(out=rows[v][:, :], out_offset=None, in_=d.support,
                                                in_offset=bass.IndirectOffsetOnAxis(ap=idx[h][:, u:u + 1], axis=0))\
                            .then_inc(s_row[v], 16)

            for i, g in enumerate(parts):
                pool.wait_ge(s_tanh, i + 1)
                pool.tensor_tensor(m.x[:, g, :], m.x[:, g, :], tmp[:, g, :], ALU.add).then_inc(s_whole, 1)

        @block.vector
        def _(dve):
            dve.memset(acc[:, :, :], 0.0).then_inc(s_zero, 1)
            dve.sem_inc(s_add, OH)
            dve.wait_ge(s_zero, 1)
            dve.wait_ge(s_rec, 48)

            def weigh(j, u):
                dve.wait_ge(s_sum, j + 1 + GB - OH)
                dve.tensor_scalar(hot[u % OH][:, :], m.iota[:, 0:P], recs[:, bass.ds(j, 1), 0], recs[:, bass.ds(j, 1), 1],
                                  ALU.is_equal, ALU.mult).then_inc(s_hot, 1)

            def owners(j):
                _, tile = nc.values_load_multi_w_load_instructions(m.eowner[0:1, bass.ds(j, GROUP)], [mybir.EngineType.DVE],
                                                                   min_val=0, max_val=T - 1)
                return tile

            def add(j, u, owner):
                dve.wait_ge(s_sum, j + GB + 1)
                dve.wait_ge(s_add, j + OH)
                a = acc[:, bass.ds(owner, 1), :]
                dve.tensor_tensor(a, a, bank[u % OH][:, 0:C].unsqueeze(1), ALU.add).then_inc(s_add, 1)

            for u in range(AHEAD):
                weigh(u, u)
            with dve.Fori(0, EBLK // GROUP - 1) as k:
                tile = owners(k * GROUP)
                for u in range(GROUP):
                    weigh(k * GROUP + u + AHEAD, u + AHEAD)
                    add(k * GROUP + u, u, tile[u])
            tile = owners(EBLK - GROUP)
            for u in range(GROUP):
                if u + AHEAD < GROUP:
                    weigh(EBLK - GROUP + u + AHEAD, u + AHEAD)
                add(EBLK - GROUP + u, u, tile[u])
            link = Chain(dve, s_wchain)
            dve.wait_ge(s_add, EBLK + OH)
            mean, var, gain, shift = (stat[:, i, :] for i in range(4))
            dve.tensor_reduce(mean, acc[:, :, :].rearrange("p t c -> p c t"), AX.X, ALU.add).then_inc(s_mean, 1)
            dve.wait_ge(s_mean, 2)
            link(dve.tensor_scalar(mean, m.psum[4][:, 0:C], 1.0 / N, None, ALU.mult))
            for g in parts:
                dve.tensor_tensor(acc[:, g, :], acc[:, g, :], stat[:, 0:1, :].to_broadcast([P, PART, C]),
                                  ALU.subtract).then_inc(s_dev, 1)
            dve.wait_ge(s_sq, len(parts))
            dve.tensor_scalar(tmp[:, T - 1, :], tmp[:, T - 1, :], m.lastmask[:, 0:1], None, ALU.mult).then_inc(s_masked, 1)
            dve.wait_ge(s_var, 1)
            dve.tensor_scalar(var, m.psum[5][:, 0:C], 1.0 / N, 1e-5, ALU.mult, ALU.add).then_inc(s_vare, 1)
            dve.wait_ge(s_sd, 1)
            link(dve.reciprocal(gain, shift))
            link(dve.tensor_tensor(gain, gain, bn[:, 0, :], ALU.mult))

            def take_stats(i):
                g = parts[i]
                dve.wait_ge(s_whole, i + 1)
                for t in range(g.start, g.stop):
                    row_stats(dve, m.x, m.stats, t, s_stats)

            for i, g in enumerate(parts):
                link(dve.tensor_tensor(acc[:, g, :], acc[:, g, :], stat[:, 2:3, :].to_broadcast([P, PART, C]), ALU.mult))
                dve.tensor_tensor(acc[:, g, :], acc[:, g, :], bn[:, 1:2, :].to_broadcast([P, PART, C]), ALU.add).then_inc(s_aff, 1)
                if i > 1:
                    take_stats(i - 2)
            take_stats(len(parts) - 2)
            take_stats(len(parts) - 1)
            dve.wait_ge(s_stats, T)

        @block.scalar
        def _(act):
            act.wait_ge(s_rec, 48)
            with act.Fori(0, EBLK // GB) as k:
                for h in range(2):
                    col = k * GB + h * HALF
                    act.wait_ge(s_sum, col + HALF)
                    act.activation(idx[h][:, :], recs.bitcast(I32)[:, bass.ds(col, HALF), 2], ACT.Copy).then_inc(s_idx, 1)
            for i, g in enumerate(parts):
                act.wait_ge(s_dev, i + 1)
                act.activation(tmp[:, g, :], acc[:, g, :], ACT.Square).then_inc(s_sq, 1)
            act.wait_ge(s_vare, 1)
            act.activation(stat[:, 3, :], stat[:, 1, :], ACT.Sqrt).then_inc(s_sd, 1)
            for i, g in enumerate(parts):
                act.wait_ge(s_aff, i + 1)
                act.activation(tmp[:, g, :], acc[:, g, :], ACT.Tanh).then_inc(s_tanh, 1)

        @block.tensor
        def _(pe):
            pe.sem_inc(s_sum, GB)
            with pe.Fori(0, EBLK // GB) as k:
                for u in range(GB):
                    j = k * GB + u
                    pe.wait_ge(s_hot, j + 1)
                    pe.wait_ge(s_row[u], k * 16 + 16)
                    pe.wait_ge(s_add, j + 1)
                    pe.matmul(bank[u % OH][:, 0:C], hot[u % OH][:, :], rows[u][:, :], start=True, stop=True)\
                      .then_inc(s_sum, 1)

            pe.wait_ge(s_mean, 1)
            pe.matmul(m.psum[4][:, 0:C], m.ones[:, :], stat[:, 0, :], start=True, stop=True).then_inc(s_mean, 1)
            for i, g in enumerate(parts):
                if i < len(parts) - 1:
                    pe.wait_ge(s_sq, i + 1)
                else:
                    pe.wait_ge(s_masked, 1)
                for t in range(g.start, g.stop):
                    ins = pe.matmul(m.psum[5][:, 0:C], m.ones[:, :], tmp[:, t, :], start=t == 0, stop=t == T - 1)
            ins.then_inc(s_var, 1)


def first_best(dve, m, link, score, best, place, tmp):
    wide = lambda a: a.unsqueeze(2).to_broadcast([P, T, X])
    link(dve.tensor_reduce(best, score[:, :, :], AX.X, ALU.max))
    link(dve.tensor_tensor(tmp[:, :, :], score[:, :, :], wide(best), ALU.is_lt))
    link(dve.scalar_tensor_tensor(out=tmp[:, :, :], in0=tmp[:, :, :], scalar=float(X),
                                  in1=m.iota[:, 0:X].unsqueeze(1).to_broadcast([P, T, X]), op0=ALU.mult, op1=ALU.add))
    link(dve.tensor_reduce(place, tmp[:, :, :], AX.X, ALU.min))



def phase_route0(nc, m, d, w2):
    s_w, s_copied, s_flipped, s_row, s_gate, s_gated, s_wchain, s_diff, s_exp, s_counts, s_totals, \
        s_hot, s_placed, s_lchain = m.sems(
            "rt0", "w copied flipped row gate gated wchain diff exp counts totals hot placed lchain")
    s_var, s_std = m.sems("rt0", "var std")
    s_kept = m.sems("rt0", "kept0 kept1")
    s_bias = m.sem("rt0_bias")
    K = 2
    with ExitStack() as mem, nc.Block() as block:
        sb = lambda name, shape, dt=F32: mem.enter_context(nc.sbuf_tensor("rt0_" + name, shape, dt))
        small6 = sb("small6", [P, 6, 32])
        wg = sb("wg", [P, CH, X])
        bg = sb("bg", [P, X])
        xs = [sb(f"xs{s}", [P, C]) for s in range(SLOTS)]
        xt = [sb(f"xt{s}", [P, CH, P]) for s in range(SLOTS)]
        score = sb("score", [P, T, X])
        equal = sb("equal", [P, T, X])
        top = sb("top", [P, T, K])
        key = sb("key", [P, T, K])
        onehot = sb("onehot", [P, K * T * X])
        count = sb("count", [P, K * T * X])
        pos = sb("pos", [P, T * K])
        work = sb("work", [P, 4, max(K * T, FBLK0)])
        whole = sb("whole", [P, 3, K * T], I32)
        hi_hot = sb("hi_hot", [P, K * T, 2 * FBLK0], BF16)
        lo_hot = [sb(f"lo_hot{s}", [P, PICK, P], BF16) for s in range(SLOTS)]
        flip, gp = m.psum[0:2], m.psum[2:4]

        @block.sync
        def _(sp):
            sp.dma_start(wg[:, :, :], d.f0_wg.rearrange("(h p) e -> p h e", p=P)).then_inc(s_w, 16)
            sp.dma_start(bg[:, :], d.f0_bg.rearrange("(a c) -> a c", a=1).to_broadcast([P, X])).then_inc(s_w, 16)

            def keep(t, s, k, last):
                sp.wait_ge(s_copied, done(t))
                sp.dma_start(d.normed0[bass.ds(t * P, P), :], xs[s][:, :]).then_inc(s_kept[s], 16)
            tiles(sp, keep)
            sp.dma_start(m.b1_all[:, :, :], d.f0_b1).then_inc(s_bias, 16)
            sp.dma_start(m.b2[:, :, :].rearrange("p e c -> p (e c)"),
                         d.f0_b2.rearrange("e c -> (e c)").rearrange("(a c) -> a c", a=1).to_broadcast([P, X * C])).then_inc(s_bias, 16)
            for e in range(X):
                sp.dma_start(w2[:, e, :, :], d.f0_w2[e, :, :].rearrange("(h p) o -> p h o", p=P)).then_inc(m.s_w2, 16)
            for s in range(SLOTS):
                sp.wait_ge(s_kept[s], 16 * ((T - s + 1) // 2))
            sp.wait_ge(s_bias, 32)

        @block.scalar
        def _(act):
            stats_scalar(act, m, s_var, s_std)
            act.wait_ge(s_diff, 1)
            act.activation(m.prob[:, :, 1], top[:, :, 1], ACT.Exp).then_inc(s_exp, 1)

        @block.vector
        def _(dve):
            link = Chain(dve, s_wchain)
            stats_vector(dve, link, m, m.stats[:, :, :], s_var, s_std)
            dve.wait_ge(s_w, 32)
            opened(dve, s_copied, s_row, s_gated)

            def norm(t, s, uses):
                dve.wait_ge(s_flipped, freed(t))
                landed(dve, s_kept[s], uses)
                normalise(dve, m, xs[s][:, :].unsqueeze(1), t).then_inc(s_copied, 1)

            def turn(t, s):
                dve.wait_ge(s_flipped, done(t))
                dve.wait_ge(s_gate, freed(t))
                dve.tensor_copy(xt[s][:, :, :], flip[s][:, 0:C].rearrange("p (h c) -> p h c", h=CH)).then_inc(s_row, 1)

            def scores(t, s):
                dve.wait_ge(s_gate, done(t))
                dve.tensor_tensor(row(score, t), gp[s][:, 0:X].unsqueeze(1), bg[:, :].unsqueeze(1), ALU.add).then_inc(s_gated, 1)

            def step(t, s, k, last):
                if not last:
                    norm(t + 2, s, k + 1)
                turn(t + 1, 1 - s)
                scores(t, s)

            for t in range(2):
                norm(t, t, 0)
            turn(0, 0)
            tiles(dve, step, T - 1)
            scores(T - 1, (T - 1) % 2)
            dve.wait_ge(s_gated, done(T - 1))
            link = Chain(dve, s_lchain)
            first_best(dve, m, link, score, top[:, :, 0], key[:, :, 0], equal)
            link(dve.tensor_tensor(equal[:, :, :], m.iota[:, 0:X].unsqueeze(1).to_broadcast([P, T, X]),
                                   key[:, :, 0].unsqueeze(2).to_broadcast([P, T, X]), ALU.is_equal))
            link(dve.scalar_tensor_tensor(out=score[:, :, :], in0=equal[:, :, :], scalar=-3e38, in1=score[:, :, :],
                                          op0=ALU.mult, op1=ALU.add))
            first_best(dve, m, link, score, top[:, :, 1], key[:, :, 1], equal)
            dve.tensor_tensor(top[:, :, 1], top[:, :, 1], top[:, :, 0], ALU.subtract).then_inc(s_diff, 1)
            dve.wait_ge(s_exp, 1)
            link(dve.tensor_scalar(m.prob[:, :, 0], m.prob[:, :, 1], 1.0, None, ALU.add))
            link(dve.reciprocal(m.prob[:, :, 0], m.prob[:, :, 0]))
            link(dve.tensor_tensor(m.prob[:, :, 1], m.prob[:, :, 1], m.prob[:, :, 0], ALU.mult))
            sort_vector(dve, m, link, key[:, :, :].rearrange("p t k -> p (t k)"), onehot, count, small6, m.psum[4],
                        pos[:, :], s_counts, s_totals, X, K * T)
            invert_vector(dve, m, link, pos[:, :], m.tile2[:, :, :].rearrange("p t k -> p (t k)"), work, whole, hi_hot[:, :, :], lo_hot, m.psum[5],
                          K * T, FBLK0, s_hot, s_placed)
            sort_owner(dve, m, link, small6[:, 5, :], count[:, 0:FBLK0], m.fown[:, 0:FBLK0], X, FBLK0)

        @block.tensor
        def _(pe):
            opened(pe, s_flipped, s_gate)
            pe.wait_ge(s_w, 32)

            def flips(t, s):
                pe.wait_ge(s_copied, done(t))
                pe.wait_ge(s_row, freed(t))
                for h in range(CH):
                    ins = pe.transpose(flip[s][:, h * P:h * P + P], xs[s][:, h * P:h * P + P], m.ident[:, :])
                ins.then_inc(s_flipped, 1)

            def gates(t, s):
                pe.wait_ge(s_row, done(t))
                pe.wait_ge(s_gated, freed(t))
                for h in range(CH):
                    ins = pe.matmul(gp[s][:, 0:X], xt[s][:, h, :], wg[:, h, :], start=h == 0, stop=h == CH - 1)
                ins.then_inc(s_gate, 1)

            def step(t, s, k, last):
                if not last:
                    flips(t + 2, s)
                gates(t + 1, 1 - s)

            flips(0, 0)
            flips(1, 1)
            gates(0, 0)
            tiles(pe, step, T - 1)
            sort_tensor(pe, m, small6, m.psum[4], s_counts, s_totals, X)
            invert_tensor(pe, m, hi_hot, lo_hot, m.psum[5], K * T, FBLK0, s_hot, s_placed)


def hidden_turned(pe, hp, w1, xt):
    for q in range(HC):
        for h in range(CH):
            ins = pe.matmul(hp[q // 4][:, q % 4 * P:q % 4 * P + P], w1[:, h, q * P:q * P + P], xt[:, h, :],
                            start=h == 0, stop=h == CH - 1)
    return ins


def gather(pool, m, rows, xin, slot, j, s_token, s_gather, s_load):
    pool.tensor_copy(slot[:, :], m.token[:, bass.ds(j, 1)]).then_inc(s_token, 1)
    pool.wait_ge(s_token, j + 1)
    pool.sem_inc(s_gather, 1)
    pool.indirect_dma_start(out=xin[:, :], out_offset=None, in_=rows,
                            in_offset=bass.IndirectOffsetOnAxis(ap=slot[:, 0:1], axis=0)).then_inc(s_load, 16)


def results(pool, m, rows, k, ys, slot, j, s_slot, s_issue, s_store):
    pool.tensor_copy(slot[:, :], m.dest[:, bass.ds(j, 1)]).then_inc(s_slot, 1)
    pool.wait_ge(s_slot, j + 1)
    pool.sem_inc(s_issue, 1)
    pool.indirect_dma_start(out=rows, out_offset=bass.IndirectOffsetOnAxis(ap=slot[:, 0:1], axis=0), in_=ys[:, :],
                            in_offset=None, bounds_check=k * T * P - 1, oob_is_err=False).then_inc(s_store, 16)



def phase_experts(nc, m, name, nblk, normed, out, K, function, w2, s_w2, own):
    s_flipped, s_row, s_hid, s_held, s_y, s_out, s_picked = m.sems(name, "flipped row hid held y out picked")
    s_slot, s_issue, s_token, s_gather = m.sems(name, "slot issue token gather")
    s_load, s_store = m.sems(name, "load0 load1"), m.sems(name, "store0 store1")
    with ExitStack() as mem, nc.Block() as block:
        sb = lambda what, shape, dt=F32: mem.enter_context(nc.sbuf_tensor(name + "_" + what, shape, dt))
        b2, b1_all = m.b2, m.b1_all
        xin = [sb(f"xin{s}", [P, C]) for s in range(SLOTS)]
        token = [sb(f"token{s}", [P, 1], I32) for s in range(SLOTS)]
        slot = [sb(f"slot{s}", [P, 1], I32) for s in range(SLOTS)]
        xt = [sb(f"xt{s}", [P, CH, P]) for s in range(SLOTS)]
        hs = [sb(f"hs{s}", [P, HC, P]) for s in range(SLOTS)]
        ys = [sb(f"ys{s}", [P, C]) for s in range(SLOTS)]
        if own:
            w1 = [sb(f"w1{s}", [P, CH, HID]) for s in range(SLOTS)]
            b1 = [sb(f"b1{s}", [P, HC]) for s in range(SLOTS)]
        else:
            w1, b1 = [m.f1_w1] * SLOTS, [m.f1_b1] * SLOTS
        flip, yp, hp = m.psum[0:2], m.psum[2:4], [m.psum[4:6], m.psum[6:8]]

        @block.gpsimd
        def _(pool):
            fetch = lambda j, s: gather(pool, m, normed, xin[s], token[s], j, s_token, s_gather, s_load[s])
            send = lambda j, s: results(pool, m, out, K, ys[s], slot[s], j, s_slot, s_issue, s_store[s])
            fetch(0, 0)
            fetch(1, 1)

            def step(j, s, k, last):
                if not last:
                    pool.wait_ge(s_row, done(j))
                    fetch(j + 2, s)
                if not isinstance(j, int) or j > 0:
                    pool.wait_ge(s_out, done(j - 1))
                    send(j - 1, 1 - s)
            tiles(pool, step, nblk - 1, peel=True)
            pool.wait_ge(s_out, done(nblk - 1))
            send(nblk - 2, (nblk - 2) % 2)
            send(nblk - 1, (nblk - 1) % 2)
            for s in range(SLOTS):
                pool.wait_ge(s_store[s], 16 * ((nblk - s + 1) // 2))

        @block.scalar
        def _(act):
            opened(act, s_held)

            def step(j, s, k, last):
                act.wait_ge(s_hid, done(j))
                act.wait_ge(s_y, freed(j))
                for q in range(HC):
                    ins = act.activation(hs[s][:, q, :], hp[s][q // 4][:, q % 4 * P:q % 4 * P + P], function, bias=b1[s][:, q:q + 1])
                ins.then_inc(s_held, 1)
            tiles(act, step, nblk)

        @block.vector
        def _(dve):
            opened(dve, s_row, s_out, s_picked)
            if own:
                dve.wait_ge(m.s_w1, 16 * X)

            def turn(j, s):
                dve.wait_ge(s_flipped, done(j))
                dve.wait_ge(s_hid, freed(j))
                dve.tensor_copy(xt[s][:, :, :], flip[s][:, 0:C].rearrange("p (h c) -> p h c", h=CH)).then_inc(s_row, 1)

            def pick(j, s):
                if own:
                    e = dve.value_load(m.fown[0:1, bass.ds(j, 1)], min_val=0, max_val=X - 1)
                    dve.wait_ge(s_hid, freed(j))
                    dve.wait_ge(s_held, freed(j))
                    dve.tensor_copy(b1[s][:, :].unsqueeze(1), b1_all[:, bass.ds(e, 1), :])
                    dve.tensor_copy(w1[s][:, :, :].unsqueeze(1), m.w1[:, bass.ds(e, 1), :, :]).then_inc(s_picked, 1)

            def result(j, s, k):
                e = dve.value_load(m.fown[0:1, bass.ds(j, 1)], min_val=0, max_val=X - 1)
                dve.wait_ge(s_y, done(j))
                landed(dve, s_store[s], k)
                dve.tensor_tensor(ys[s][:, :].unsqueeze(1), yp[s][:, 0:C].unsqueeze(1), b2[:, bass.ds(e, 1), :], ALU.add).then_inc(s_out, 1)

            for j in range(2):
                pick(j, j)
                turn(j, j)

            def step(j, s, k, last):
                if not last:
                    turn(j + 2, s)
                    pick(j + 2, s)
                result(j, s, k)
            tiles(dve, step, nblk - 1, peel=True)
            result(nblk - 1, (nblk - 1) % 2, (nblk - 1) // 2)

        @block.tensor
        def _(pe):
            opened(pe, s_flipped, s_hid, s_y)

            def flips(j, s, k):
                pe.wait_ge(s_load[s], 16 * k + 16)
                pe.wait_ge(s_row, freed(j))
                for h in range(CH):
                    ins = pe.transpose(flip[s][:, h * P:h * P + P], xin[s][:, h * P:h * P + P], m.ident[:, :])
                ins.then_inc(s_flipped, 1)

            def hidden(j, s):
                pe.wait_ge(s_row, done(j))
                pe.wait_ge(s_held, freed(j))
                if own:
                    pe.wait_ge(s_picked, done(j))
                hidden_turned(pe, hp[s], w1[s], xt[s]).then_inc(s_hid, 1)

            def result(j, s):
                e = pe.value_load(m.fown[0:1, bass.ds(j, 1)], min_val=0, max_val=X - 1)
                pe.wait_ge(s_held, done(j))
                pe.wait_ge(s_out, freed(j))
                for q in range(HC):
                    ins = pe.matmul(yp[s][:, 0:C], hs[s][:, q, :], w2[:, bass.ds(e, 1), q, :], start=q == 0, stop=q == HC - 1)
                ins.then_inc(s_y, 1)

            flips(0, 0, 0)
            hidden(0, 0)
            flips(1, 1, 0)
            pe.wait_ge(s_w2, 16 * X)

            def step(j, s, k, last):
                hidden(j + 1, 1 - s)
                if not last:
                    flips(j + 2, s, k + 1)
                result(j, s)
            tiles(pe, step, nblk - 1)
            result(nblk - 1, (nblk - 1) % 2)



G = 2 * H1
PROJECT_LOADS = 7 + 2 * G


def load_project(sp, m, d):
    for i, a in enumerate((d.wk, d.wv, d.g_w)):
        sp.dma_start(m.p_w[:, :, i * C:i * C + C], a.rearrange("(h p) o -> p h o", p=P)).then_inc(m.s_project, 16)
    for u, a in enumerate((d.g_al, d.g_ar)):
        sp.dma_start(m.p_attn[:, u, :], a.rearrange("h c -> (h c)").rearrange("(a c) -> a c", a=1).to_broadcast([P, C])).then_inc(m.s_project, 16)
    sp.dma_start(m.p_wo[:, :, :], d.wo.rearrange("(h p) o -> p h o", p=P)).then_inc(m.s_project, 16)
    sp.dma_start(m.p_wq[:, :, :], d.wq.rearrange("(h p) o -> p h o", p=P)).then_inc(m.s_project, 16)
    for i, pair in enumerate(((d.k_g, d.v_g), (d.k_b, d.v_b))):
        for g in range(G):
            v = pair[g // H1]
            sp.dma_start(m.p_gb[:, i, g * D1:g * D1 + D1], v.rearrange("(a c) -> a c", a=1).to_broadcast([P, D1])).then_inc(m.s_project, 16)


def load_hidden(sp, m, d):
    sp.dma_start(m.f1_w1[:, :, :], d.f1_w1.rearrange("(h p) o -> p h o", p=P)).then_inc(m.s_hidden, 16)
    sp.dma_start(m.f1_b1[:, :], d.f1_b1).then_inc(m.s_hidden, 16)
    sp.dma_start(m.f1_wg[:, :, :], d.f1_wg.rearrange("(q p) e -> p q e", p=P)).then_inc(m.s_hidden, 16)
    sp.dma_start(m.f1_bg[:, :], d.f1_bg.rearrange("(a c) -> a c", a=1).to_broadcast([P, X])).then_inc(m.s_hidden, 16)


def phase_combine(nc, m, d, name, results, K, last):
    GROUP = 5
    s_chain, s_stats, s_wchain, s_var, s_std, s_stored = m.sems(name, "chain stats wchain var std stored")
    s_y = m.sems(name, " ".join(f"y{g}" for g in range(T // GROUP)))
    groups = [slice(t, t + GROUP) for t in range(0, T, GROUP)]
    with ExitStack() as mem, nc.Block() as block:
        sb = lambda n, shape, dt=F32: mem.enter_context(nc.sbuf_tensor(name + n, shape, dt))
        y = sb("y", [P, K, T, C])
        stats = sb("stats", [P, T, 6])
        by_tile = results.rearrange("(k t p) c -> p k t c", k=K, p=P)

        @block.sync
        def _(sp):
            for g, s in zip(groups, s_y):
                for k in range(K):
                    sp.dma_start(y[:, k, g, :], by_tile[:, k, g, :]).then_inc(s, 16)
            if last:
                for i, g in enumerate(groups):
                    sp.wait_ge(s_chain, (i + 1) * K * GROUP)
                    whole = min(g.stop, T - 1)
                    sp.dma_start(d.out[g.start * P:whole * P, :].rearrange("(t p) c -> p t c", p=P),
                                 m.x[:, g.start:whole, :]).then_inc(s_stored, 16)
                sp.dma_start(d.out[(T - 1) * P:N, :], m.x[0:LAST, T - 1, :]).then_inc(s_stored, 16)
                sp.wait_ge(s_stored, 16 * (len(groups) + 1))
            else:
                load_project(sp, m, d)
                load_hidden(sp, m, d)
                for e in range(X):
                    sp.dma_start(m.wd[:, e, :, :], d.f1_wd[e, :, :].rearrange("(q p) o -> p q o", p=P)).then_inc(m.s_wd, 16)

        @block.scalar
        def _(act):
            if not last:
                stats_scalar(act, m, s_var, s_std)

        @block.vector
        def _(dve):
            for i, g in enumerate(groups):
                dve.wait_ge(s_y[i], 16 * K)
                for k in range(K):
                    if k > 0:
                        dve.wait_ge(s_chain, (i * K + k) * GROUP)
                    for t in range(g.start, g.stop):
                        dve.scalar_tensor_tensor(out=row(m.x, t), in0=y[:, k, t:t + 1, :], scalar=m.prob[:, t:t + 1, k],
                                                 in1=row(m.x, t), op0=ALU.mult, op1=ALU.add).then_inc(s_chain, 1)
                if not last:
                    dve.wait_ge(s_chain, (i + 1) * K * GROUP)
                    for t in range(g.start, g.stop):
                        row_stats(dve, m.x, stats, t, s_stats)
            if not last:
                dve.wait_ge(s_stats, T)
                stats_vector(dve, Chain(dve, s_wchain), m, stats[:, :, :], s_var, s_std)



def phase_project1(nc, m, d):
    s_normed, s_flipped, s_row, s_rowall, s_proj, s_xt, s_chain, s_var, s_std, s_centred, s_gain, s_kv, s_block, \
        s_r, s_rheld, s_m = m.sems(
            "pr1", "normed flipped row rowall proj xt chain var std centred gain kv block r rheld m")
    s_store = m.sems("pr1", "store0 store1")
    s_fold, s_ends, s_endload = m.sems("pr1", "fold ends endload")
    s_wchain, s_gchain = m.sems("pr1", "wchain gchain")
    with ExitStack() as mem, nc.Block() as block:
        sb = lambda name, shape, dt=F32: mem.enter_context(nc.sbuf_tensor("pr1_" + name, shape, dt))
        w, attn, wo, wq, gb = m.p_w, m.p_attn, m.p_wo, m.p_wq, m.p_gb
        scaled = [sb(f"scaled{u}", [P, CH, C]) for u in range(2)]
        xs = [sb(f"xs{s}", [P, C]) for s in range(SLOTS)]
        xt = [sb(f"xt{s}", [P, CH, P]) for s in range(SLOTS)]
        gr = [sb(f"gr{s}", [P, GROW]) for s in range(SLOTS)]
        stats = [sb(f"stats{s}", [P, G, 6]) for s in range(SLOTS)]
        mean = [sb(f"mean{s}", [P, G]) for s in range(SLOTS)]
        dif = [sb(f"dif{s}", [P, G]) for s in range(SLOTS)]
        var = [sb(f"var{s}", [P, G]) for s in range(SLOTS)]
        std = [sb(f"std{s}", [P, G]) for s in range(SLOTS)]
        kn = [sb(f"kn{s}", [P, G * D1]) for s in range(SLOTS)]
        kv = [sb(f"kv{s}", [P, G * D1]) for s in range(SLOTS)]
        bd = sb("bd", [P, CH, P])
        r_ = sb("r", [P, CH, C])
        flip, kvp, grp, acc = m.psum[0:2], m.psum[2:4], m.psum[4:6], m.psum[6:8]

        @block.sync
        def _(sp):
            sp.wait_ge(s_ends, 1)
            sp.dma_start(m.ends[:, 0:T - 1, :], d.ends).then_inc(s_endload, 16)
            sp.dma_start(m.ends[0:LAST, T - 1, :], d.ends_last).then_inc(s_endload, 16)

            def step(t, s, k, last):
                sp.wait_ge(s_xt, done(t))
                sp.dma_start(d.graph[bass.ds(t * P, P), :], gr[s][:, :]).then_inc(s_store[s], 16)
            tiles(sp, step)
            sp.wait_ge(s_endload, 32)
            for s in range(SLOTS):
                sp.wait_ge(s_store[s], 16 * ((T - s + 1) // 2))

        @block.gpsimd
        def _(pool):
            opened(pool, s_gain)
            pool.memset(m.ends[:, :, :], 0).then_inc(s_ends, 1)
            pool.wait_ge(m.s_project, 16 * PROJECT_LOADS)

            def step(t, s, k, last):
                pool.wait_ge(s_centred, done(t))
                pool.wait_ge(s_kv, freed(t))
                pool.tensor_tensor(kv[s][:, :], kn[s][:, :], gb[:, 0, :], ALU.mult).then_inc(s_gchain, 1)
                pool.wait_ge(s_gchain, t + 1)
                ins = pool.tensor_tensor(kv[s][:, :], kv[s][:, :], gb[:, 1, :], ALU.add)
                if last:
                    ins.then_inc(s_gchain, 1)
                    pool.wait_ge(s_gchain, T + 1)
                    ins = pool.tensor_tensor(kv[s][:, 0:C], kv[s][:, 0:C], m.lastmask[:, 0:1].to_broadcast([P, C]), ALU.mult)
                ins.then_inc(s_gain, 1)
            tiles(pool, step)

        @block.scalar
        def _(act):
            opened(act, s_row, s_rowall, s_xt, s_std)

            def turn(t, s):
                act.wait_ge(s_flipped, done(t))
                act.wait_ge(s_proj, freed(t))
                turned = flip[s][:, 0:C].rearrange("p (h c) -> p h c", h=CH)
                act.activation(xt[s][:, :, :], turned, ACT.Copy).then_inc(s_row, 1)
                act.activation(m.xnT[:, :, bass.ds(t * P, P)], turned, ACT.Copy).then_inc(s_rowall, 1)

            def step(t, s, k, last):
                act.wait_ge(s_var, done(t))
                act.activation(std[s][:, :], var[s][:, :], ACT.Sqrt).then_inc(s_std, 1)
                act.wait_ge(s_proj, done(t))
                landed(act, s_store[s], k)
                act.activation(gr[s][:, :], grp[s][:, 0:GROW], ACT.Copy).then_inc(s_xt, 1)
                if not last:
                    turn(t + 2, s)

            for t in range(2):
                turn(t, t)
            tiles(act, step, T - 1, peel=True)
            step(T - 1, (T - 1) % 2, (T - 1) // 2, True)

        @block.vector
        def _(dve):
            opened(dve, s_normed, s_var, s_centred)
            wlink = Chain(dve, s_wchain)
            wlink(dve.memset(bd[:, :, :], 0.0))

            def norm(t, s):
                dve.wait_ge(s_flipped, freed(t))
                normalise(dve, m, xs[s][:, :].unsqueeze(1), t).then_inc(s_normed, 1)

            def step(t, s, k, last):
                dve.wait_ge(s_proj, done(t))
                link = Chain(dve, s_chain, t * 5)
                for g in range(G):
                    ins = dve.bn_stats(stats[s][:, g, :], kvp[s][:, g * D1:g * D1 + D1])
                link(ins)
                even, odd = stats[s][:, :, 0:3], stats[s][:, :, 3:6]
                dve.tensor_tensor(dif[s][:, :], even[:, :, 1], odd[:, :, 1], ALU.subtract)
                dve.tensor_tensor(var[s][:, :], even[:, :, 2], odd[:, :, 2], ALU.add)
                link(dve.tensor_tensor(mean[s][:, :], even[:, :, 1], odd[:, :, 1], ALU.add))
                dve.tensor_scalar(mean[s][:, :], mean[s][:, :], 0.5, None, ALU.mult)
                dve.scalar_tensor_tensor(out=dif[s][:, :], in0=dif[s][:, :], scalar=0.25, in1=dif[s][:, :], op0=ALU.mult, op1=ALU.mult)
                link(dve.tensor_scalar(var[s][:, :], var[s][:, :], 1.0 / D1, 1e-5, ALU.mult, ALU.add))
                dve.tensor_tensor(var[s][:, :], var[s][:, :], dif[s][:, :], ALU.add).then_inc(s_var, 1)
                if not last:
                    norm(t + 2, s)
                dve.wait_ge(s_std, done(t))
                link(dve.reciprocal(std[s][:, :], std[s][:, :]))
                dve.wait_ge(s_gain, freed(t))
                heads = lambda a: a[:, :].rearrange("p (g c) -> p g c", g=G)
                wide = lambda a: a[:, :].unsqueeze(2).to_broadcast([P, G, D1])
                link(dve.tensor_tensor(heads(kn[s]), heads(kvp[s]), wide(mean[s]), ALU.subtract))
                dve.tensor_tensor(heads(kn[s]), heads(kn[s]), wide(std[s]), ALU.mult).then_inc(s_centred, 1)

            for t in range(2):
                norm(t, t)
            dve.wait_ge(m.s_project, 16 * PROJECT_LOADS)
            for u in range(2):
                ins = dve.tensor_tensor(scaled[u][:, :, :], w[:, :, 2 * C:3 * C], attn[:, u:u + 1, :].to_broadcast([P, CH, C]), ALU.mult)
            wlink(ins)
            for u in range(2):
                ins = dve.tensor_reduce(w[:, :, 3 * C + u * H1:3 * C + (u + 1) * H1],
                                        scaled[u][:, :, :].rearrange("p k (h c) -> p k h c", h=H1), AX.X, ALU.add)
            ins.then_inc(s_fold, 1)
            tiles(dve, step, T - 1)
            step(T - 1, (T - 1) % 2, (T - 1) // 2, True)
            dve.wait_ge(s_kv, done(T - 1))
            for h in range(CH):
                for i in range(P // D1):
                    q = slice(D1 * i, D1 * i + D1)
                    ins = dve.tensor_scalar(bd[q, h, q], acc[h][q, q], 1.0 / N, None, ALU.mult)
            ins.then_inc(s_block, 1)
            dve.wait_ge(s_r, 1)
            for h in range(CH):
                ins = dve.tensor_copy(r_[:, h, :], m.psum[h][:, 0:C])
            ins.then_inc(s_rheld, 1)
            dve.wait_ge(s_m, 1)
            for h in range(CH):
                ins = dve.tensor_copy(m.mixer[:, h, :], m.psum[2 + h][:, 0:C])
            wlink(ins)

        @block.tensor
        def _(pe):
            opened(pe, s_flipped, s_proj, s_kv)
            for h in range(CH):
                pe.matmul(acc[h][:, 0:P], m.zeros[:, 0:P], m.zeros[:, 0:P], start=True, stop=False)

            def flips(t, s):
                pe.wait_ge(s_normed, done(t))
                pe.wait_ge(s_rowall, freed(t))
                for h in range(CH):
                    ins = pe.transpose(flip[s][:, h * P:h * P + P], xs[s][:, h * P:h * P + P], m.ident[:, :])
                ins.then_inc(s_flipped, 1)

            def project(t, s):
                pe.wait_ge(s_row, done(t))
                pe.wait_ge(s_centred, freed(t))
                pe.wait_ge(s_xt, freed(t))
                for h in range(CH):
                    pe.matmul(kvp[s][:, :], xt[s][:, h, :], w[:, h, 0:2 * C], start=h == 0, stop=h == CH - 1)
                for h in range(CH):
                    ins = pe.matmul(grp[s][:, 0:GROW], xt[s][:, h, :], w[:, h, 2 * C:2 * C + GROW], start=h == 0, stop=h == CH - 1)
                ins.then_inc(s_proj, 1)

            def products(t, s, last):
                pe.wait_ge(s_gain, done(t))
                for h in range(CH):
                    v = C + h * P
                    ins = pe.matmul(acc[h][:, 0:P], kv[s][:, v:v + P], kv[s][:, h * P:h * P + P], start=False, stop=last)
                ins.then_inc(s_kv, 1)

            flips(0, 0)
            flips(1, 1)
            pe.wait_ge(m.s_project, 16 * PROJECT_LOADS)
            pe.wait_ge(s_fold, 1)
            project(0, 0)

            def step(t, s, k, last):
                project(t + 1, 1 - s)
                if not last:
                    flips(t + 2, s)
                if not isinstance(t, int) or t > 0:
                    products(t - 1, 1 - s, False)
            tiles(pe, step, T - 1, peel=True)
            products(T - 2, (T - 2) % 2, False)
            products(T - 1, (T - 1) % 2, True)
            pe.wait_ge(s_block, 1)
            for h in range(CH):
                ins = pe.matmul(m.psum[h][:, 0:C], bd[:, h, :], wo[:, h, :], start=True, stop=True)
            ins.then_inc(s_r, 1)
            pe.wait_ge(s_rheld, 1)
            for c in range(CH):
                for h in range(CH):
                    ins = pe.matmul(m.psum[2 + c][:, 0:C], wq[:, h, c * P:c * P + P], r_[:, h, :], start=h == 0, stop=h == CH - 1)
            ins.then_inc(s_m, 1)



def phase_graph1(nc, m, d):
    s_w, s_copied, s_y, s_out, s_pcopy, s_issue, s_moved, s_chain, s_exp, s_exped = m.sems(
        "gr1", "w copied y out pcopy issue moved chain exp exped")
    GOT = 4
    s_got = m.sems("gr1", " ".join(f"got{s}" for s in range(GOT)))
    s_stats, s_var, s_std = m.sems("gr1", "stats var std")
    with ExitStack() as mem, nc.Block() as block:
        sb = lambda name, shape, dt=F32: mem.enter_context(nc.sbuf_tensor("gr1_" + name, shape, dt))
        bo = sb("bo", [1, C])
        ps = [sb(f"ps{s}", [P, 2], I32) for s in range(GOT)]
        got = [sb(f"got{s}", [P, 2, GROW]) for s in range(GOT)]
        source = sb("source", [P, T, H1])
        dest = sb("dest", [P, T, GROW])
        prod = sb("prod", [P, T, C])
        logit = sb("logit", [P, T, H1])
        tmp = sb("tmp", [P, T, H1])
        one = sb("one", [P, T])
        mean = sb("mean", [P, T, D1])
        xt = [sb(f"xt{s}", [P, CH, P]) for s in range(SLOTS)]
        stats = sb("stats", [P, T, 6])
        yp = m.psum[0:2]

        @block.sync
        def _(sp):
            sp.dma_start(bo[:, :], d.bo.rearrange("(a c) -> a c", a=1)).then_inc(s_w, 16)

        @block.gpsimd
        def _(pool):

            def step(t, s, k, last):
                pool.wait_ge(s_moved, t + 1)
                pool.tensor_copy(ps[s][:, :].unsqueeze(1), row(m.ends, t)).then_inc(s_pcopy, 1)
                pool.wait_ge(s_pcopy, t + 1)
                pool.sem_inc(s_issue, 1)
                for u in range(2):
                    pool.indirect_dma_start(out=got[s][:, u, :], out_offset=None, in_=d.graph,
                                            in_offset=bass.IndirectOffsetOnAxis(ap=ps[s][:, u:u + 1], axis=0)).then_inc(s_got[s], 16)
            tiles(pool, step, slots=GOT)

        @block.scalar
        def _(act):
            opened(act, s_copied)
            act.sem_inc(s_moved, GOT)

            def step(t, s, k, last):
                act.wait_ge(s_y, freed(t))
                act.activation(xt[s % SLOTS][:, :, :], m.xnT[:, :, bass.ds(t * P, P)], ACT.Copy).then_inc(s_copied, 1)
                act.wait_ge(s_got[s], k * 32 + 32)
                act.activation(row(source, t), got[s][:, 0:1, C:C + H1], ACT.Copy)
                act.activation(row(dest, t), got[s][:, 1:2, :], ACT.Copy).then_inc(s_moved, 1)
            tiles(act, step, slots=GOT)
            act.wait_ge(s_exp, 1)
            act.activation(tmp[:, :, :], logit[:, :, :], ACT.Exp).then_inc(s_exped, 1)
            stats_scalar(act, m, s_var, s_std)

        @block.tensor
        def _(pe):
            opened(pe, s_y)
            pe.wait_ge(s_w, 16)

            def step(t, s, k, last):
                pe.wait_ge(s_copied, done(t))
                pe.wait_ge(s_out, freed(t))
                pe.matmul(yp[s][:, 0:C], m.ones[0:1, :], bo[:, :], start=True, stop=False)
                for h in range(CH):
                    ins = pe.matmul(yp[s][:, 0:C], xt[s][:, h, :], m.mixer[:, h, :], start=False, stop=h == CH - 1)
                ins.then_inc(s_y, 1)
            tiles(pe, step)

        @block.vector
        def _(dve):
            opened(dve, s_out)

            def step(t, s, k, last):
                dve.wait_ge(s_y, done(t))
                dve.tensor_tensor(row(m.x, t), yp[s][:, 0:C].unsqueeze(1), row(m.x, t), ALU.add).then_inc(s_out, 1)
            tiles(dve, step)
            dve.wait_ge(s_out, done(T - 1))
            link = Chain(dve, s_chain)
            dve.wait_ge(s_moved, T + GOT)
            link(dve.tensor_tensor(logit[:, :, :], source[:, :, :], dest[:, :, C + H1:GROW], ALU.add))
            link(dve.scalar_tensor_tensor(out=logit[:, :, :], in0=logit[:, :, :], scalar=0.01, in1=logit[:, :, :], op0=ALU.mult, op1=ALU.max))
            link(dve.tensor_reduce(one[:, :], logit[:, :, :], AX.X, ALU.max))
            dve.tensor_tensor(logit[:, :, :], logit[:, :, :], one[:, :].unsqueeze(2).to_broadcast([P, T, H1]), ALU.subtract).then_inc(s_exp, 1)
            dve.wait_ge(s_exped, 1)
            link(dve.tensor_reduce(one[:, :], tmp[:, :, :], AX.X, ALU.add))
            link(dve.reciprocal(one[:, :], one[:, :]))
            link(dve.tensor_tensor(logit[:, :, :], tmp[:, :, :], one[:, :].unsqueeze(2).to_broadcast([P, T, H1]), ALU.mult))
            link(dve.tensor_tensor(prod[:, :, :].rearrange("p t (h c) -> p t h c", h=H1),
                                   dest[:, :, 0:C].rearrange("p t (h c) -> p t h c", h=H1),
                                   logit[:, :, :].unsqueeze(3).to_broadcast([P, T, H1, D1]), ALU.mult))
            link(dve.tensor_reduce(mean[:, :, :], prod[:, :, :].rearrange("p t (h c) -> p t c h", h=H1), AX.X, ALU.add))
            x4 = m.x[:, :, :].rearrange("p t (h c) -> p t h c", h=H1)
            link(dve.tensor_tensor(x4, x4, mean[:, :, :].unsqueeze(2).to_broadcast([P, T, H1, D1]), ALU.add))
            each_tile(dve, lambda t: row_stats(dve, m.x, stats, t, s_stats))
            dve.wait_ge(s_stats, T)
            stats_vector(dve, link, m, stats[:, :, :], s_var, s_std)



def phase_route1(nc, m, d):
    s_copied, s_flipped, s_row, s_hid, s_gelu, s_gate, s_gated, s_diff, s_exp, s_counts, s_totals, \
        s_hot, s_placed, s_lchain = m.sems(
            "rt1", "copied flipped row hid gelu gate gated diff exp counts totals hot placed lchain")
    s_kept = m.sems("rt1", "kept0 kept1")
    s_bias = m.sem("rt1_bias")
    with ExitStack() as mem, nc.Block() as block:
        sb = lambda name, shape, dt=F32: mem.enter_context(nc.sbuf_tensor("rt1_" + name, shape, dt))
        small6 = sb("small6", [P, 6, 32])
        wg, bg = m.f1_wg, m.f1_bg
        xs = [sb(f"xs{s}", [P, C]) for s in range(SLOTS)]
        xt = [sb(f"xt{s}", [P, CH, P]) for s in range(SLOTS)]
        hs = [sb(f"hs{s}", [P, HC, P]) for s in range(SLOTS)]
        score = sb("score", [P, T, X])
        equal = sb("equal", [P, T, X])
        best = sb("best", [P, T])
        key = sb("key", [P, T])
        onehot = sb("onehot", [P, max(T, FBLK1) * X])
        count = sb("count", [P, max(T, FBLK1) * X])
        pos = sb("pos", [P, T])
        work = sb("work", [P, 4, max(T, FBLK1)])
        whole = sb("whole", [P, 3, T], I32)
        hi_hot = sb("hi_hot", [P, T, 2 * FBLK1], BF16)
        lo_hot = [sb(f"lo_hot{s}", [P, PICK, P], BF16) for s in range(SLOTS)]
        flip, gp, hp = m.psum[0:2], m.psum[2:4], [m.psum[4:6], m.psum[6:8]]

        @block.sync
        def _(sp):
            def keep(t, s, k, last):
                sp.wait_ge(s_copied, done(t))
                sp.dma_start(d.normed1[bass.ds(t * P, P), :], xs[s][:, :]).then_inc(s_kept[s], 16)
            tiles(sp, keep)
            sp.dma_start(m.b2[:, :, :].rearrange("p e c -> p (e c)"),
                         d.f1_bd.rearrange("e c -> (e c)").rearrange("(a c) -> a c", a=1).to_broadcast([P, X * C])).then_inc(s_bias, 16)
            for s in range(SLOTS):
                sp.wait_ge(s_kept[s], 16 * ((T - s + 1) // 2))
            sp.wait_ge(s_bias, 16)

        @block.scalar
        def _(act):
            opened(act, s_gelu)
            act.wait_ge(m.s_hidden, 64)

            def step(t, s, k, last):
                act.wait_ge(s_hid, done(t))
                act.wait_ge(s_gate, freed(t))
                for q in range(HC):
                    ins = act.activation(hs[s][:, q, :], hp[s][q // 4][:, q % 4 * P:q % 4 * P + P], ACT.Gelu, bias=m.f1_b1[:, q:q + 1])
                ins.then_inc(s_gelu, 1)
            tiles(act, step)
            act.wait_ge(s_diff, 1)
            act.activation(score[:, :, :], equal[:, :, :], ACT.Exp).then_inc(s_exp, 1)

        @block.vector
        def _(dve):
            opened(dve, s_copied, s_row, s_gated)
            dve.wait_ge(m.s_hidden, 64)

            def norm(t, s, uses):
                dve.wait_ge(s_flipped, freed(t))
                landed(dve, s_kept[s], uses)
                normalise(dve, m, xs[s][:, :].unsqueeze(1), t).then_inc(s_copied, 1)

            def turn(t, s):
                dve.wait_ge(s_flipped, done(t))
                dve.wait_ge(s_hid, freed(t))
                dve.tensor_copy(xt[s][:, :, :], flip[s][:, 0:C].rearrange("p (h c) -> p h c", h=CH)).then_inc(s_row, 1)

            def step(t, s, k, last):
                if not last:
                    norm(t + 2, s, k + 1)
                    turn(t + 2, s)
                dve.wait_ge(s_gate, done(t))
                dve.tensor_tensor(row(score, t), gp[s][:, 0:X].unsqueeze(1), bg[:, :].unsqueeze(1), ALU.add).then_inc(s_gated, 1)
            norm(0, 0, 0)
            norm(1, 1, 0)
            turn(0, 0)
            turn(1, 1)
            tiles(dve, step, T - 1)
            step(T - 1, (T - 1) % 2, 0, True)
            dve.wait_ge(s_gated, done(T - 1))
            link = Chain(dve, s_lchain)
            wide = lambda a: a.unsqueeze(2).to_broadcast([P, T, X])
            link(dve.tensor_reduce(best[:, :], score[:, :, :], AX.X, ALU.max))
            dve.tensor_tensor(equal[:, :, :], score[:, :, :], wide(best[:, :]), ALU.subtract).then_inc(s_diff, 1)
            dve.wait_ge(s_exp, 1)
            link(dve.tensor_reduce(best[:, :], score[:, :, :], AX.X, ALU.add))
            link(dve.reciprocal(best[:, :], best[:, :]))
            link(dve.tensor_tensor(score[:, :, :], score[:, :, :], wide(best[:, :]), ALU.mult))
            first_best(dve, m, link, score, m.prob[:, :, 0], key[:, :], equal)
            sort_vector(dve, m, link, key[:, :], onehot, count, small6, m.psum[0], pos[:, :], s_counts, s_totals, X, T)
            invert_vector(dve, m, link, pos[:, :], m.iota[:, 0:T], work, whole, hi_hot[:, :, :], lo_hot, m.psum[1],
                          T, FBLK1, s_hot, s_placed)
            sort_owner(dve, m, link, small6[:, 5, :], count[:, 0:FBLK1], m.fown[:, 0:FBLK1], X, FBLK1)

        @block.tensor
        def _(pe):
            opened(pe, s_flipped, s_hid, s_gate)
            pe.wait_ge(m.s_hidden, 64)

            def flips(t, s):
                pe.wait_ge(s_copied, done(t))
                pe.wait_ge(s_row, freed(t))
                for h in range(CH):
                    ins = pe.transpose(flip[s][:, h * P:h * P + P], xs[s][:, h * P:h * P + P], m.ident[:, :])
                ins.then_inc(s_flipped, 1)

            def hidden(t, s):
                pe.wait_ge(s_row, done(t))
                pe.wait_ge(s_gelu, freed(t))
                hidden_turned(pe, hp[s], m.f1_w1, xt[s]).then_inc(s_hid, 1)

            def gates(t, s):
                pe.wait_ge(s_gelu, done(t))
                pe.wait_ge(s_gated, freed(t))
                for q in range(HC):
                    ins = pe.matmul(gp[s][:, 0:X], hs[s][:, q, :], wg[:, q, :], start=q == 0, stop=q == HC - 1)
                ins.then_inc(s_gate, 1)

            flips(0, 0)
            hidden(0, 0)
            flips(1, 1)

            def step(t, s, k, last):
                hidden(t + 1, 1 - s)
                if not last:
                    flips(t + 2, s)
                gates(t, s)
            tiles(pe, step, T - 1)
            gates(T - 1, (T - 1) % 2)
            sort_tensor(pe, m, small6, m.psum[0], s_counts, s_totals, X)
            invert_tensor(pe, m, hi_hot, lo_hot, m.psum[1], T, FBLK1, s_hot, s_placed)



class Tensors:
    pass


def build(nc, d):
    dram = lambda name, rows, width: nc.dram_tensor(name, (rows, width), F32, kind="Internal").ap()
    d.support = dram("support", T * P, C)
    d.rec = dram("records", P * EBLK, 4)
    d.normed0, d.results0 = dram("normed0", T * P, C), dram("results0", 2 * T * P, C)
    d.normed1, d.results1 = dram("normed1", T * P, C), dram("results1", T * P, C)
    d.graph = dram("graph", T * P, GROW)
    with ExitStack() as whole:
        m = Machine(nc, whole)
        m.x = m.sb("x", [P, T, C])
        m.ident = m.sb("ident", [P, P])
        m.earlier = m.sb("earlier", [P, P])
        m.ones = m.sb("ones", [P, P])
        m.zeros = m.sb("zeros", [P, C])
        m.iota = m.sb("iota", [P, EBLK])
        m.lastmask = m.sb("lastmask", [P, 1])
        m.small_int = m.sb("small_int", [P, 32], I32)
        m.fown = m.sb("fown", [P, FBLK0], I32)
        m.prob = m.sb("prob", [P, T, 2])
        m.mean = m.sb("mean", [P, T])
        m.rstd = m.sb("rstd", [P, T])
        m.scratch = m.sb("scratch", [P, 4, T])
        m.stats = m.sb("stats", [P, T, 6])
        m.tile2 = m.sb("tile2", [P, T, 2])
        m.number = m.sb("number", [P, 1])
        m.token = m.sb("token", [P, FBLK0], I32)
        m.dest = m.sb("dest", [P, FBLK0], I32)
        with m.scope():
            m.w1 = m.sb("ffn0_w1", [P, X, CH, HID])
            m.s_w1, m.s_w2 = m.sems("ffn0", "w1 w2")
            with m.scope():
                m.rec = m.sb("rec", [P, ECOLS, 4])
                m.epos = m.sb("epos", [P, ECOLS], I32)
                m.eowner = m.sb("eowner", [P, EBLK], I32)
                m.eend = m.sb("eend", [P, T])
                m.buf_rec = [m.sb(f"buf_rec{h}", [P, EBUF * 4]) for h in range(2)]
                m.buf_pos = [m.sb(f"buf_pos{h}", [P, EBUF], I32) for h in range(2)]
                m.s_copied, m.s_issue = m.sems("edges", "copied issue")
                m.s_sent = m.sems("edges", "sent0 sent1")
                phase_start(nc, m, d)
                m.mix = m.sb("mix", [P, T, C])
                with m.scope():
                    m.xn = m.sb("xn", [P, T, C])
                    m.xnT = m.sb("xnT", [P, CH, T * P])
                    m.bd = m.sb("bd", [P, CH, KVW])
                    phase_support_kv(nc, m, d, (0, 5 * ESTEP))
                    phase_attend(nc, m, d, (5 * ESTEP, 8 * ESTEP))
                phase_mlp(nc, m, d, (8 * ESTEP, ECOLS))
                phase_aggregate(nc, m, d)
            w2 = m.sb("ffn0_w2", [P, X, HC, C])
            m.b1_all = m.sb("ffn0_b1", [P, X, HC])
            m.b2 = m.sb("ffn0_b2", [P, X, C])
            phase_route0(nc, m, d, w2)
            phase_experts(nc, m, "ex0", FBLK0, d.normed0, d.results0, 2, ACT.Relu, w2, m.s_w2, True)
        m.recycle()
        m.f1_w1 = m.sb("f1_w1", [P, CH, HID])
        m.f1_b1 = m.sb("f1_b1", [P, HC])
        m.f1_wg = m.sb("f1_wg", [P, HC, X])
        m.f1_bg = m.sb("f1_bg", [P, X])
        m.s_hidden = m.sem("f1_hidden")
        m.wd = m.sb("f1_wd", [P, X, HC, C])
        m.s_wd = m.sem("f1_wd")
        with m.scope():
            m.xnT = m.sb("xnT1", [P, CH, T * P])
            m.mixer = m.sb("mixer", [P, CH, C])
            m.ends = m.sb("ends", [P, T, 2], I32)
            with m.scope():
                m.p_w = m.sb("project_w", [P, CH, 2 * C + GROW])
                m.p_attn = m.sb("project_attn", [P, 2, C])
                m.p_wo, m.p_wq = m.sb("project_wo", [P, CH, C]), m.sb("project_wq", [P, CH, C])
                m.p_gb = m.sb("project_gb", [P, 2, G * D1])
                m.s_project = m.sem("project")
                phase_combine(nc, m, d, "cmb0", d.results0, 2, False)
                phase_project1(nc, m, d)
            phase_graph1(nc, m, d)
        m.b2 = m.sb("f1_bd", [P, X, C])
        phase_route1(nc, m, d)
        phase_experts(nc, m, "ex1", FBLK1, d.normed1, d.results1, 1, ACT.Gelu, m.wd, m.s_wd, False)
        phase_combine(nc, m, d, "cmb1", d.results1, 1, True)


def kernel(x, src, dst, edge_weight, L0_gnn_A, L0_gnn_B, L0_gnn_bn_weight, L0_gnn_bn_bias, L0_mix_Wqkv, L0_mix_ln1_g,
           L0_mix_ln1_b, L0_mix_W1, L0_mix_b1, L0_mix_W2, L0_mix_b2, L0_mix_ln2_g, L0_mix_ln2_b, L0_ffn_Wg, L0_ffn_bg,
           L0_ffn_W1, L0_ffn_b1, L0_ffn_W2, L0_ffn_b2, L1_gnn_weight, L1_gnn_attn_l, L1_gnn_attn_r, L1_mix_wq,
           L1_mix_wk, L1_mix_wv, L1_mix_wo, L1_mix_bo, L1_mix_ln_k_g, L1_mix_ln_k_b, L1_mix_ln_v_g, L1_mix_ln_v_b,
           L1_ffn_W1, L1_ffn_b1, L1_ffn_Wg, L1_ffn_bg, L1_ffn_Wd, L1_ffn_bd):
    import numpy as np
    from concourse import bacc
    from concourse.bass_utils import run_bass_kernel_spmd

    laid = {
        "ends": np.transpose(np.reshape(np.stack([src[:N], dst[:N]], -1)[:(T - 1) * P], (T - 1, P, 2)), (1, 0, 2)),
        "ends_last": np.stack([src[(T - 1) * P:N], dst[(T - 1) * P:N]], -1),
        "x": x, "src": src, "dst": dst, "edge_weight": edge_weight,
        "A": L0_gnn_A, "B": L0_gnn_B, "bn_w": L0_gnn_bn_weight, "bn_b": L0_gnn_bn_bias,
        "wqkv": np.transpose(L0_mix_Wqkv), "ln1_g": L0_mix_ln1_g, "ln1_b": L0_mix_ln1_b,
        "mw1": np.transpose(L0_mix_W1), "mb1": np.transpose(np.reshape(L0_mix_b1, (CH, P))), "mw2": np.transpose(L0_mix_W2), "mb2": L0_mix_b2,
        "ln2_g": L0_mix_ln2_g, "ln2_b": L0_mix_ln2_b,
        "f0_wg": np.transpose(L0_ffn_Wg), "f0_bg": L0_ffn_bg,
        "f0_w1": np.transpose(L0_ffn_W1, (0, 2, 1)), "f0_b1": np.transpose(np.reshape(L0_ffn_b1, (X, HC, P)), (2, 0, 1)),
        "f0_w2": np.transpose(L0_ffn_W2, (0, 2, 1)), "f0_b2": L0_ffn_b2,
        "g_w": L1_gnn_weight, "g_al": L1_gnn_attn_l, "g_ar": L1_gnn_attn_r,
        "wq": L1_mix_wq, "wk": np.transpose(L1_mix_wk), "wv": np.transpose(L1_mix_wv), "wo": np.transpose(L1_mix_wo),
        "bo": L1_mix_bo, "k_g": L1_mix_ln_k_g, "k_b": L1_mix_ln_k_b, "v_g": L1_mix_ln_v_g, "v_b": L1_mix_ln_v_b,
        "f1_w1": L1_ffn_W1, "f1_b1": np.transpose(np.reshape(L1_ffn_b1, (HC, P))), "f1_wg": L1_ffn_Wg, "f1_bg": L1_ffn_bg, "f1_wd": L1_ffn_Wd,
        "f1_bd": L1_ffn_bd,
    }
    nc = bacc.Bacc("TRN2", target_bir_lowering=False, num_devices=1)
    d = Tensors()
    arrays = {}
    for name, a in laid.items():
        arrays["in_" + name] = a = np.ascontiguousarray(a)
        ap = nc.dram_tensor("in_" + name, a.shape, mybir.dt.from_np(a.dtype), kind="ExternalInput").ap()
        d.__dict__[name] = ap
    d.out = nc.dram_tensor("out", (N, C), F32, kind="ExternalOutput").ap()
    build(nc, d)
    r = run_bass_kernel_spmd(nc, [arrays], core_ids=[0])
    return r.results[0]["out"]
```
